# Optimizing a Trainium2 kernel written in Bass

```python
import numpy as np
import jax
import jax.numpy as jnp

def _softmax(x, axis=-1):
    return jax.nn.softmax(x, axis=axis)

def _gelu(x):
    return jax.nn.gelu(x, approximate=True)

def _silu(x):
    return jax.nn.silu(x)

def _sigmoid(x):
    return jax.nn.sigmoid(x)

def _layernorm(x, axis=-1, eps=1e-05):
    m = jnp.mean(x, axis=axis, keepdims=True)
    v = jnp.var(x, axis=axis, keepdims=True)
    return (x - m) / jnp.sqrt(v + eps)

def _scatter_add(tgt, idx, src, axis=0):
    return tgt.at[idx].add(src)

def _segment_sum(src, seg, n):
    return jax.ops.segment_sum(src, seg, n)
kernel_name = 'mk_seq_postln_d2_jaxref_r8_842173'

def setup_inputs(seed: int=0):
    np.random.seed(seed)
    _w = jnp.asarray

    def _L0_attn_setup():
        import jax, jax.numpy as jnp
        import numpy as np
        BATCH, SEQ, HIDDEN = (2, 512, 512)
        HEADS, HEAD_DIM, BLOCK = (32, 128, 32)
        LAYER_IDX, N_LAYERS = (1, 32)
        EPS = 1e-05

        def _decays():
            base = 1.0 / 2.0 ** (8.0 / HEADS)
            exponent = jnp.arange(HEADS, dtype=jnp.float32) + 1.0
            factor = 1.0 - LAYER_IDX / (N_LAYERS - 1 + 1e-05) + 1e-05
            slope = (base ** exponent * factor)[:, None, None]
            r = jnp.arange(BLOCK, dtype=jnp.float32) + 1.0
            q_decay = jnp.exp(-slope * r[:, None])
            k_decay = jnp.exp(-slope * (BLOCK - r)[:, None])
            diff = r[:, None] - r[None, :]
            diag = slope[None] * diff[None, None]
            diag = jnp.where(diag >= 0, -diag, -jnp.inf)
            diag_decay = jnp.exp(diag)
            block_decay = jnp.exp(-slope * BLOCK)
            return (q_decay, k_decay, diag_decay, block_decay)
        key = jax.random.key(seed)
        ks = jax.random.split(key, 5)
        s = 0.02
        return {'hidden_states': jax.random.normal(ks[0], (BATCH, SEQ, HIDDEN), jnp.float32), 'qkv_w': jax.random.normal(ks[1], (3 * HEADS * HEAD_DIM, HIDDEN), jnp.float32) * s, 'out_w': jax.random.normal(ks[2], (HIDDEN, HEADS * HEAD_DIM), jnp.float32) * s, 'gate_w': jax.random.normal(ks[3], (HEADS * HEAD_DIM, HIDDEN), jnp.float32) * s, 'norm_w': jnp.ones((HEADS * HEAD_DIM,), jnp.float32)}
    _L0_attn_in = _L0_attn_setup()

    def _L0_ffn_setup():
        import jax, jax.numpy as jnp
        import numpy as np
        N_EXPERTS = 8
        TOP_K = 2
        D_MODEL = 512
        RANK = 64
        key = jax.random.key(seed)
        k0, k1, k2, k3 = jax.random.split(key, 4)
        inputs = jax.random.normal(k0, (4, 256, D_MODEL), dtype=jnp.float32)
        gate_w = jax.random.normal(k1, (N_EXPERTS, D_MODEL), dtype=jnp.float32) * 0.02
        lora_A = jax.random.normal(k2, (N_EXPERTS, RANK, D_MODEL), dtype=jnp.float32) * 0.02
        lora_B = jax.random.normal(k3, (N_EXPERTS, D_MODEL, RANK), dtype=jnp.float32) * 0.02
        return {'inputs': inputs, 'gate_w': gate_w, 'lora_A': lora_A, 'lora_B': lora_B}
    _L0_ffn_in = _L0_ffn_setup()

    def _L1_attn_setup():
        import jax, jax.numpy as jnp
        import numpy as np
        B, N, D = (2, 256, 512)
        H, HD = (32, 128)
        EPS = 1e-06

        def rmsnorm(x, w):
            xf = x.astype(jnp.float32)
            var = jnp.mean(xf * xf, axis=-1, keepdims=True)
            return (w * (xf * jax.lax.rsqrt(var + EPS))).astype(x.dtype)
        key = jax.random.key(seed)
        ks = jax.random.split(key, 11)
        s = 1.0 / np.sqrt(D)
        return {'hidden_states': jax.random.normal(ks[0], (B, N, D), jnp.float32), 'Wq': jax.random.normal(ks[1], (D, H * HD), jnp.float32) * s, 'bq': jax.random.normal(ks[2], (H * HD,), jnp.float32) * 0.01, 'Wk': jax.random.normal(ks[3], (D, H * HD), jnp.float32) * s, 'bk': jax.random.normal(ks[4], (H * HD,), jnp.float32) * 0.01, 'Wv': jax.random.normal(ks[5], (D, H * HD), jnp.float32) * s, 'bv': jax.random.normal(ks[6], (H * HD,), jnp.float32) * 0.01, 'Wo': jax.random.normal(ks[7], (H * HD, D), jnp.float32) * s, 'bo': jax.random.normal(ks[8], (D,), jnp.float32) * 0.01, 'gq': jnp.ones((HD,), jnp.float32), 'gk': jnp.ones((HD,), jnp.float32)}
    _L1_attn_in = _L1_attn_setup()

    def _L1_ffn_setup():
        import jax, jax.numpy as jnp
        import numpy as np
        GROUP_SIZE = 128

        def dequantize(imatrix, scales, zeros, group_size, out_dtype):
            rs = jnp.repeat(scales, group_size, axis=0)
            rz = jnp.repeat(zeros, group_size, axis=0)
            return ((imatrix.astype(rs.dtype) - rz.astype(rs.dtype)) * rs).astype(out_dtype)
        key = jax.random.key(seed)
        ks = jax.random.split(key, 10)
        H, I, G = (512, 1792, GROUP_SIZE)
        B, S = (4, 256)
        x = jax.random.normal(ks[0], (B, S, H), dtype=jnp.float32)
        gate_w = jax.random.randint(ks[1], (H, I), 0, 16, dtype=jnp.int32)
        gate_z = jax.random.randint(ks[2], (H // G, I), 0, 16, dtype=jnp.int32)
        gate_s = jax.random.uniform(ks[3], (H // G, I), dtype=jnp.float32) * 0.01
        up_w = jax.random.randint(ks[4], (H, I), 0, 16, dtype=jnp.int32)
        up_z = jax.random.randint(ks[5], (H // G, I), 0, 16, dtype=jnp.int32)
        up_s = jax.random.uniform(ks[6], (H // G, I), dtype=jnp.float32) * 0.01
        down_w = jax.random.randint(ks[7], (I, H), 0, 16, dtype=jnp.int32)
        down_z = jax.random.randint(ks[8], (I // G, H), 0, 16, dtype=jnp.int32)
        down_s = jax.random.uniform(ks[9], (I // G, H), dtype=jnp.float32) * 0.01
        return {'x': x, 'gate_w': gate_w, 'gate_z': gate_z, 'gate_s': gate_s, 'up_w': up_w, 'up_z': up_z, 'up_s': up_s, 'down_w': down_w, 'down_z': down_z, 'down_s': down_s}
    _L1_ffn_in = _L1_ffn_setup()
    _d = {'L0_attn_hidden_states': _L0_attn_in['hidden_states'], 'L0_attn_qkv_w': _L0_attn_in['qkv_w'], 'L0_attn_out_w': _L0_attn_in['out_w'], 'L0_attn_gate_w': _L0_attn_in['gate_w'], 'L0_attn_norm_w': _L0_attn_in['norm_w'], 'L0_ffn_gate_w': _L0_ffn_in['gate_w'], 'L0_ffn_lora_A': _L0_ffn_in['lora_A'], 'L0_ffn_lora_B': _L0_ffn_in['lora_B'], 'L1_attn_Wq': _L1_attn_in['Wq'], 'L1_attn_bq': _L1_attn_in['bq'], 'L1_attn_Wk': _L1_attn_in['Wk'], 'L1_attn_bk': _L1_attn_in['bk'], 'L1_attn_Wv': _L1_attn_in['Wv'], 'L1_attn_bv': _L1_attn_in['bv'], 'L1_attn_Wo': _L1_attn_in['Wo'], 'L1_attn_bo': _L1_attn_in['bo'], 'L1_attn_gq': _L1_attn_in['gq'], 'L1_attn_gk': _L1_attn_in['gk'], 'L1_ffn_gate_w': _L1_ffn_in['gate_w'], 'L1_ffn_gate_z': _L1_ffn_in['gate_z'], 'L1_ffn_gate_s': _L1_ffn_in['gate_s'], 'L1_ffn_up_w': _L1_ffn_in['up_w'], 'L1_ffn_up_z': _L1_ffn_in['up_z'], 'L1_ffn_up_s': _L1_ffn_in['up_s'], 'L1_ffn_down_w': _L1_ffn_in['down_w'], 'L1_ffn_down_z': _L1_ffn_in['down_z'], 'L1_ffn_down_s': _L1_ffn_in['down_s']}
    _x0 = _d['L0_attn_hidden_states']
    _d['L0_attn_hidden_states'] = jax.random.normal(jax.random.fold_in(jax.random.key(seed), 1), (1, 1024, 512), dtype=_x0.dtype)
    del _x0
    return _d

def reference(L0_attn_hidden_states, L0_attn_qkv_w, L0_attn_out_w, L0_attn_gate_w, L0_attn_norm_w, L0_ffn_gate_w, L0_ffn_lora_A, L0_ffn_lora_B, L1_attn_Wq, L1_attn_bq, L1_attn_Wk, L1_attn_bk, L1_attn_Wv, L1_attn_bv, L1_attn_Wo, L1_attn_bo, L1_attn_gq, L1_attn_gk, L1_ffn_gate_w, L1_ffn_gate_z, L1_ffn_gate_s, L1_ffn_up_w, L1_ffn_up_z, L1_ffn_up_s, L1_ffn_down_w, L1_ffn_down_z, L1_ffn_down_s):

    def _L0_attn_ref(hidden_states, qkv_w, out_w, gate_w, norm_w):
        import jax, jax.numpy as jnp
        import numpy as np
        BATCH, SEQ, HIDDEN = (2, 512, 512)
        HEADS, HEAD_DIM, BLOCK = (32, 128, 32)
        LAYER_IDX, N_LAYERS = (1, 32)
        EPS = 1e-05

        def _decays():
            base = 1.0 / 2.0 ** (8.0 / HEADS)
            exponent = jnp.arange(HEADS, dtype=jnp.float32) + 1.0
            factor = 1.0 - LAYER_IDX / (N_LAYERS - 1 + 1e-05) + 1e-05
            slope = (base ** exponent * factor)[:, None, None]
            r = jnp.arange(BLOCK, dtype=jnp.float32) + 1.0
            q_decay = jnp.exp(-slope * r[:, None])
            k_decay = jnp.exp(-slope * (BLOCK - r)[:, None])
            diff = r[:, None] - r[None, :]
            diag = slope[None] * diff[None, None]
            diag = jnp.where(diag >= 0, -diag, -jnp.inf)
            diag_decay = jnp.exp(diag)
            block_decay = jnp.exp(-slope * BLOCK)
            return (q_decay, k_decay, diag_decay, block_decay)
        b, s, _ = hidden_states.shape
        h, d, bs = (HEADS, HEAD_DIM, BLOCK)
        nb = s // bs
        q_decay, k_decay, diag_decay, block_decay = _decays()
        qkv = jax.nn.silu(hidden_states @ qkv_w.T)
        qkv = qkv.reshape(b, s, h, 3, d)
        q = jnp.moveaxis(qkv[:, :, :, 0], 2, 1)
        k = jnp.moveaxis(qkv[:, :, :, 1], 2, 1)
        v = jnp.moveaxis(qkv[:, :, :, 2], 2, 1)

        def to_blocks(x):
            return jnp.moveaxis(x.reshape(b, h, nb, bs, d), 2, 0)
        qb, kb, vb = (to_blocks(q), to_blocks(k), to_blocks(v))

        def step(kv, blk):
            cq, ck, cv = blk
            scores = jnp.einsum('bhnd,bhmd->bhnm', cq, ck) * diag_decay
            intra = jnp.einsum('bhnm,bhmd->bhnd', scores, cv)
            inter = jnp.einsum('bhnd,bhde->bhne', cq * q_decay, kv)
            kv_next = kv * block_decay + jnp.einsum('bhnd,bhne->bhde', ck * k_decay, cv)
            return (kv_next, intra + inter)
        kv0 = jnp.zeros((b, h, d, d), hidden_states.dtype)
        _, out_blocks = jax.lax.scan(step, kv0, (qb, kb, vb))
        attn = jnp.moveaxis(out_blocks, 0, 2)
        attn = attn.reshape(b, h, s, d).transpose(0, 2, 1, 3).reshape(b, s, h * d)
        xf = attn.astype(jnp.float32)
        xf = xf * jax.lax.rsqrt(jnp.mean(xf * xf, axis=-1, keepdims=True) + EPS)
        normed = norm_w * xf.astype(attn.dtype)
        gate = jax.nn.sigmoid(hidden_states @ gate_w.T)
        return gate * normed @ out_w.T

    def _L0_ffn_ref(inputs, gate_w, lora_A, lora_B):
        import jax, jax.numpy as jnp
        import numpy as np
        N_EXPERTS = 8
        TOP_K = 2
        D_MODEL = 512
        RANK = 64
        x = inputs.reshape(-1, inputs.shape[-1])
        T = x.shape[0]
        gate_probs = jax.nn.softmax(x @ gate_w.T, axis=-1)
        weights, sel = jax.lax.top_k(gate_probs, TOP_K)
        weights = weights / jnp.sum(weights, axis=-1, keepdims=True)
        w_full = jnp.zeros((T, N_EXPERTS), dtype=x.dtype).at[jnp.arange(T)[:, None], sel].add(weights)
        out = jnp.zeros((T, D_MODEL), dtype=x.dtype)
        for e in range(N_EXPERTS):
            y = x @ lora_A[e].T @ lora_B[e].T
            out = out + w_full[:, e:e + 1] * y
        return out.reshape(inputs.shape[:-1] + (D_MODEL,))

    def _L1_attn_ref(hidden_states, Wq, bq, Wk, bk, Wv, bv, Wo, bo, gq, gk):
        import jax, jax.numpy as jnp
        import numpy as np
        B, N, D = (2, 256, 512)
        H, HD = (32, 128)
        EPS = 1e-06

        def rmsnorm(x, w):
            xf = x.astype(jnp.float32)
            var = jnp.mean(xf * xf, axis=-1, keepdims=True)
            return (w * (xf * jax.lax.rsqrt(var + EPS))).astype(x.dtype)
        b, n, _ = hidden_states.shape
        q = (hidden_states @ Wq + bq).reshape(b, n, H, HD)
        k = (hidden_states @ Wk + bk).reshape(b, n, H, HD)
        v = (hidden_states @ Wv + bv).reshape(b, n, H, HD)
        q = rmsnorm(q, gq)
        k = rmsnorm(k, gk)
        scale = 1.0 / np.sqrt(HD)
        scores = jnp.einsum('bnhd,bmhd->bhnm', q, k) * scale
        attn = jax.nn.softmax(scores.astype(jnp.float32), axis=-1).astype(q.dtype)
        out = jnp.einsum('bhnm,bmhd->bnhd', attn, v).reshape(b, n, H * HD)
        return out @ Wo + bo

    def _L1_ffn_ref(x, gate_w, gate_z, gate_s, up_w, up_z, up_s, down_w, down_z, down_s):
        import jax, jax.numpy as jnp
        import numpy as np
        GROUP_SIZE = 128

        def dequantize(imatrix, scales, zeros, group_size, out_dtype):
            rs = jnp.repeat(scales, group_size, axis=0)
            rz = jnp.repeat(zeros, group_size, axis=0)
            return ((imatrix.astype(rs.dtype) - rz.astype(rs.dtype)) * rs).astype(out_dtype)
        dt = x.dtype
        gate_proj = dequantize(gate_w, gate_s, gate_z, GROUP_SIZE, dt)
        up_proj = dequantize(up_w, up_s, up_z, GROUP_SIZE, dt)
        down_proj = dequantize(down_w, down_s, down_z, GROUP_SIZE, dt)
        gate = jax.nn.silu(jnp.dot(x, gate_proj))
        up = jnp.dot(x, up_proj)
        return jnp.dot(gate * up, down_proj)
    x = L0_attn_hidden_states
    x = _layernorm(x + _L0_attn_ref(x, L0_attn_qkv_w, L0_attn_out_w, L0_attn_gate_w, L0_attn_norm_w), axis=-1)
    x = _layernorm(x + _L0_ffn_ref(x, L0_ffn_gate_w, L0_ffn_lora_A, L0_ffn_lora_B), axis=-1)
    x = _layernorm(x + _L1_attn_ref(x, L1_attn_Wq, L1_attn_bq, L1_attn_Wk, L1_attn_bk, L1_attn_Wv, L1_attn_bv, L1_attn_Wo, L1_attn_bo, L1_attn_gq, L1_attn_gk), axis=-1)
    x = _layernorm(x + _L1_ffn_ref(x, L1_ffn_gate_w, L1_ffn_gate_z, L1_ffn_gate_s, L1_ffn_up_w, L1_ffn_up_z, L1_ffn_up_s, L1_ffn_down_w, L1_ffn_down_z, L1_ffn_down_s), axis=-1)
    return x

_drawn_inputs = setup_inputs


def setup_inputs(seed=0):
    import zlib

    import numpy as np

    out = dict(_drawn_inputs(seed))
    spreads = {'L0_attn_norm_w': (1.0, 0.2), 'L1_attn_gq': (1.0, 0.591), 'L1_attn_gk': (1.0, 0.2)}
    factors = {'L1_attn_bq': 28.707, 'L1_attn_bk': 64.0, 'L1_attn_bv': 2.945, 'L1_attn_bo': 7.976}
    for name, (base, spread) in spreads.items():
        noise = np.random.default_rng([zlib.crc32(name.encode()), seed]).standard_normal(out[name].shape)
        drawn = base * np.exp(spread * noise) if base else spread * noise
        out[name] = jnp.asarray(drawn.astype(out[name].dtype))
    for name, factor in factors.items():
        out[name] = (out[name] * factor).astype(out[name].dtype)
    return out
```

```python
from contextlib import ExitStack

import numpy as np

import concourse.bass as bass
from concourse import mybir

F32 = mybir.dt.float32
F32R = mybir.dt.float32r
I32 = mybir.dt.int32
U32 = mybir.dt.uint32
ACT = mybir.ActivationFunctionType
ALU = mybir.AluOpType
AX_X = mybir.AxisListType.X
ds = bass.ds

P = 128
TOK = 1024
NT = TOK // P
D = 512
KB = D // P
HALF = 512
HEADS = 32
HD = 128
LN_EPS = 1e-5

CHUNK = P
CH = HALF // CHUNK
L0_EPS = 1e-5


def decay_tables():
    factor = 1.0 - 1 / (HEADS - 1 + 1e-05) + 1e-05
    slope = (1.0 / 2.0 ** (8.0 / HEADS)) ** (np.arange(HEADS) + 1.0) * factor
    r = np.arange(CHUNK, dtype=np.float64)
    diff = r[None, None, :] - r[None, :, None]
    mask = np.where(diff >= 0, np.exp(-slope[:, None, None] * np.maximum(diff, 0)), 0.0)
    q_decay = np.broadcast_to(np.exp(-slope[:, None] * (r + 1)[None, :])[:, None], (HEADS, P, CHUNK))
    k_decay = np.exp(-(CHUNK - 1 - r)[None, :, None] * slope[:, None, None])
    chunk_decay = np.broadcast_to(np.exp(-slope * CHUNK)[:, None, None], (HEADS, P, 1))
    return np.concatenate([mask, q_decay, k_decay, chunk_decay], 2).astype(np.float32)


def wait(eng, sem, value):
    if isinstance(value, int) and value <= 0:
        return
    eng.wait_ge(sem, value)


def f(ap):
    return ap.bitcast(F32)


def three_pass(pe, out, w_hi, w_lo, x_hi, x_lo, first, last):
    pe.matmul(out, w_hi, x_hi, start=first, stop=False)
    pe.matmul(out, w_hi, x_lo, start=False, stop=False)
    return pe.matmul(out, w_lo, x_hi, start=False, stop=last)


class Shared:

    def __init__(self, nc, ctx):
        def sb(name, shape, dt=F32):
            return ctx.enter_context(nc.sbuf_tensor(name, shape, dt))

        self.x_nat = sb("x_nat", [P, NT, D])
        self.xT_hi = sb("xT_hi", [P, KB, TOK], F32R)
        self.xT_lo = sb("xT_lo", [P, KB, TOK], F32R)
        self.ident = sb("ident", [P, P])
        self.stats = sb("ln_stats", [P, NT, 6])
        self.mv = sb("ln_mv", [P, NT, 2])
        self.var = sb("ln_var", [P, NT])
        self.rstd = sb("ln_rstd", [P, NT])
        self.tmp = sb("ln_tmp", [P, NT])


class LayerNorm:

    def __init__(self, nc, ctx, name, sh, banks, transpose=True):
        def sem(s):
            return ctx.enter_context(nc.semaphore(f"{name}_{s}"))

        self.sh, self.banks, self.transpose = sh, banks, transpose
        self.chain = sem("dve_chain")
        self.chained = 0
        self.var_ready = sem("var_ready")
        self.ln_done = sem("ln_done")
        self.root = sem("root_ready")
        self.normed = sem("normed")
        self.tr = sem("transposed")
        self.hi = sem("hi_ready")
        self.lo = sem("lo_ready")

    def link(self, dve, ins):
        self.chained += 1
        ins.then_inc(self.chain, 1)
        dve.wait_ge(self.chain, self.chained)

    def rsqrt_refine(self, dve, v, y, tmp):
        self.link(dve, dve.tensor_tensor(tmp, y, y, ALU.mult))
        self.link(dve, dve.tensor_tensor(tmp, tmp, v, ALU.mult))
        self.link(dve, dve.tensor_scalar(tmp, tmp, -0.5, 1.5, ALU.mult, ALU.add))
        self.link(dve, dve.tensor_tensor(y, y, tmp, ALU.mult))

    def vector_stats(self, dve, t):
        sh = self.sh
        self.link(dve, dve.bn_stats(sh.stats[:, t, :], sh.x_nat[:, t, :]))
        self.link(dve, dve.bn_aggr(sh.mv[:, t, :], sh.stats[:, t, :]))

    def vector(self, dve, stored=None):
        sh = self.sh
        dve.tensor_scalar(sh.var[:, :], sh.mv[:, :, 1], LN_EPS, None, ALU.add).then_inc(self.var_ready, 1)
        dve.wait_ge(self.root, 1)
        dve.wait_ge(self.var_ready, 1)
        self.rsqrt_refine(dve, sh.var[:, :], sh.rstd[:, :], sh.tmp[:, :])
        for t in range(NT):
            dve.tensor_scalar(sh.x_nat[:, t, :], sh.x_nat[:, t, :], sh.mv[:, t, 0:1], sh.rstd[:, t:t + 1],
                              ALU.subtract, ALU.mult).then_inc(self.normed, 1)
        if self.transpose:
            for t in range(NT):
                dve.wait_ge(self.hi, t + 1)
                dve.wait_ge(self.tr, t + 1)
                dve.tensor_tensor(sh.xT_lo[:, :, t * P:(t + 1) * P],
                                  self.banks[t % 2][:, :].rearrange("p (k n) -> p k n", k=KB),
                                  f(sh.xT_hi[:, :, t * P:(t + 1) * P]), ALU.subtract).then_inc(self.lo, 1)

    def scalar(self, act):
        sh = self.sh
        act.wait_ge(self.var_ready, 1)
        act.activation(sh.rstd[:, :], sh.var[:, :], ACT.Ln).then_inc(self.ln_done, 1)
        act.wait_ge(self.ln_done, 1)
        act.activation(sh.rstd[:, :], sh.rstd[:, :], ACT.Exp, scale=-0.5).then_inc(self.root, 1)
        if self.transpose:
            for t in range(NT):
                act.wait_ge(self.tr, t + 1)
                act.activation(sh.xT_hi[:, :, t * P:(t + 1) * P],
                               self.banks[t % 2][:, :].rearrange("p (k n) -> p k n", k=KB),
                               ACT.Copy).then_inc(self.hi, 1)

    def tensor(self, pe):
        sh = self.sh
        for t in range(NT):
            pe.wait_ge(self.normed, t + 1)
            if t >= 2:
                pe.wait_ge(self.lo, t - 1)
            for k in range(KB):
                last = pe.transpose(self.banks[t % 2][:, k * P:(k + 1) * P],
                                    sh.x_nat[:, t, k * P:(k + 1) * P], sh.ident[:, :])
            last.then_inc(self.tr, 1)


def l0_attention(nc, sh, x, xT, w, ow, norm_w, decay_in):
    NG = 8
    GATE = 3
    with ExitStack() as ctx:
        def sb(name, shape, dt=F32):
            return ctx.enter_context(nc.sbuf_tensor(f"a_{name}", shape, dt))

        def bank(name, shape):
            return ctx.enter_context(nc.psum_tensor(f"a_{name}", shape, F32))

        def sem(name):
            return ctx.enter_context(nc.semaphore(f"a_{name}"))

        w_raw = [sb(f"w_raw{t}", [P, KB, HD]) for t in range(4)]
        w_hi = [sb(f"w_hi{t}", [P, KB, HD], F32R) for t in range(4)]
        w_lo = [sb(f"w_lo{t}", [P, KB, HD], F32R) for t in range(4)]
        ow_raw = sb("ow_raw", [P, D])
        ow_hi = [sb(f"ow_hi{b}", [P, D], F32R) for b in range(2)]
        ow_lo = [sb(f"ow_lo{b}", [P, D], F32R) for b in range(2)]
        qkvg = [[sb(f"qkvg{t}_{b}", [P, TOK]) for b in range(2)] for t in range(4)]
        sig_tmp = [sb(f"sig{i}", [P, HALF]) for i in range(2)]
        q_dec = sb("q_dec", [P, TOK])
        k_nat = sb("k_nat", [P, NT, HD])
        v_nat = sb("v_nat", [P, NT, HD])
        s_masked = sb("s_masked", [P, TOK])
        state = sb("state", [P, NT, HD])
        gated = sb("gated", [P, TOK])
        ga_hi = [sb(f"ga_hi{b}", [P, TOK], F32R) for b in range(2)]
        ga_lo = [sb(f"ga_lo{b}", [P, TOK], F32R) for b in range(2)]
        squares = sb("squares", [P, TOK])
        sq_sum = sb("sq_sum", [P, TOK])
        acc = sb("acc", [P, NT, D])
        decay = [sb(f"decay{b}", [P, 2 * CHUNK + 2]) for b in range(2)]
        mask = [d[:, 0:CHUNK].unsqueeze(1) for d in decay]
        q_decay = [d[:, CHUNK:2 * CHUNK].unsqueeze(1) for d in decay]
        k_decay = [d[:, 2 * CHUNK:2 * CHUNK + 1] for d in decay]
        chunk_decay = [d[:, 2 * CHUNK + 1:2 * CHUNK + 2] for d in decay]
        norm_sb = sb("norm_sb", [P, HEADS])
        ones = sb("ones", [P, 1])
        ms = sb("ms", [P, NT])
        rms = sb("rms", [P, NT])

        pj = [bank(f"pj{i}", [P, HALF]) for i in range(2)]
        tk = bank("tk", [P, HALF])
        tv = bank("tv", [P, HALF])
        s_ps = bank("s_ps", [P, HALF])
        u_ps = bank("u_ps", [P, HALF])
        o_ps = bank("o_ps", [P, HALF])
        y_ps = bank("y_ps", [P, HALF])

        w_in = [sem(f"w_in{t}") for t in range(4)]
        ow_in = sem("ow_in")
        decay_in_sem = [sem(f"decay_in{b}") for b in range(2)]
        w_hi_done, w_lo_done = sem("w_hi_done"), sem("w_lo_done")
        ow_hi_done, ow_lo_done = sem("ow_hi_done"), sem("ow_lo_done")
        proj = sem("proj")
        sig = sem("sig")
        silu = sem("silu")
        kv_tr = sem("kv_tr")
        kv_nat = sem("kv_nat")
        scored, masked = sem("scored"), sem("masked")
        q_decayed = sem("q_decayed")
        upd, state_done = sem("upd"), sem("state_done")
        attn = sem("attn")
        squared, sq_added = sem("squared"), sem("sq_added")
        gated_done, ga_hi_done, ga_lo_done = sem("gated_done"), sem("ga_hi_done"), sem("ga_lo_done")
        y_done, y_added = sem("y_done"), sem("y_added")
        x_in, const_in, x_split = sem("x_in"), sem("const_in"), sem("x_split")
        xt_hi_done = sem("xt_hi_done")
        zeroed = sem("zeroed")
        ms_ready, ms_done, ms_ln, ms_root, rms_done, x_nat_in, added = (
            sem("ms_ready"), sem("ms_done"), sem("ms_ln"), sem("ms_root"), sem("rms_done"), sem("x_nat_in"),
            sem("added"))
        ln = LayerNorm(nc, ctx, "a_ln", sh, [tk, tv])
        xT_raw = [gated, squares, sq_sum, q_dec]

        def steps(eng, step):
            def one(h):
                step(h, h % 2, 0 <= h < HEADS, h + 1 < HEADS, h >= 1, h + 2 < HEADS)
            for h in (-1, 0, 1):
                one(h)
            with eng.Fori(2, HEADS - 3, 2) as h:
                step(h, 0, True, True, True, True)
                step(h + 1, 1, True, True, True, True)
            for h in (HEADS - 2, HEADS - 1, HEADS):
                one(h)

        block = ctx.enter_context(nc.Block())

        @block.sync
        def _(sp):
            for k in range(KB):
                sp.dma_start(xT_raw[k][:, :], xT[k * P:(k + 1) * P, :]).then_inc(x_in, 16)

            def load_weights(h, t):
                wait(sp, w_lo_done, 4 * (h - 1) + t + 1)
                sp.dma_start(w_raw[t][:, :, :], w[ds(h, 1), t].rearrange("a p k d -> (a p) k d")).then_inc(w_in[t], 16)

            def load_output_weights(h):
                wait(sp, ow_lo_done, h)
                sp.dma_start(ow_raw[:, :], ow[ds(h, 1)].rearrange("a p d -> (a p) d")).then_inc(ow_in, 16)

            def load_decays(h, b):
                wait(sp, attn, 2 * (h - 1))
                sp.dma_start(decay[b][:, :], decay_in[ds(h, 1)].rearrange("a p n -> (a p) n")).then_inc(
                    decay_in_sem[b], 16)

            def load(h, b):
                load_weights(h, 0)
                load_weights(h, 1)
                load_output_weights(h - 2)
                load_weights(h, 2)
                load_weights(h, 3)
                load_decays(h - 1, 1 - b)

            for h in range(2):
                for t in range(4):
                    load_weights(h, t)
            load_decays(0, 0)
            sp.dma_start(sh.x_nat[:, :, :], x.rearrange("(t p) d -> p t d", p=P)).then_inc(x_nat_in, 16)
            with sp.Fori(2, HEADS - 1, 2) as h:
                load(h, 0)
                load(h + 1, 1)
            load_output_weights(HEADS - 2)
            load_decays(HEADS - 1, 1)
            load_output_weights(HEADS - 1)

        @block.gpsimd
        def _(pool):
            pool.dma_start(norm_sb[:, :], norm_w).then_inc(const_in, 16)
            pool.memset(sh.ident[:, :], 0.0).then_inc(zeroed, 1)
            pool.wait_ge(zeroed, 1)
            pool.affine_select(out=sh.ident[:, :], in_=sh.ident[:, :], compare_op=ALU.not_equal, fill=1.0, base=0,
                               pattern=[[-1, P]], channel_multiplier=1).then_inc(zeroed, 1)
            pool.memset(ones[:, :], 1.0).then_inc(zeroed, 1)
            pool.memset(acc[:, :, :], 0.0).then_inc(zeroed, 1)

            def split_lo(h, t):
                pool.wait_ge(w_in[t], 16 * (h + 1))
                pool.wait_ge(w_hi_done, 4 * h + t + 1)
                wait(pool, proj, NG * (h - 1) + 2 * t + 2)
                pool.tensor_tensor(w_lo[t][:, :, :], w_raw[t][:, :, :], f(w_hi[t][:, :, :]),
                                   ALU.subtract).then_inc(w_lo_done, 1)

            for t in range(4):
                split_lo(0, t)
            pool.wait_ge(x_split, KB)
            pool.memset(sq_sum[:, :], 0.0).then_inc(zeroed, 1)
            pool.wait_ge(zeroed, 5)

            def half_out(h, b, j):
                cut = slice(j * HALF, (j + 1) * HALF)
                pool.wait_ge(squared, 2 * h + j + 1)
                wait(pool, sq_added, 2 * (h - 1) + j + 1)
                pool.tensor_tensor(sq_sum[:, cut], sq_sum[:, cut], squares[:, cut], ALU.add).then_inc(sq_added, 1)
                pool.wait_ge(ga_hi_done, 2 * h + j + 1)
                pool.wait_ge(gated_done, 2 * h + j + 1)
                wait(pool, y_done, NT * (h - 1))
                pool.tensor_tensor(ga_lo[b][:, cut], gated[:, cut], f(ga_hi[b][:, cut]),
                                   ALU.subtract).then_inc(ga_lo_done, 1)

            def step(h, b, attention, project, output, split):
                for s in range(NG):
                    if attention and s == 3:
                        pool.wait_ge(ow_in, 16 * (h + 1))
                        pool.wait_ge(ow_hi_done, h + 1)
                        wait(pool, y_done, NT * (h - 1))
                        pool.tensor_tensor(ow_lo[b][:, :], ow_raw[:, :], f(ow_hi[b][:, :]),
                                           ALU.subtract).then_inc(ow_lo_done, 1)
                    if attention and s == 6:
                        half_out(h, b, 0)
                    if split and s % 2:
                        split_lo(h + 2, s // 2)
                if attention:
                    half_out(h, b, 1)

            steps(pool, step)

        @block.scalar
        def _(act):
            def split_hi(h, t):
                act.wait_ge(w_in[t], 16 * (h + 1))
                wait(act, proj, NG * (h - 1) + 2 * t + 2)
                act.activation(w_hi[t][:, :, :], w_raw[t][:, :, :], ACT.Copy).then_inc(w_hi_done, 1)

            for k in range(KB):
                act.wait_ge(x_in, 16 * KB)
                act.activation(sh.xT_hi[:, k, :], xT_raw[k][:, :], ACT.Copy).then_inc(xt_hi_done, 1)
                split_hi(0, k)

            def to_nat(h, b, j):
                wait(act, attn, 2 * h)
                act.wait_ge(kv_tr, 4 * h + 2 * j + 1)
                act.wait_ge(decay_in_sem[b], 8 * h + 16 - 8 * b)
                act.activation(k_nat[:, CH * j:CH * (j + 1), :], tk[:, :].rearrange("p (c d) -> p c d", c=CH),
                               ACT.Copy, scale=k_decay[b]).then_inc(kv_nat, 1)
                act.wait_ge(kv_tr, 4 * h + 2 * j + 2)
                act.activation(v_nat[:, CH * j:CH * (j + 1), :], tv[:, :].rearrange("p (c d) -> p c d", c=CH),
                               ACT.Copy).then_inc(kv_nat, 1)

            def square(h, j):
                cut = slice(j * HALF, (j + 1) * HALF)
                act.wait_ge(attn, 2 * h + j + 1)
                wait(act, sq_added, 2 * (h - 1) + j + 1)
                act.activation(squares[:, cut], o_ps[:, :], ACT.Square).then_inc(squared, 1)

            def gated_hi(h, b, j):
                cut = slice(j * HALF, (j + 1) * HALF)
                act.wait_ge(gated_done, 2 * h + j + 1)
                wait(act, y_done, NT * (h - 1))
                act.activation(ga_hi[b][:, cut], gated[:, cut], ACT.Copy).then_inc(ga_hi_done, 1)

            def sigmoid(g, bg, s):
                act.wait_ge(proj, NG * g + s + 1)
                half = s % 2
                if s // 2 == GATE:
                    wait(act, gated_done, 2 * (g - 1))
                    out = qkvg[GATE][bg][:, half * HALF:(half + 1) * HALF]
                else:
                    wait(act, silu, 6 * g + s - 1 if s >= 2 else 6 * (g - 1) + 5 + s)
                    out = sig_tmp[half][:, :]
                act.activation(out, pj[half][:, :], ACT.Sigmoid).then_inc(sig, 1)

            def step(h, b, attention, project, output, split):
                for s in range(NG):
                    if attention:
                        if s in (0, 2):
                            to_nat(h, b, s // 2)
                        if s == 3:
                            act.wait_ge(ow_in, 16 * (h + 1))
                            wait(act, y_done, NT * (h - 1))
                            act.activation(ow_hi[b][:, :], ow_raw[:, :], ACT.Copy).then_inc(ow_hi_done, 1)
                        if s in (5, 7):
                            square(h, s // 6)
                        if s == 6:
                            gated_hi(h, b, 0)
                    if project:
                        sigmoid(h + 1, 1 - b, s)
                    if split and s % 2:
                        split_hi(h + 2, s // 2)
                if attention:
                    gated_hi(h, b, 1)

            steps(act, step)
            act.wait_ge(ms_ready, 1)
            act.activation(rms[:, :], ms[:, :], ACT.Ln).then_inc(ms_ln, 1)
            act.wait_ge(ms_ln, 1)
            act.activation(rms[:, :], rms[:, :], ACT.Exp, scale=-0.5).then_inc(ms_root, 1)
            ln.scalar(act)

        @block.tensor
        def _(pe):
            def project_group(g, s):
                t, half = s // 2, s % 2
                cut = slice(half * HALF, (half + 1) * HALF)
                pe.wait_ge(w_lo_done, 4 * g + t + 1)
                if s >= 2:
                    pe.wait_ge(silu, 6 * g + s - 1)
                else:
                    wait(pe, sig, NG * (g - 1) + 7 + s)
                for k in range(KB):
                    last = three_pass(pe, pj[half][:, :], w_hi[t][:, k, :], w_lo[t][:, k, :],
                                      sh.xT_hi[:, k, cut], sh.xT_lo[:, k, cut], k == 0, k == KB - 1)
                last.then_inc(proj, 1)

            def transposes(h, b, j):
                pe.wait_ge(silu, 6 * h + 5 + j)
                wait(pe, kv_nat, 4 * h + 2 * j)
                for t, out in ((1, tk), (2, tv)):
                    for c in range(CH):
                        at = (j * CH + c) * CHUNK
                        last = pe.transpose(out[:, c * CHUNK:(c + 1) * CHUNK], qkvg[t][b][:, at:at + CHUNK],
                                            sh.ident[:, :])
                    last.then_inc(kv_tr, 1)

            def scores(h, b, j):
                wait(pe, masked, 2 * h + j)
                for c in range(CH):
                    at = (j * CH + c) * CHUNK
                    last = pe.matmul(s_ps[:, c * CHUNK:(c + 1) * CHUNK], qkvg[1][b][:, at:at + CHUNK],
                                     qkvg[0][b][:, at:at + CHUNK], start=True, stop=True)
                last.then_inc(scored, 1)

            def updates(h, j):
                pe.wait_ge(kv_nat, 4 * h + 2 * j + 2)
                wait(pe, state_done, 7 * h + CH * j)
                for c in range(j * CH, min((j + 1) * CH, NT - 1)):
                    last = pe.matmul(u_ps[:, (c % CH) * HD:(c % CH + 1) * HD], k_nat[:, c, :], v_nat[:, c, :],
                                     start=True, stop=True)
                last.then_inc(upd, 1)

            def outputs(h, j):
                pe.wait_ge(masked, 2 * h + j + 1)
                pe.wait_ge(q_decayed, h + 1)
                wait(pe, squared, 2 * h + j)
                wait(pe, gated_done, 2 * h + j)
                for c in range(j * CH, (j + 1) * CH):
                    out = o_ps[:, (c % CH) * CHUNK:(c % CH + 1) * CHUNK]
                    at = c * CHUNK
                    last = pe.matmul(out, v_nat[:, c, :], s_masked[:, at:at + CHUNK], start=True, stop=(c == 0))
                    if c:
                        if c == j * CH or c == 1:
                            pe.wait_ge(state_done, 7 * h + (3 if j == 0 else 7))
                        last = pe.matmul(out, state[:, c, :], q_dec[:, at:at + CHUNK], start=False, stop=True)
                last.then_inc(attn, 1)

            def output_tile(h, b, t):
                pe.wait_ge(ga_lo_done, 2 * h + t // CH + 1)
                pe.wait_ge(ow_lo_done, h + 1)
                wait(pe, y_added, NT * h + t)
                cut = slice(t * P, (t + 1) * P)
                three_pass(pe, y_ps[:, :], ga_hi[b][:, cut], ga_lo[b][:, cut], ow_hi[b][:, :], ow_lo[b][:, :],
                           True, True).then_inc(y_done, 1)

            def step(h, b, attention, project, output, split):
                for s in range(NG):
                    if attention:
                        if s in (0, 2):
                            transposes(h, b, s // 2)
                        if s in (1, 3):
                            scores(h, b, s // 2)
                        if s in (4, 5):
                            updates(h, s - 4)
                        if s in (5, 7):
                            outputs(h, s // 6)
                    if project:
                        project_group(h + 1, s)
                    if output:
                        output_tile(h - 1, 1 - b, s)

            pe.wait_ge(x_split, KB)
            pe.wait_ge(zeroed, 5)
            steps(pe, step)
            pe.wait_ge(sq_added, 2 * HEADS)
            for t in range(NT):
                last = pe.matmul(s_ps[:, t:t + 1], sq_sum[:, t * P:(t + 1) * P], ones[:, :], start=True, stop=True)
            last.then_inc(ms_done, 1)
            ln.tensor(pe)

        @block.vector
        def _(dve):
            for k in range(KB):
                dve.wait_ge(xt_hi_done, k + 1)
                dve.wait_ge(x_in, 16 * KB)
                dve.tensor_tensor(sh.xT_lo[:, k, :], xT_raw[k][:, :], f(sh.xT_hi[:, k, :]),
                                  ALU.subtract).then_inc(x_split, 1)
            dve.wait_ge(x_split, KB)
            dve.wait_ge(const_in, 16)
            dve.wait_ge(zeroed, 5)

            def decay_q(h, b):
                dve.wait_ge(silu, 6 * h + 2)
                dve.wait_ge(decay_in_sem[b], 8 * h + 16 - 8 * b)
                wait(dve, attn, 2 * h)
                dve.tensor_tensor(q_dec[:, :].rearrange("p (c n) -> p c n", n=CHUNK),
                                  qkvg[0][b][:, :].rearrange("p (c n) -> p c n", n=CHUNK),
                                  q_decay[b].broadcast_to([P, NT, CHUNK]), ALU.mult).then_inc(q_decayed, 1)

            def mask_scores(h, b, j):
                dve.wait_ge(scored, 2 * h + j + 1)
                wait(dve, attn, 2 * (h - 1) + j + 1)
                dve.tensor_tensor(s_masked[:, j * HALF:(j + 1) * HALF].rearrange("p (c n) -> p c n", n=CHUNK),
                                  s_ps[:, :].rearrange("p (c n) -> p c n", n=CHUNK),
                                  mask[b].broadcast_to([P, CH, CHUNK]), ALU.mult).then_inc(masked, 1)

            def states(h, b, j):
                dve.wait_ge(upd, 2 * h + j + 1)
                wait(dve, attn, 2 * h)
                for c in range(j * CH, min((j + 1) * CH, NT - 1)):
                    u = u_ps[:, (c % CH) * HD:(c % CH + 1) * HD]
                    if c == 0:
                        ins = dve.tensor_copy(state[:, 1, :], u)
                    else:
                        dve.wait_ge(state_done, 7 * h + c)
                        ins = dve.scalar_tensor_tensor(out=state[:, c + 1, :], in0=state[:, c, :],
                                                       scalar=chunk_decay[b], in1=u,
                                                       op0=ALU.mult, op1=ALU.add)
                    ins.then_inc(state_done, 1)

            def gate_out(h, b, j):
                cut = slice(j * HALF, (j + 1) * HALF)
                dve.wait_ge(squared, 2 * h + j + 1)
                dve.wait_ge(sig, NG * h + 7 + j)
                wait(dve, ga_lo_done, 2 * (h - 1) + j + 1)
                dve.scalar_tensor_tensor(out=gated[:, cut], in0=o_ps[:, :], scalar=norm_sb[:, ds(h, 1)],
                                         in1=qkvg[GATE][b][:, cut], op0=ALU.mult, op1=ALU.mult).then_inc(gated_done, 1)

            def silu_half(g, bg, s):
                dve.wait_ge(sig, NG * g + s + 1)
                wait(dve, attn, 2 * (g - 1))
                half = s % 2
                dve.tensor_tensor(qkvg[s // 2][bg][:, half * HALF:(half + 1) * HALF], pj[half][:, :],
                                  sig_tmp[half][:, :], ALU.mult).then_inc(silu, 1)

            def add_output(h, t):
                dve.wait_ge(y_done, NT * h + t + 1)
                wait(dve, y_added, NT * (h - 1) + t + 1)
                dve.tensor_tensor(acc[:, t, :], acc[:, t, :], y_ps[:, :], ALU.add).then_inc(y_added, 1)

            def step(h, b, attention, project, output, split):
                for s in range(NG):
                    if attention:
                        if s == 0:
                            decay_q(h, b)
                        if s in (1, 3):
                            mask_scores(h, b, s // 2)
                        if s in (4, 5):
                            states(h, b, s - 4)
                        if s in (5, 7):
                            gate_out(h, b, s // 6)
                    if project and s // 2 < GATE:
                        silu_half(h + 1, 1 - b, s)
                    if output:
                        add_output(h - 1, s)

            steps(dve, step)
            dve.wait_ge(ms_done, 1)
            dve.tensor_scalar(ms[:, :], s_ps[:, 0:NT], 1.0 / (HEADS * HD), L0_EPS, ALU.mult,
                              ALU.add).then_inc(ms_ready, 1)
            dve.wait_ge(ms_ready, 1)
            dve.wait_ge(ms_root, 1)
            ln.rsqrt_refine(dve, ms[:, :], rms[:, :], sh.tmp[:, :])
            dve.wait_ge(x_nat_in, 16)
            dve.wait_ge(y_added, NT * HEADS)
            for t in range(NT):
                dve.scalar_tensor_tensor(out=sh.x_nat[:, t, :], in0=acc[:, t, :], scalar=rms[:, t:t + 1],
                                         in1=sh.x_nat[:, t, :], op0=ALU.mult, op1=ALU.add).then_inc(added, 1)
                dve.wait_ge(added, t + 1)
                ln.vector_stats(dve, t)
            ln.vector(dve)


EXPERTS = 8
RANK = 64


def l0_experts(nc, sh, router, lora_a, lora_b):
    with ExitStack() as ctx:
        def sb(name, shape, dt=F32):
            return ctx.enter_context(nc.sbuf_tensor(f"e_{name}", shape, dt))

        def bank(name, shape):
            return ctx.enter_context(nc.psum_tensor(f"e_{name}", shape, F32))

        def sem(name):
            return ctx.enter_context(nc.semaphore(f"e_{name}"))

        widths = (EXPERTS, EXPERTS * RANK, D)
        raw = [sb(f"raw{i}", [P, KB, n]) for i, n in enumerate(widths)]
        hi = [sb(f"hi{i}", [P, KB, n], F32R) for i, n in enumerate(widths)]
        lo = [sb(f"lo{i}", [P, KB, n], F32R) for i, n in enumerate(widths)]
        logits = sb("logits", [P, NT, EXPERTS])
        top = sb("top", [P, NT, 8])
        prob = sb("prob", [P, NT, EXPERTS])
        index = sb("index", [P, NT, 8], U32)
        index_f = sb("index_f", [P, NT, 8])
        weight = sb("weight", [P, NT, EXPERTS])
        other = sb("other", [P, NT, EXPERTS])
        total = sb("total", [P, NT, 1])
        iota_i = sb("iota_i", [P, EXPERTS], I32)
        iota = sb("iota", [P, 1, EXPERTS])
        scaled = [sb(f"scaled{i}", [P, EXPERTS * RANK]) for i in range(2)]
        hT_hi = [sb(f"hT_hi{i}", [P, KB, P], F32R) for i in range(2)]
        hT_lo = [sb(f"hT_lo{i}", [P, KB, P], F32R) for i in range(2)]

        lg = bank("lg", [P, HALF])
        h_ps = [bank(f"h_ps{i}", [P, HALF]) for i in range(2)]
        t_ps = [bank(f"t_ps{i}", [P, HALF]) for i in range(2)]
        y_ps = [bank(f"y_ps{i}", [P, HALF]) for i in range(2)]

        w_in = [sem(f"w_in{i}") for i in range(3)]
        w_hi, w_lo = sem("w_hi"), sem("w_lo")
        iota_ready = sem("iota_ready")
        logits_ready, shifted, exp_ready = sem("logits_ready"), sem("shifted"), sem("exp_ready")
        h_ready, h_scaled = sem("h_ready"), sem("h_scaled")
        hT_ready, hT_hi_ready, hT_lo_ready = sem("hT_ready"), sem("hT_hi_ready"), sem("hT_lo_ready")
        y_ready, y_added = sem("y_ready"), sem("y_added")
        ln = LayerNorm(nc, ctx, "e_ln", sh, t_ps)

        block = ctx.enter_context(nc.Block())

        @block.sync
        def _(sp):
            for i, w in enumerate((router, lora_a, lora_b)):
                sp.dma_start(raw[i][:, :, :], w).then_inc(w_in[i], 16)

        @block.gpsimd
        def _(pool):
            pool.iota(iota_i[:, :], pattern=[[1, EXPERTS]], base=0, channel_multiplier=0).then_inc(iota_ready, 1)

        @block.scalar
        def _(act):
            for i in range(3):
                act.wait_ge(w_in[i], 16)
                act.activation(hi[i][:, :, :], raw[i][:, :, :], ACT.Copy).then_inc(w_hi, 1)
            act.wait_ge(shifted, 1)
            act.activation(prob[:, :, :], logits[:, :, :], ACT.Exp).then_inc(exp_ready, 1)
            for t in range(NT):
                act.wait_ge(hT_ready, t + 1)
                if t >= 2:
                    act.wait_ge(y_ready, t - 1)
                act.activation(hT_hi[t % 2][:, :, :], t_ps[t % 2][:, :].rearrange("p (k n) -> p k n", k=KB),
                               ACT.Copy).then_inc(hT_hi_ready, 1)
            ln.scalar(act)

        @block.tensor
        def _(pe):
            def product(out, lhs_hi, lhs_lo, i):
                for k in range(KB):
                    last = three_pass(pe, out, lhs_hi(k), lhs_lo(k), hi[i][:, k, :], lo[i][:, k, :],
                                      k == 0, k == KB - 1)
                return last

            def x_part(part, t):
                return lambda k: part[:, k, t * P:(t + 1) * P]

            pe.wait_ge(w_lo, 1)
            for t in range(NT):
                last = product(lg[:, t * EXPERTS:(t + 1) * EXPERTS], x_part(sh.xT_hi, t), x_part(sh.xT_lo, t), 0)
            last.then_inc(logits_ready, 1)
            for i in range(NT + 2):
                if i < NT:
                    if i == 0:
                        pe.wait_ge(w_lo, 2)
                    if i >= 2:
                        pe.wait_ge(h_scaled, i - 1)
                    product(h_ps[i % 2][:, :], x_part(sh.xT_hi, i), x_part(sh.xT_lo, i), 1).then_inc(h_ready, 1)
                if 1 <= i <= NT:
                    t = i - 1
                    pe.wait_ge(h_scaled, t + 1)
                    if t >= 2:
                        pe.wait_ge(hT_lo_ready, t - 1)
                    for k in range(KB):
                        last = pe.transpose(t_ps[t % 2][:, k * P:(k + 1) * P], scaled[t % 2][:, k * P:(k + 1) * P],
                                            sh.ident[:, :])
                    last.then_inc(hT_ready, 1)
                if i >= 2:
                    t = i - 2
                    if t == 0:
                        pe.wait_ge(w_lo, 3)
                    pe.wait_ge(hT_lo_ready, t + 1)
                    if t >= 2:
                        pe.wait_ge(y_added, t - 1)
                    product(y_ps[t % 2][:, :], lambda k: hT_hi[t % 2][:, k, :], lambda k: hT_lo[t % 2][:, k, :],
                            2).then_inc(y_ready, 1)
            ln.tensor(pe)

        @block.vector
        def _(dve):
            link = ln.link
            dve.wait_ge(iota_ready, 1)
            link(dve, dve.tensor_copy(iota[:, 0, :], iota_i[:, :]))
            for i in range(3):
                dve.wait_ge(w_hi, i + 1)
                dve.wait_ge(w_in[i], 16)
                dve.tensor_tensor(lo[i][:, :, :], raw[i][:, :, :], f(hi[i][:, :, :]), ALU.subtract).then_inc(w_lo, 1)
                if i == 0:
                    dve.wait_ge(logits_ready, 1)
                    lg_t = lg[:, 0:NT * EXPERTS].rearrange("p (t e) -> p t e", e=EXPERTS)
                    link(dve, dve.tensor_reduce(total[:, :, :], lg_t, AX_X, ALU.max))
                    dve.tensor_tensor(logits[:, :, :], lg_t, total[:, :, :].broadcast_to([P, NT, EXPERTS]),
                                      ALU.subtract).then_inc(shifted, 1)
            dve.wait_ge(exp_ready, 1)
            wide = [P, NT, EXPERTS]
            link(dve, dve.tensor_reduce(total[:, :, :], prob[:, :, :], AX_X, ALU.add))
            link(dve, dve.reciprocal(total[:, :, :], total[:, :, :]))
            link(dve, dve.tensor_tensor(prob[:, :, :], prob[:, :, :], total[:, :, :].broadcast_to(wide), ALU.mult))
            for t in range(NT):
                last = dve.max(top[:, t, :], prob[:, t, :])
                link(dve, last)
                last = dve.max_index(index[:, t, :], top[:, t, :], prob[:, t, :])
                link(dve, last)
            link(dve, dve.tensor_copy(index_f[:, :, :], index[:, :, :]))
            link(dve, dve.tensor_tensor(total[:, :, :], top[:, :, 0:1], top[:, :, 1:2], ALU.add))
            link(dve, dve.reciprocal(total[:, :, :], total[:, :, :]))
            link(dve, dve.tensor_tensor(top[:, :, 0:2], top[:, :, 0:2], total[:, :, :].broadcast_to([P, NT, 2]), ALU.mult))
            for n, out in ((0, weight), (1, other)):
                link(dve, dve.tensor_tensor(out[:, :, :], iota[:, :, :].broadcast_to(wide),
                                            index_f[:, :, n:n + 1].broadcast_to(wide), ALU.is_equal))
                link(dve, dve.tensor_tensor(out[:, :, :], out[:, :, :], top[:, :, n:n + 1].broadcast_to(wide), ALU.mult))
            link(dve, dve.tensor_tensor(weight[:, :, :], weight[:, :, :], other[:, :, :], ALU.add))

            for i in range(NT + 2):
                if i < NT:
                    dve.wait_ge(h_ready, i + 1)
                    if i >= 2:
                        dve.wait_ge(hT_ready, i - 1)
                    dve.tensor_tensor(scaled[i % 2][:, :].rearrange("p (e r) -> p e r", e=EXPERTS),
                                      h_ps[i % 2][:, :].rearrange("p (e r) -> p e r", e=EXPERTS),
                                      weight[:, i, :].unsqueeze(2).broadcast_to([P, EXPERTS, RANK]),
                                      ALU.mult).then_inc(h_scaled, 1)
                if 1 <= i <= NT:
                    t = i - 1
                    dve.wait_ge(hT_hi_ready, t + 1)
                    if t >= 2:
                        dve.wait_ge(y_ready, t - 1)
                    dve.tensor_tensor(hT_lo[t % 2][:, :, :], t_ps[t % 2][:, :].rearrange("p (k n) -> p k n", k=KB),
                                      f(hT_hi[t % 2][:, :, :]), ALU.subtract).then_inc(hT_lo_ready, 1)
                if i >= 2:
                    t = i - 2
                    dve.wait_ge(y_ready, t + 1)
                    dve.tensor_tensor(sh.x_nat[:, t, :], sh.x_nat[:, t, :], y_ps[t % 2][:, :],
                                      ALU.add).then_inc(y_added, 1)
                    dve.wait_ge(y_added, t + 1)
                    ln.vector_stats(dve, t)
            ln.vector(dve)


L1_EPS = 1e-6


def l1_attention(nc, sh, w, ow, bias, bo, gains):
    NG = 6
    K, Q, V = range(3)
    with ExitStack() as ctx:
        def sb(name, shape, dt=F32):
            return ctx.enter_context(nc.sbuf_tensor(f"b_{name}", shape, dt))

        def bank(name, shape):
            return ctx.enter_context(nc.psum_tensor(f"b_{name}", shape, F32))

        def sem(name):
            return ctx.enter_context(nc.semaphore(f"b_{name}"))

        w_raw = [sb(f"w_raw{i}", [P, KB, HD]) for i in range(2)]
        w_hi = [sb(f"w_hi{i}", [P, KB, HD], F32R) for i in range(2)]
        w_lo = [sb(f"w_lo{i}", [P, KB, HD], F32R) for i in range(2)]
        ow_raw = sb("ow_raw", [P, D])
        ow_hi = [sb(f"ow_hi{b}", [P, D], F32R) for b in range(2)]
        ow_lo = [sb(f"ow_lo{b}", [P, D], F32R) for b in range(2)]
        k_hi = [sb(f"k_hi{b}", [P, TOK], F32R) for b in range(2)]
        k_lo = [sb(f"k_lo{b}", [P, TOK], F32R) for b in range(2)]
        q_hi = [sb(f"q_hi{b}", [P, TOK], F32R) for b in range(2)]
        q_lo = [sb(f"q_lo{b}", [P, TOK], F32R) for b in range(2)]
        v_hi = [sb(f"v_hi{b}", [P, NT, HD], F32R) for b in range(2)]
        v_lo = [sb(f"v_lo{b}", [P, NT, HD], F32R) for b in range(2)]
        q_rstd = [sb(f"q_rstd{b}", [P, NT]) for b in range(2)]
        lin = [sb(f"lin{i}", [P, HALF]) for i in range(2)]
        sq = sb("sq", [P, HALF])
        sq_sum = sb("sq_sum", [P, CH])
        mean_sq = sb("mean_sq", [P, CH])
        k_rstd = sb("k_rstd", [P, CH])
        prob = [sb(f"prob{i}", [P, TOK]) for i in range(2)]
        row_max = sb("row_max", [P, NT])
        shift = sb("shift", [P, NT])
        row_sum = [sb(f"row_sum{b}", [P, NT]) for b in range(2)]
        row_inv = sb("row_inv", [P, NT])
        pT_hi = [sb(f"pT_hi{j}", [P, NT, HALF], F32R) for j in range(2)]
        pT_lo = [sb(f"pT_lo{j}", [P, NT, HALF], F32R) for j in range(2)]
        o_hi = sb("o_hi", [P, TOK], F32R)
        o_lo = sb("o_lo", [P, TOK], F32R)
        bias_sb = sb("bias_sb", [P, 3, HEADS])
        bias_now = sb("bias_now", [P, 3, 1])
        gain_in = sb("gain_in", [P, 2])
        gain = sb("gain", [P, 1])
        power = sb("power", [P, CH])
        bo_sb = prob[0][:, 0:D]

        s_ps = bank("s_ps", [P, TOK])
        t_ps = bank("t_ps", [P, TOK])
        pj = bank("pj", [P, HALF])
        m_ps = bank("m_ps", [P, HALF])
        o_ps = bank("o_ps", [P, HALF])
        y_ps = bank("y_ps", [P, HALF])

        w_in = [sem(f"w_in{i}") for i in range(2)]
        w_hi_done, w_lo_done = sem("w_hi_done"), sem("w_lo_done")
        ow_in, ow_hi_done, ow_lo_done = sem("ow_in"), sem("ow_hi_done"), sem("ow_lo_done")
        proj = sem("proj")
        taken = sem("taken")
        sq_tr = sem("sq_tr")
        summed = sem("summed")
        mean_ready = sem("mean_ready")
        rstd_ready = sem("rstd_ready")
        spread = sem("spread")
        k_scaled, k_hi_done, k_lo_done = sem("k_scaled"), sem("k_hi_done"), sem("k_lo_done")
        q_hi_done, q_lo_done = sem("q_hi_done"), sem("q_lo_done")
        v_tr, v_hi_done, v_lo_done = sem("v_tr"), sem("v_hi_done"), sem("v_lo_done")
        scored, max_done, shift_done, exp_done = sem("scored"), sem("max_done"), sem("shift_done"), sem("exp_done")
        inv_done = sem("inv_done")
        p_tr, pT_hi_done, pT_lo_done = sem("p_tr"), sem("pT_hi_done"), sem("pT_lo_done")
        pv, o_hi_done, o_lo_done = sem("pv"), sem("o_hi_done"), sem("o_lo_done")
        y_done, y_added = sem("y_done"), sem("y_added")
        bias_picked = sem("bias_picked")
        const_in, bias_added, gain_ready, set_up = sem("const_in"), sem("bias_added"), sem("gain_ready"), sem("set_up")
        ln = LayerNorm(nc, ctx, "b_ln", sh, [pj, m_ps])

        def steps(eng, step):
            def one(h):
                step(h, h % 2, 0 <= h < HEADS, h >= 1, h + 1 < HEADS, h + 2 < HEADS)
            for h in (-1, 0, 1):
                one(h)
            with eng.Fori(2, HEADS - 3, 2) as h:
                step(h, 0, True, True, True, True)
                step(h + 1, 1, True, True, True, True)
            for h in (HEADS - 2, HEADS - 1, HEADS):
                one(h)

        OUTPUT_TILES = [[0], [1], [2], [3], [], [4], [5, 6], [7]]
        VALUES = [None, (-1, 1, (0, 1)), (-1, 1, (1, 2)), (-1, 1, (2, 4)), (-1, 1, (4, 6)), (-1, 1, (6, 8)),
                  (0, 0, (0, 4)), (0, 0, (4, 8))]
        SPLITS = {2: (V, 1), 4: (K, 2), 6: (Q, 2)}

        def to_split(s, project, more):
            if s not in SPLITS:
                return None
            kind, ahead = SPLITS[s]
            return (kind, ahead) if (project if ahead == 1 else more) else None

        def slot_loads(h, b, kind):
            return 8 * (3 * h + kind) + (8 if (b + kind) % 2 else 16)

        block = ctx.enter_context(nc.Block())

        @block.sync
        def _(sp):
            sp.dma_start(bias_sb[:, :, :], bias).then_inc(const_in, 16)
            sp.dma_start(gain_in[:, :], gains).then_inc(const_in, 16)
            sp.dma_start(bo_sb, bo.partition_broadcast(P)).then_inc(const_in, 16)

            def load_weights(h, b, kind):
                wait(sp, w_lo_done, 3 * h + kind - 1)
                slot = (b + kind) % 2
                sp.dma_start(w_raw[slot][:, :, :], w[ds(h, 1), kind].rearrange("a p k d -> (a p) k d")).then_inc(
                    w_in[slot], 16)

            def load_output_weights(h):
                wait(sp, ow_lo_done, h)
                sp.dma_start(ow_raw[:, :], ow[ds(h, 1)].rearrange("a p d -> (a p) d")).then_inc(ow_in, 16)

            def load(h, b):
                load_weights(h, b, K)
                load_weights(h, b, Q)
                load_output_weights(h - 2)
                load_weights(h, b, V)

            for h in range(2):
                for kind in (K, Q, V):
                    load_weights(h, h, kind)
            with sp.Fori(2, HEADS - 1, 2) as h:
                load(h, 0)
                load(h + 1, 1)
            load_output_weights(HEADS - 2)
            load_output_weights(HEADS - 1)

        @block.gpsimd
        def _(pool):
            pool.memset(power[:, :], -0.5).then_inc(set_up, 1)
            pool.wait_ge(set_up, 1)

            def split_lo(h, b, kind):
                slot = (b + kind) % 2
                pool.wait_ge(w_in[slot], slot_loads(h, b, kind))
                pool.wait_ge(w_hi_done, 3 * h + kind + 1)
                wait(pool, proj, 2 * (3 * h + kind - 1))
                pool.tensor_tensor(w_lo[slot][:, :, :], w_raw[slot][:, :, :], f(w_hi[slot][:, :, :]),
                                   ALU.subtract).then_inc(w_lo_done, 1)

            split_lo(0, 0, K)
            split_lo(0, 0, Q)

            def inverse_rms(g, bg, s):
                pool.wait_ge(mean_ready, 4 * g + s + 1)
                if s < 2:
                    wait(pool, spread, 2 * g + s)
                    out = k_rstd[:, :]
                else:
                    wait(pool, exp_done, NT * (g - 1))
                    out = q_rstd[bg][:, (s - 2) * CH:(s - 1) * CH]
                pool.tensor_tensor(out, mean_sq[:, :], power[:, :], ALU.pow).then_inc(rstd_ready, 1)

            def k_low(g, bg, j):
                cut = slice(j * HALF, (j + 1) * HALF)
                pool.wait_ge(k_hi_done, 2 * g + j + 1)
                wait(pool, scored, NT * (g - 1))
                pool.tensor_tensor(k_lo[bg][:, cut], lin[j][:, :], f(k_hi[bg][:, cut]),
                                   ALU.subtract).then_inc(k_lo_done, 1)

            def step(h, b, attention, rest, project, more):
                for s in range(NT):
                    if attention and s == 4:
                        pool.wait_ge(ow_in, 16 * (h + 1))
                        pool.wait_ge(ow_hi_done, h + 1)
                        wait(pool, y_done, NT * (h - 1))
                        pool.tensor_tensor(ow_lo[b][:, :], ow_raw[:, :], f(ow_hi[b][:, :]),
                                           ALU.subtract).then_inc(ow_lo_done, 1)
                    if project and 1 <= s <= 4:
                        inverse_rms(h + 1, 1 - b, s - 1)
                    if project and 1 <= s <= 2:
                        k_low(h + 1, 1 - b, s - 1)
                    split = to_split(s, project, more)
                    if split:
                        kind, ahead = split
                        split_lo(h + ahead, (b + ahead) % 2, kind)

            steps(pool, step)

        @block.scalar
        def _(act):
            def split_hi(h, b, kind):
                slot = (b + kind) % 2
                act.wait_ge(w_in[slot], slot_loads(h, b, kind))
                wait(act, proj, 2 * (3 * h + kind - 1))
                act.activation(w_hi[slot][:, :, :], w_raw[slot][:, :, :], ACT.Copy).then_inc(w_hi_done, 1)

            split_hi(0, 0, K)
            split_hi(0, 0, Q)

            def out_hi(h, j):
                act.wait_ge(pv, 2 * h + j + 1)
                wait(act, y_done, NT * (h - 1) + CH * (j + 1))
                act.activation(o_hi[:, j * HALF:(j + 1) * HALF], o_ps[:, :], ACT.Copy).then_inc(o_hi_done, 1)

            def prob_hi(h, t):
                j, at = t // CH, (t % CH) * P
                act.wait_ge(p_tr, NT * h + t + 1)
                wait(act, pv, 2 * (h - 1) + j + 1)
                act.activation(pT_hi[j][:, :, at:at + P], t_ps[:, :].rearrange("p (m n) -> p m n", m=NT),
                               ACT.Copy).then_inc(pT_hi_done, 1)

            def exponent(h, b, t):
                act.wait_ge(shift_done, NT * h + t + 1)
                wait(act, p_tr, NT * h + t - 1)
                act.activation(prob[t % 2][:, :], s_ps[:, :], ACT.Exp, bias=shift[:, t:t + 1],
                               scale=q_rstd[b][:, t:t + 1], accum_out=row_sum[b][:, t:t + 1]).then_inc(exp_done, 1)

            def take(g, bg, s):
                act.wait_ge(proj, NG * g + s + 1)
                if s < 2:
                    wait(act, v_tr, 2 * (g - 1) + s + 1)
                elif s < 4:
                    act.wait_ge(k_lo_done, 2 * g + s - 1)
                else:
                    act.wait_ge(q_lo_done, 2 * g + s - 3)
                b_ap = bias_now[:, s // 2, :]
                act.wait_ge(bias_picked, g + 1)
                ins = act.activation(lin[s % 2][:, :], pj[:, :], ACT.Identity, bias=b_ap)
                if s < 4:
                    wait(act, sq_tr, 4 * g + s)
                    ins = act.activation(sq[:, :], pj[:, :], ACT.Square, bias=b_ap)
                ins.then_inc(taken, 1)

            def k_high(g, bg, j):
                act.wait_ge(k_scaled, 2 * g + j + 1)
                wait(act, scored, NT * (g - 1))
                act.activation(k_hi[bg][:, j * HALF:(j + 1) * HALF], lin[j][:, :], ACT.Copy).then_inc(k_hi_done, 1)

            def v_high(g, bg, j):
                act.wait_ge(v_tr, 2 * g + j + 1)
                wait(act, pv, 2 * (g - 1))
                act.activation(v_hi[bg][:, j * CH:(j + 1) * CH, :], pj[:, :].rearrange("p (c d) -> p c d", c=CH),
                               ACT.Copy).then_inc(v_hi_done, 1)

            def step(h, b, attention, rest, project, more):
                for s in range(NT):
                    if project and s >= NG:
                        v_high(h + 1, 1 - b, s - NG)
                    if project and s < NG:
                        take(h + 1, 1 - b, s)
                    if rest and s == 5:
                        out_hi(h - 1, 1)
                    if attention and s == 7:
                        out_hi(h, 0)
                    if rest and s == 0:
                        prob_hi(h - 1, NT - 1)
                    if attention and s:
                        prob_hi(h, s - 1)
                    if attention:
                        exponent(h, b, s)
                    if project and 1 <= s <= 2:
                        k_high(h + 1, 1 - b, s - 1)
                    if attention and s == 4:
                        act.wait_ge(ow_in, 16 * (h + 1))
                        wait(act, y_done, NT * (h - 1))
                        act.activation(ow_hi[b][:, :], ow_raw[:, :], ACT.Copy).then_inc(ow_hi_done, 1)
                    split = to_split(s, project, more)
                    if split:
                        kind, ahead = split
                        split_hi(h + ahead, (b + ahead) % 2, kind)

            steps(act, step)
            ln.scalar(act)

        @block.tensor
        def _(pe):
            def transpose_squares(g, s):
                pe.wait_ge(taken, NG * g + s + 1)
                if s % 3 == 0:
                    wait(pe, summed, 4 * g + s)
                else:
                    pe.wait_ge(k_scaled, 2 * g + s)
                for c in range(CH):
                    last = pe.transpose(m_ps[:, c * P:(c + 1) * P], sq[:, c * P:(c + 1) * P], sh.ident[:, :])
                last.then_inc(sq_tr, 1)

            def spread_k(g, j):
                pe.wait_ge(rstd_ready, 4 * g + j + 1)
                for c in range(CH):
                    last = pe.matmul(m_ps[:, c * P:(c + 1) * P], k_rstd[:, c:c + 1].broadcast_to([P, P]),
                                     sh.ident[:, :], start=True, stop=True)
                last.then_inc(spread, 1)

            def values(h, b, j, blocks):
                if blocks[0] == 0:
                    pe.wait_ge(pT_lo_done, NT * h + CH * (j + 1))
                    pe.wait_ge(v_lo_done, 2 * h + 2)
                    wait(pe, o_lo_done, 2 * h + j)
                for m in range(*blocks):
                    last = three_pass(pe, o_ps[:, :], v_hi[b][:, m, :], v_lo[b][:, m, :], pT_hi[j][:, m, :],
                                      pT_lo[j][:, m, :], m == 0, m == NT - 1)
                if blocks[1] == NT:
                    last.then_inc(pv, 1)

            def scores(h, b, t):
                if t == 0:
                    pe.wait_ge(k_lo_done, 2 * h + 2)
                    pe.wait_ge(q_lo_done, 2 * h + 2)
                wait(pe, exp_done, NT * h + t)
                cut = slice(t * P, (t + 1) * P)
                for j in range(2):
                    keys = slice(j * HALF, (j + 1) * HALF)
                    last = three_pass(pe, s_ps[:, keys], q_hi[b][:, cut], q_lo[b][:, cut], k_hi[b][:, keys],
                                      k_lo[b][:, keys], True, True)
                last.then_inc(scored, 1)

            def transpose_probs(h, t):
                pe.wait_ge(exp_done, NT * h + t + 1)
                wait(pe, pT_lo_done, NT * h + t)
                for m in range(NT):
                    cut = slice(m * P, (m + 1) * P)
                    last = pe.transpose(t_ps[:, cut], prob[t % 2][:, cut], sh.ident[:, :])
                last.then_inc(p_tr, 1)

            def project_group(g, bg, s):
                kind, half = s // 2, s % 2
                slot = (bg + kind) % 2
                pe.wait_ge(w_lo_done, 3 * g + kind + 1)
                if s == 0:
                    wait(pe, v_lo_done, 2 * g)
                else:
                    pe.wait_ge(taken, NG * g + s)
                cut = slice(half * HALF, (half + 1) * HALF)
                for k in range(KB):
                    last = three_pass(pe, pj[:, :], w_hi[slot][:, k, :], w_lo[slot][:, k, :], sh.xT_hi[:, k, cut],
                                      sh.xT_lo[:, k, cut], k == 0, k == KB - 1)
                last.then_inc(proj, 1)

            def transpose_v(g, j):
                pe.wait_ge(taken, NG * (g + 1))
                if j:
                    pe.wait_ge(v_lo_done, 2 * g + 1)
                for c in range(CH):
                    last = pe.transpose(pj[:, c * P:(c + 1) * P], lin[j][:, c * P:(c + 1) * P], sh.ident[:, :])
                last.then_inc(v_tr, 1)

            def output_tile(h, b, t):
                pe.wait_ge(o_lo_done, 2 * h + t // CH + 1)
                pe.wait_ge(ow_lo_done, h + 1)
                wait(pe, y_added, NT * h + t)
                cut = slice(t * P, (t + 1) * P)
                three_pass(pe, y_ps[:, :], o_hi[:, cut], o_lo[:, cut], ow_hi[b][:, :], ow_lo[b][:, :],
                           True, True).then_inc(y_done, 1)

            def step(h, b, attention, rest, project, more):
                for s in range(NT):
                    if project and s < NG:
                        project_group(h + 1, 1 - b, s)
                    if project and 1 <= s <= 4:
                        transpose_squares(h + 1, s - 1)
                    if project and s >= NG:
                        transpose_v(h + 1, s - NG)
                    if VALUES[s]:
                        ahead, j, blocks = VALUES[s]
                        if (attention, rest)[-ahead]:
                            values(h + ahead, (b + ahead) % 2, j, blocks)
                    if rest and s == 0:
                        transpose_probs(h - 1, NT - 1)
                    if attention and s:
                        transpose_probs(h, s - 1)
                    if rest and s == 6:
                        output_tile(h - 1, 1 - b, OUTPUT_TILES[s][0])
                    if attention:
                        scores(h, b, s)
                    if project and 1 <= s <= 2:
                        spread_k(h + 1, s - 1)
                    if rest and OUTPUT_TILES[s]:
                        output_tile(h - 1, 1 - b, OUTPUT_TILES[s][-1])

            steps(pe, step)
            ln.tensor(pe)

        @block.vector
        def _(dve):
            dve.wait_ge(const_in, 48)
            ln.link(dve, dve.tensor_tensor(gain[:, :], gain_in[:, 0:1], gain_in[:, 1:2], ALU.mult))
            dve.tensor_scalar(gain[:, :], gain[:, :], float(HD) ** -0.5, None, ALU.mult).then_inc(gain_ready, 1)
            for t in range(NT):
                dve.tensor_tensor(sh.x_nat[:, t, :], sh.x_nat[:, t, :], bo_sb, ALU.add).then_inc(bias_added, 1)
            dve.wait_ge(gain_ready, 1)
            dve.wait_ge(bias_added, NT)

            def maxima(h, b, t):
                dve.wait_ge(scored, NT * h + t + 1)
                dve.tensor_reduce(row_max[:, t:t + 1], s_ps[:, :], AX_X, ALU.max).then_inc(max_done, 1)
                dve.wait_ge(max_done, NT * h + t + 1)
                if t == 0:
                    dve.wait_ge(rstd_ready, 4 * h + 4)
                dve.tensor_scalar(shift[:, t:t + 1], row_max[:, t:t + 1], q_rstd[b][:, t:t + 1], -1.0,
                                  ALU.mult, ALU.mult).then_inc(shift_done, 1)

            def prob_lo(h, t):
                j, at = t // CH, (t % CH) * P
                dve.wait_ge(pT_hi_done, NT * h + t + 1)
                dve.tensor_tensor(pT_lo[j][:, :, at:at + P], t_ps[:, :].rearrange("p (m n) -> p m n", m=NT),
                                  f(pT_hi[j][:, :, at:at + P]), ALU.subtract).then_inc(pT_lo_done, 1)

            def invert_sums(h, b):
                dve.wait_ge(exp_done, NT * h + NT)
                wait(dve, y_added, NT * h)
                dve.reciprocal(row_inv[:, :], row_sum[b][:, :]).then_inc(inv_done, 1)

            def means(g, s):
                dve.wait_ge(sq_tr, 4 * g + s + 1)
                dve.tensor_reduce(sq_sum[:, :], m_ps[:, :].rearrange("p (c n) -> p c n", c=CH), AX_X,
                                  ALU.add).then_inc(summed, 1)
                dve.wait_ge(summed, 4 * g + s + 1)
                wait(dve, rstd_ready, 4 * g + s)
                dve.tensor_scalar(mean_sq[:, :], sq_sum[:, :], 1.0 / HD, L1_EPS, ALU.mult,
                                  ALU.add).then_inc(mean_ready, 1)

            def scale_k(g, j):
                dve.wait_ge(spread, 2 * g + j + 1)
                dve.tensor_tensor(lin[j][:, :], lin[j][:, :], m_ps[:, :], ALU.mult).then_inc(k_scaled, 1)

            def split_q(g, bg, j):
                cut = slice(j * HALF, (j + 1) * HALF)
                dve.wait_ge(taken, NG * g + j + 3)
                wait(dve, scored, NT * (g - 1))
                dve.tensor_scalar(q_hi[bg][:, cut], lin[j][:, :], gain[:, 0:1], None, ALU.mult).then_inc(q_hi_done, 1)
                dve.wait_ge(q_hi_done, 2 * g + j + 1)
                dve.scalar_tensor_tensor(out=q_lo[bg][:, cut], in0=lin[j][:, :], scalar=gain[:, 0:1],
                                         in1=f(q_hi[bg][:, cut]), op0=ALU.mult, op1=ALU.subtract).then_inc(q_lo_done, 1)

            def v_low(g, bg, j):
                dve.wait_ge(v_hi_done, 2 * g + j + 1)
                dve.tensor_tensor(v_lo[bg][:, j * CH:(j + 1) * CH, :], pj[:, :].rearrange("p (c d) -> p c d", c=CH),
                                  f(v_hi[bg][:, j * CH:(j + 1) * CH, :]), ALU.subtract).then_inc(v_lo_done, 1)

            def out_lo(h, j):
                cut = slice(j * HALF, (j + 1) * HALF)
                dve.wait_ge(o_hi_done, 2 * h + j + 1)
                dve.tensor_tensor(o_lo[:, cut], o_ps[:, :], f(o_hi[:, cut]), ALU.subtract).then_inc(o_lo_done, 1)

            def add_output(h, t):
                dve.wait_ge(y_done, NT * h + t + 1)
                dve.wait_ge(inv_done, h + 1)
                wait(dve, y_added, NT * (h - 1) + t + 1)
                dve.scalar_tensor_tensor(out=sh.x_nat[:, t, :], in0=y_ps[:, :], scalar=row_inv[:, t:t + 1],
                                         in1=sh.x_nat[:, t, :], op0=ALU.mult, op1=ALU.add).then_inc(y_added, 1)

            def pick_bias(g):
                wait(dve, taken, NG * g)
                dve.tensor_scalar(bias_now[:, :, :], bias_sb[:, :, ds(g, 1)], 1.0, None,
                                  ALU.mult).then_inc(bias_picked, 1)

            def step(h, b, attention, rest, project, more):
                if project:
                    pick_bias(h + 1)
                for s in range(NT):
                    if rest and s == 0:
                        invert_sums(h - 1, 1 - b)
                    if project and 1 <= s <= 4:
                        means(h + 1, s - 1)
                    if project and s >= NG:
                        v_low(h + 1, 1 - b, s - NG)
                    if project and 3 <= s <= 4:
                        split_q(h + 1, 1 - b, s - 3)
                    if rest and s == 5:
                        out_lo(h - 1, 1)
                    if attention and s == 7:
                        out_lo(h, 0)
                    if rest and s == 6:
                        add_output(h - 1, OUTPUT_TILES[s][0])
                    if attention:
                        maxima(h, b, s)
                    if rest and s == 0:
                        prob_lo(h - 1, NT - 1)
                    if attention and s:
                        prob_lo(h, s - 1)
                    if project and 1 <= s <= 2:
                        scale_k(h + 1, s - 1)
                    if rest and OUTPUT_TILES[s]:
                        add_output(h - 1, OUTPUT_TILES[s][-1])

            steps(dve, step)
            dve.wait_ge(y_added, NT * HEADS)
            for t in range(NT):
                ln.vector_stats(dve, t)
            ln.vector(dve)


def l1_mlp(nc, sh, w, z, s, down_w, down_z, down_s, out):
    FB = w.shape[0]
    GATE, UP, DOWN = range(3)
    with ExitStack() as ctx:
        def sb(name, shape, dt=F32):
            return ctx.enter_context(nc.sbuf_tensor(f"m_{name}", shape, dt))

        def bank(name):
            return ctx.enter_context(nc.psum_tensor(f"m_{name}", [P, HALF], F32))

        def sem(name):
            return ctx.enter_context(nc.semaphore(f"m_{name}"))

        raw_w = [[sb(f"raw_w{b}{i}", [P, D], I32) for i in range(3)] for b in range(2)]
        raw_z = [[sb(f"raw_z{b}{i}", [P, D], I32) for i in range(3)] for b in range(2)]
        raw_s = [[sb(f"raw_s{b}{i}", [P, D]) for i in range(3)] for b in range(2)]
        deq = [sb(f"deq{i}", [P, D]) for i in range(3)]
        w_hi = [[sb(f"w_hi{b}{i}", [P, D], F32R) for i in range(3)] for b in range(2)]
        w_lo = [[sb(f"w_lo{b}{i}", [P, D], F32R) for i in range(3)] for b in range(2)]
        sig = [sb(f"sig{i}", [P, HALF]) for i in range(2)]
        act_f = [sb(f"act_f{i}", [P, HALF]) for i in range(2)]
        a_hi = [sb(f"a_hi{b}", [P, TOK], F32R) for b in range(2)]
        a_lo = [sb(f"a_lo{b}", [P, TOK], F32R) for b in range(2)]

        g_ps = [bank(f"g_ps{i}") for i in range(2)]
        u_ps = [bank(f"u_ps{i}") for i in range(2)]
        y_ps = [bank(f"y_ps{i}") for i in range(2)]

        raw_in = [[sem(f"raw_in{b}{i}") for i in range(3)] for b in range(2)]
        subbed, scaled, dq_hi, dq_lo = sem("subbed"), sem("scaled"), sem("dq_hi"), sem("dq_lo")
        prod = sem("prod")
        sig_done, silu_done, act_done = sem("sig_done"), sem("silu_done"), sem("act_done")
        a_hi_done, a_lo_done = sem("a_hi_done"), sem("a_lo_done")
        y_done, y_added = sem("y_done"), sem("y_added")
        stored = sem("stored")
        ln = LayerNorm(nc, ctx, "m_ln", sh, None, transpose=False)

        def steps(eng, step):
            for j in (0, 1):
                step(j, j, True, j >= 1, True)
            with eng.Fori(2, FB - 3, 2) as j:
                step(j, 0, True, True, True)
                step(j + 1, 1, True, True, True)
            for j in (FB - 2, FB - 1, FB):
                step(j, j % 2, j < FB, True, j + 1 < FB)

        block = ctx.enter_context(nc.Block())

        @block.sync
        def _(sp):
            def load(j, b):
                for i in range(3):
                    wait(sp, scaled, 3 * (j - 2) + i + 1)
                    if i == DOWN:
                        parts = (down_w[ds(j, 1)].rearrange("a p d -> (a p) d"), down_z[ds(j, 1), :],
                                 down_s[ds(j, 1), :])
                    else:
                        parts = (w[ds(j, 1), i].rearrange("a p k f -> (a p) (k f)"),
                                 z[ds(j, 1), i].rearrange("a k f -> a (k f)"),
                                 s[ds(j, 1), i].rearrange("a k f -> a (k f)"))
                    sp.dma_start(raw_w[b][i][:, :], parts[0]).then_inc(raw_in[b][i], 16)
                    sp.dma_start(raw_z[b][i][:, :], parts[1].partition_broadcast(P)).then_inc(raw_in[b][i], 16)
                    sp.dma_start(raw_s[b][i][:, :], parts[2].partition_broadcast(P)).then_inc(raw_in[b][i], 16)

            load(0, 0)
            load(1, 1)
            with sp.Fori(2, FB - 1, 2) as j:
                load(j, 0)
                load(j + 1, 1)
            for t in range(NT):
                sp.wait_ge(ln.normed, t + 1)
                sp.dma_start(out[t * P:(t + 1) * P, :], sh.x_nat[:, t, :]).then_inc(stored, 16)
            sp.wait_ge(stored, 16 * NT)

        @block.gpsimd
        def _(pool):
            def dequantise(j, b, i):
                pool.wait_ge(subbed, 3 * j + i + 1)
                pool.tensor_tensor(deq[i][:, :], deq[i][:, :], raw_s[b][i][:, :], ALU.mult).then_inc(scaled, 1)
                pool.wait_ge(dq_hi, 3 * j + i + 1)
                pool.wait_ge(scaled, 3 * j + i + 1)
                if i == DOWN:
                    wait(pool, y_done, NT * (j - 1))
                else:
                    wait(pool, prod, 4 * (j - 1))
                pool.tensor_tensor(w_lo[b][i][:, :], deq[i][:, :], f(w_hi[b][i][:, :]), ALU.subtract).then_inc(dq_lo, 1)

            def act_low(j, b, half):
                cut = slice(half * HALF, (half + 1) * HALF)
                pool.wait_ge(a_hi_done, 2 * j + half + 1)
                wait(pool, y_done, NT * (j - 1))
                pool.tensor_tensor(a_lo[b][:, cut], act_f[half][:, :], f(a_hi[b][:, cut]),
                                   ALU.subtract).then_inc(a_lo_done, 1)

            def step(j, b, products, output, prepare):
                for q in range(4):
                    if products and q == 2:
                        act_low(j, b, 0)
                    if prepare and q < 3:
                        dequantise(j + 1, 1 - b, q)
                if products:
                    act_low(j, b, 1)

            for i in range(3):
                dequantise(0, 0, i)
            steps(pool, step)

        @block.scalar
        def _(act):
            def weight_high(j, b, i):
                act.wait_ge(scaled, 3 * j + i + 1)
                if i == DOWN:
                    wait(act, y_done, NT * (j - 1))
                else:
                    wait(act, prod, 4 * (j - 1))
                act.activation(w_hi[b][i][:, :], deq[i][:, :], ACT.Copy).then_inc(dq_hi, 1)

            def sigmoid(j, half):
                act.wait_ge(prod, 4 * j + 2 * half + 1)
                wait(act, act_done, 2 * (j - 1) + half + 1)
                act.activation(sig[half][:, :], g_ps[half][:, :], ACT.Sigmoid).then_inc(sig_done, 1)

            def act_high(j, b, half):
                act.wait_ge(act_done, 2 * j + half + 1)
                wait(act, y_done, NT * (j - 1))
                act.activation(a_hi[b][:, half * HALF:(half + 1) * HALF], act_f[half][:, :],
                               ACT.Copy).then_inc(a_hi_done, 1)

            def step(j, b, products, output, prepare):
                for q in range(4):
                    if products and q % 2 == 0:
                        sigmoid(j, q // 2)
                    if products and q == 2:
                        act_high(j, b, 0)
                    if prepare and q < 3:
                        weight_high(j + 1, 1 - b, q)
                if products:
                    act_high(j, b, 1)

            for i in range(3):
                weight_high(0, 0, i)
            steps(act, step)
            ln.scalar(act)

        @block.tensor
        def _(pe):
            def product(j, b, q):
                half, kind = q // 2, q % 2
                pe.wait_ge(dq_lo, 3 * j + kind + 1)
                wait(pe, (silu_done, act_done)[kind], 2 * (j - 1) + half + 1)
                out_ps = (g_ps, u_ps)[kind][half]
                cut = slice(half * HALF, (half + 1) * HALF)
                for k in range(KB):
                    col = slice(k * P, (k + 1) * P)
                    last = three_pass(pe, out_ps[:, :], w_hi[b][kind][:, col], w_lo[b][kind][:, col],
                                      sh.xT_hi[:, k, cut], sh.xT_lo[:, k, cut], k == 0, k == KB - 1)
                last.then_inc(prod, 1)

            def output_tile(j, b, t):
                pe.wait_ge(a_lo_done, 2 * j + t // CH + 1)
                pe.wait_ge(dq_lo, 3 * j + 3)
                wait(pe, y_added, NT * j + max(t - 1, 0))
                cut = slice(t * P, (t + 1) * P)
                three_pass(pe, y_ps[t % 2][:, :], a_hi[b][:, cut], a_lo[b][:, cut], w_hi[b][DOWN][:, :],
                           w_lo[b][DOWN][:, :], True, True).then_inc(y_done, 1)

            def step(j, b, products, output, prepare):
                for q in range(4):
                    if products:
                        product(j, b, q)
                    if output:
                        output_tile(j - 1, 1 - b, 2 * q)
                        output_tile(j - 1, 1 - b, 2 * q + 1)

            steps(pe, step)

        @block.vector
        def _(dve):
            def subtract_zeros(j, b, i):
                dve.wait_ge(raw_in[b][i], 24 * j - 24 * b + 48)
                wait(dve, dq_lo, 3 * (j - 1) + i + 1)
                dve.tensor_tensor(deq[i][:, :], raw_w[b][i][:, :], raw_z[b][i][:, :], ALU.subtract).then_inc(subbed, 1)

            def activate(j, half):
                dve.wait_ge(sig_done, 2 * j + half + 1)
                dve.tensor_tensor(sig[half][:, :], sig[half][:, :], g_ps[half][:, :], ALU.mult).then_inc(silu_done, 1)
                dve.wait_ge(silu_done, 2 * j + half + 1)
                dve.wait_ge(prod, 4 * j + 2 * half + 2)
                wait(dve, a_lo_done, 2 * (j - 1) + half + 1)
                dve.tensor_tensor(act_f[half][:, :], sig[half][:, :], u_ps[half][:, :], ALU.mult).then_inc(act_done, 1)

            def add_output(j, t):
                dve.wait_ge(y_done, NT * j + t + 1)
                wait(dve, y_added, NT * (j - 1) + t + 1)
                dve.tensor_tensor(sh.x_nat[:, t, :], sh.x_nat[:, t, :], y_ps[t % 2][:, :], ALU.add).then_inc(y_added, 1)

            def step(j, b, products, output, prepare):
                for q in range(4):
                    if prepare and q < 3:
                        subtract_zeros(j + 1, 1 - b, q)
                    if products and q % 2:
                        activate(j, q // 2)
                    if output:
                        add_output(j - 1, 2 * q)
                        add_output(j - 1, 2 * q + 1)

            for i in range(3):
                subtract_zeros(0, 0, i)
            steps(dve, step)
            dve.wait_ge(y_added, NT * FB)
            for t in range(NT):
                ln.vector_stats(dve, t)
            ln.vector(dve)


def transformer(nc, a, out, stages=4):
    with ExitStack() as ctx:
        sh = Shared(nc, ctx)
        l0_attention(nc, sh, a["x"], a["xT"], a["w0"], a["ow0"], a["norm_w"], a["decay"])
        if stages >= 2:
            l0_experts(nc, sh, a["router"], a["lora_a"], a["lora_b"])
        if stages >= 3:
            l1_attention(nc, sh, a["w1"], a["ow1"], a["bias1"], a["bo"], a["gains"])
        if stages >= 4:
            l1_mlp(nc, sh, a["mlp_w"], a["mlp_z"], a["mlp_s"], a["down_w"], a["down_z"], a["down_s"], out)


def layouts(i):
    def blocks(w):
        return w.reshape(KB, P, -1).transpose(1, 0, 2)

    x = i["L0_attn_hidden_states"].reshape(TOK, D)
    qkv = i["L0_attn_qkv_w"].reshape(HEADS, 3, HD, KB, P)
    gate = i["L0_attn_gate_w"].reshape(HEADS, 1, HD, KB, P)
    w0 = np.concatenate([qkv, gate], 1).transpose(0, 1, 4, 3, 2)
    w1 = np.stack([i[f"L1_attn_W{n}"].reshape(KB, P, HEADS, HD) for n in "kqv"], 0).transpose(3, 0, 2, 1, 4)
    FB = i["L1_ffn_gate_w"].shape[1] // P
    def cut(w):
        return w.reshape(w.shape[0], FB, P).transpose(1, 0, 2)
    a = {
        "x": x, "xT": x.T, "w0": w0, "ow0": i["L0_attn_out_w"].T.reshape(HEADS, HD, D),
        "norm_w": i["L0_attn_norm_w"].reshape(HEADS, HD).T, "decay": decay_tables(),
        "router": blocks(i["L0_ffn_gate_w"].T),
        "lora_a": blocks(i["L0_ffn_lora_A"].reshape(-1, D).T),
        "lora_b": blocks(i["L0_ffn_lora_B"].transpose(0, 2, 1).reshape(-1, D)),
        "w1": w1, "ow1": i["L1_attn_Wo"].reshape(HEADS, HD, D),
        "bias1": np.stack([i[f"L1_attn_b{n}"].reshape(HEADS, HD).T for n in "kqv"], 1),
        "bo": i["L1_attn_bo"].reshape(1, D), "gains": np.stack([i["L1_attn_gq"], i["L1_attn_gk"]], 1),
        "mlp_w": np.stack([cut(i[f"L1_ffn_{n}_w"]).reshape(FB, KB, P, P).transpose(0, 2, 1, 3)
                           for n in ("gate", "up")], 1),
        "mlp_z": np.stack([cut(i[f"L1_ffn_{n}_z"]) for n in ("gate", "up")], 1),
        "mlp_s": np.stack([cut(i[f"L1_ffn_{n}_s"]) for n in ("gate", "up")], 1),
        "down_w": i["L1_ffn_down_w"].reshape(FB, P, D), "down_z": i["L1_ffn_down_z"], "down_s": i["L1_ffn_down_s"],
    }
    return {k: np.ascontiguousarray(v) for k, v in a.items()}


def kernel(**inputs):
    import concourse.bacc as bacc
    from concourse.bass_utils import run_bass_kernel_spmd

    arrays = layouts({k: np.asarray(v) for k, v in inputs.items()})
    nc = bacc.Bacc("TRN2", target_bir_lowering=False, num_devices=1)
    aps = {k: nc.dram_tensor(f"in_{k}", v.shape, mybir.dt.from_np(v.dtype), kind="ExternalInput").ap()
           for k, v in arrays.items()}
    out = nc.dram_tensor("out", (TOK, D), F32, kind="ExternalOutput").ap()
    transformer(nc, aps, out)
    r = run_bass_kernel_spmd(nc, [{f"in_{k}": v for k, v in arrays.items()}], core_ids=[0])
    return r.results[0]["out"].reshape(1, TOK, D)
```

```python
from contextlib import ExitStack

import numpy as np

import concourse.bass as bass
from concourse import mybir

F32 = mybir.dt.float32
F32R = mybir.dt.float32r
I32 = mybir.dt.int32
U32 = mybir.dt.uint32
ACT = mybir.ActivationFunctionType
ALU = mybir.AluOpType
AX_X = mybir.AxisListType.X
ds = bass.ds

P = 128
TOK = 1024
NT = TOK // P
D = 512
KB = D // P
HALF = 512
HEADS = 32
HD = 128
LN_EPS = 1e-5

CHUNK = P
CH = HALF // CHUNK
L0_EPS = 1e-5


def decay_tables():
    factor = 1.0 - 1 / (HEADS - 1 + 1e-05) + 1e-05
    slope = (1.0 / 2.0 ** (8.0 / HEADS)) ** (np.arange(HEADS) + 1.0) * factor
    r = np.arange(CHUNK, dtype=np.float64)
    diff = r[None, None, :] - r[None, :, None]
    mask = np.where(diff >= 0, np.exp(-slope[:, None, None] * np.maximum(diff, 0)), 0.0)
    q_decay = np.broadcast_to(np.exp(-slope[:, None] * (r + 1)[None, :])[:, None], (HEADS, P, CHUNK))
    k_decay = np.exp(-(CHUNK - 1 - r)[None, :, None] * slope[:, None, None])
    chunk_decay = np.broadcast_to(np.exp(-slope * CHUNK)[:, None, None], (HEADS, P, 1))
    return np.concatenate([mask, q_decay, k_decay, chunk_decay], 2).astype(np.float32)


def wait(eng, sem, value):
    if isinstance(value, int) and value <= 0:
        return
    eng.wait_ge(sem, value)


def f(ap):
    return ap.bitcast(F32)


def three_pass(pe, out, w_hi, w_lo, x_hi, x_lo, first, last):
    pe.matmul(out, w_hi, x_hi, start=first, stop=False)
    pe.matmul(out, w_hi, x_lo, start=False, stop=False)
    return pe.matmul(out, w_lo, x_hi, start=False, stop=last)


class Shared:

    def __init__(self, nc, ctx):
        def sb(name, shape, dt=F32):
            return ctx.enter_context(nc.sbuf_tensor(name, shape, dt))

        self.x_nat = sb("x_nat", [P, NT, D])
        self.xT_hi = sb("xT_hi", [P, KB, TOK], F32R)
        self.xT_lo = sb("xT_lo", [P, KB, TOK], F32R)
        self.ident = sb("ident", [P, P])
        self.stats = sb("ln_stats", [P, NT, 6])
        self.mv = sb("ln_mv", [P, NT, 2])
        self.var = sb("ln_var", [P, NT])
        self.rstd = sb("ln_rstd", [P, NT])
        self.power = sb("power", [P, NT])


class LayerNorm:

    def __init__(self, nc, ctx, name, sh):
        def sem(s):
            return ctx.enter_context(nc.semaphore(f"{name}_{s}"))

        self.sh = sh
        self.chain = sem("dve_chain")
        self.chained = 0
        self.var_ready = sem("var_ready")
        self.root = sem("root_ready")
        self.normed = sem("normed")
        self.tr = sem("transposed")
        self.hi = sem("hi_ready")
        self.lo = sem("lo_ready")

    def link(self, dve, ins):
        self.chained += 1
        ins.then_inc(self.chain, 1)
        dve.wait_ge(self.chain, self.chained)

    def vector_stats(self, dve, t):
        sh = self.sh
        self.link(dve, dve.bn_stats(sh.stats[:, t, :], sh.x_nat[:, t, :]))
        self.link(dve, dve.bn_aggr(sh.mv[:, t, :], sh.stats[:, t, :]))
        if (t + 1) % CH == 0:
            half = slice(t + 1 - CH, t + 1)
            dve.tensor_scalar(sh.var[:, half], sh.mv[:, half, 1], LN_EPS, None, ALU.add).then_inc(self.var_ready, 1)

    def pool_root(self, pool):
        sh = self.sh
        for j in range(2):
            half = slice(j * CH, (j + 1) * CH)
            pool.wait_ge(self.var_ready, j + 1)
            pool.tensor_tensor(sh.rstd[:, half], sh.var[:, half], sh.power[:, half], ALU.pow).then_inc(self.root, 1)

    def vector_norm(self, dve, t):
        sh = self.sh
        dve.wait_ge(self.root, t // CH + 1)
        dve.tensor_scalar(sh.x_nat[:, t, :], sh.x_nat[:, t, :], sh.mv[:, t, 0:1], sh.rstd[:, t:t + 1],
                          ALU.subtract, ALU.mult).then_inc(self.normed, 1)

    def tensor_transpose(self, pe, banks, t):
        sh = self.sh
        pe.wait_ge(self.normed, t + 1)
        if t >= len(banks):
            pe.wait_ge(self.lo, t + 1 - len(banks))
        for k in range(KB):
            last = pe.transpose(banks[t % len(banks)][:, k * P:(k + 1) * P],
                                sh.x_nat[:, t, k * P:(k + 1) * P], sh.ident[:, :])
        last.then_inc(self.tr, 1)

    def scalar_high(self, act, banks, t):
        act.wait_ge(self.tr, t + 1)
        act.activation(self.sh.xT_hi[:, :, t * P:(t + 1) * P],
                       banks[t % len(banks)].rearrange("p (k n) -> p k n", k=KB), ACT.Copy).then_inc(self.hi, 1)

    def vector_low(self, dve, banks, t):
        cut = slice(t * P, (t + 1) * P)
        dve.wait_ge(self.tr, t + 1)
        dve.wait_ge(self.hi, t + 1)
        dve.tensor_tensor(self.sh.xT_lo[:, :, cut], banks[t % len(banks)].rearrange("p (k n) -> p k n", k=KB),
                          f(self.sh.xT_hi[:, :, cut]), ALU.subtract).then_inc(self.lo, 1)

    def vector(self, dve, banks):
        for t in range(NT + 1):
            if t < NT:
                self.vector_norm(dve, t)
            if t:
                self.vector_low(dve, banks, t - 1)


def l0_attention(nc, sh, ln, ew, aw, x, xT, w, ow, norm_w, decay_in, expert_weights):
    NG = 8
    GATE = 3
    with ExitStack() as ctx:
        def sb(name, shape, dt=F32):
            return ctx.enter_context(nc.sbuf_tensor(f"a_{name}", shape, dt))

        def bank(name, shape):
            return ctx.enter_context(nc.psum_tensor(f"a_{name}", shape, F32))

        def sem(name):
            return ctx.enter_context(nc.semaphore(f"a_{name}"))

        w_raw = aw.raw + [sb(f"w_raw{t}", [P, KB, HD]) for t in (2, 3)]
        w_hi = aw.hi + [sb(f"w_hi{t}", [P, KB, HD], F32R) for t in (2, 3)]
        w_lo = aw.lo + [sb(f"w_lo{t}", [P, KB, HD], F32R) for t in (2, 3)]
        ow_raw = sb("ow_raw", [P, D])
        ow_hi = [sb(f"ow_hi{b}", [P, D], F32R) for b in range(2)]
        ow_lo = [sb(f"ow_lo{b}", [P, D], F32R) for b in range(2)]
        qkvg = [[sb(f"qkvg{t}_{b}", [P, TOK]) for b in range(2)] for t in range(4)]
        sig_tmp = [sb(f"sig{i}", [P, HALF]) for i in range(2)]
        q_dec = sb("q_dec", [P, TOK])
        k_nat = sb("k_nat", [P, NT, HD])
        v_nat = sb("v_nat", [P, NT, HD])
        s_masked = sb("s_masked", [P, TOK])
        state = sb("state", [P, NT, HD])
        gated = sb("gated", [P, TOK])
        ga_hi = [sb(f"ga_hi{b}", [P, TOK], F32R) for b in range(2)]
        ga_lo = [sb(f"ga_lo{b}", [P, TOK], F32R) for b in range(2)]
        squares = sb("squares", [P, TOK])
        sq_sum = sb("sq_sum", [P, TOK])
        acc = sb("acc", [P, NT, D])
        decay = [sb(f"decay{b}", [P, 2 * CHUNK + 2]) for b in range(2)]
        mask = [d[:, 0:CHUNK].unsqueeze(1) for d in decay]
        q_decay = [d[:, CHUNK:2 * CHUNK].unsqueeze(1) for d in decay]
        k_decay = [d[:, 2 * CHUNK:2 * CHUNK + 1] for d in decay]
        chunk_decay = [d[:, 2 * CHUNK + 1:2 * CHUNK + 2] for d in decay]
        norm_sb = sb("norm_sb", [P, HEADS])
        ones = sb("ones", [P, 1])
        ms = sb("ms", [P, NT])
        rms = sb("rms", [P, NT])

        pj = [bank(f"pj{i}", [P, HALF]) for i in range(2)]
        tk = bank("tk", [P, HALF])
        tv = bank("tv", [P, HALF])
        s_ps = bank("s_ps", [P, HALF])
        u_ps = bank("u_ps", [P, HALF])
        o_ps = bank("o_ps", [P, HALF])
        y_ps = bank("y_ps", [P, HALF])

        w_in = [sem(f"w_in{t}") for t in range(4)]
        ow_in = sem("ow_in")
        decay_in_sem = [sem(f"decay_in{b}") for b in range(2)]
        w_hi_done, w_lo_done = sem("w_hi_done"), sem("w_lo_done")
        ow_hi_done, ow_lo_done = sem("ow_hi_done"), sem("ow_lo_done")
        proj = sem("proj")
        sig = sem("sig")
        silu = sem("silu")
        kv_tr = sem("kv_tr")
        kv_nat = sem("kv_nat")
        scored, masked = sem("scored"), sem("masked")
        q_decayed = sem("q_decayed")
        upd, state_done = sem("upd"), sem("state_done")
        attn = sem("attn")
        squared, sq_added = sem("squared"), sem("sq_added")
        gated_done, ga_hi_done, ga_lo_done = sem("gated_done"), sem("ga_hi_done"), sem("ga_lo_done")
        y_done, y_added = sem("y_done"), sem("y_added")
        x_in = [[sem(f"x_in{j}{k}") for k in range(KB)] for j in range(2)]
        const_in = sem("const_in")
        x_hi_done, x_split = sem("x_hi_done"), sem("x_split")
        zeroed = sem("zeroed")
        ms_done, ms_ready, rms_ready = sem("ms_done"), sem("ms_ready"), sem("rms_ready")
        x_nat_in, normalised, added = sem("x_nat_in"), sem("normalised"), sem("added")
        xT_raw = [gated, squares, sq_sum, q_dec]

        def y_bank(h, t):
            return pj[0] if isinstance(h, int) and h == HEADS - 1 and t % 2 else y_ps

        def steps(eng, step):
            def one(h):
                step(h, h % 2, 0 <= h < HEADS, h + 1 < HEADS, h >= 1, h + 2 < HEADS)
            for h in (-1, 0, 1):
                one(h)
            with eng.Fori(2, HEADS - 3, 2) as h:
                step(h, 0, True, True, True, True)
                step(h + 1, 1, True, True, True, True)
            for h in (HEADS - 2, HEADS - 1, HEADS):
                one(h)

        block = ctx.enter_context(nc.Block())

        @block.sync
        def _(sp):
            def load_weights(h, t):
                wait(sp, w_lo_done, 4 * (h - 1) + t + 1)
                sp.dma_start(w_raw[t][:, :, :], w[ds(h, 1), t].rearrange("a p k d -> (a p) k d")).then_inc(w_in[t], 16)

            for j in range(2):
                for k in (0, 1):
                    cut = slice(j * HALF, (j + 1) * HALF)
                    sp.dma_start(xT_raw[k][:, cut], xT[k * P:(k + 1) * P, cut]).then_inc(x_in[j][k], 16)
                if j == 0:
                    load_weights(0, 0)

            def load_output_weights(h):
                wait(sp, ow_lo_done, h)
                sp.dma_start(ow_raw[:, :], ow[ds(h, 1)].rearrange("a p d -> (a p) d")).then_inc(ow_in, 16)

            def load_decays(h, b):
                wait(sp, attn, 2 * (h - 1))
                sp.dma_start(decay[b][:, :], decay_in[ds(h, 1)].rearrange("a p n -> (a p) n")).then_inc(
                    decay_in_sem[b], 16)

            def load(h, b):
                load_weights(h, 0)
                load_weights(h, 1)
                load_output_weights(h - 2)
                load_weights(h, 2)
                load_weights(h, 3)
                load_decays(h - 1, 1 - b)

            for h in range(2):
                for t in range(4):
                    if h or t:
                        load_weights(h, t)
            load_decays(0, 0)
            sp.dma_start(sh.x_nat[:, :, :], x.rearrange("(t p) d -> p t d", p=P)).then_inc(x_nat_in, 16)
            with sp.Fori(2, HEADS - 1, 2) as h:
                load(h, 0)
                load(h + 1, 1)
            load_output_weights(HEADS - 2)
            load_decays(HEADS - 1, 1)
            load_output_weights(HEADS - 1)
            ew.load(sp, 0, expert_weights[0])
            for t in range(4):
                wait(sp, w_lo_done, 4 * HEADS + t - 3)
                sp.dma_start(w_raw[t][:, :, :], expert_weights[1][:, :, t * HD:(t + 1) * HD]).then_inc(w_in[t], 16)

        @block.gpsimd
        def _(pool):
            pool.dma_start(norm_sb[:, :], norm_w).then_inc(const_in, 16)
            pool.memset(sh.ident[:, :], 0.0).then_inc(zeroed, 1)
            pool.wait_ge(zeroed, 1)
            pool.affine_select(out=sh.ident[:, :], in_=sh.ident[:, :], compare_op=ALU.not_equal, fill=1.0, base=0,
                               pattern=[[-1, P]], channel_multiplier=1).then_inc(zeroed, 1)
            pool.memset(ones[:, :], 1.0).then_inc(zeroed, 1)
            pool.memset(sh.power[:, :], -0.5).then_inc(zeroed, 1)
            pool.memset(acc[:, :, :], 0.0).then_inc(zeroed, 1)

            def split_lo(h, t):
                pool.wait_ge(w_in[t], 16 * (h + 1))
                pool.wait_ge(w_hi_done, 4 * h + t + 1)
                wait(pool, proj, NG * (h - 1) + 2 * t + 2)
                pool.tensor_tensor(w_lo[t][:, :, :], w_raw[t][:, :, :], f(w_hi[t][:, :, :]),
                                   ALU.subtract).then_inc(w_lo_done, 1)

            for t in range(4):
                split_lo(0, t)
            pool.wait_ge(x_split, 2 * KB)
            pool.memset(sq_sum[:, :], 0.0).then_inc(zeroed, 1)
            pool.wait_ge(zeroed, 6)

            def half_out(h, b, j):
                cut = slice(j * HALF, (j + 1) * HALF)
                pool.wait_ge(squared, 2 * h + j + 1)
                wait(pool, sq_added, 2 * (h - 1) + j + 1)
                pool.tensor_tensor(sq_sum[:, cut], sq_sum[:, cut], squares[:, cut], ALU.add).then_inc(sq_added, 1)
                pool.wait_ge(ga_hi_done, 2 * h + j + 1)
                pool.wait_ge(gated_done, 2 * h + j + 1)
                wait(pool, y_done, NT * (h - 1))
                pool.tensor_tensor(ga_lo[b][:, cut], gated[:, cut], f(ga_hi[b][:, cut]),
                                   ALU.subtract).then_inc(ga_lo_done, 1)

            def step(h, b, attention, project, output, split):
                for s in range(NG):
                    if attention and s == 3:
                        pool.wait_ge(ow_in, 16 * (h + 1))
                        pool.wait_ge(ow_hi_done, h + 1)
                        wait(pool, y_done, NT * (h - 1))
                        pool.tensor_tensor(ow_lo[b][:, :], ow_raw[:, :], f(ow_hi[b][:, :]),
                                           ALU.subtract).then_inc(ow_lo_done, 1)
                    if attention and s == 6:
                        half_out(h, b, 0)
                    if split and s % 2:
                        split_lo(h + 2, s // 2)
                if attention:
                    half_out(h, b, 1)
                if isinstance(h, int) and h == HEADS - 2:
                    ew.split_low(pool, 0)
                    for t in range(4):
                        pool.wait_ge(w_in[t], 16 * (HEADS + 1))
                        pool.wait_ge(ew.w_hi, 2 + t)
                        pool.tensor_tensor(ew.lo[1][:, :, t * HD:(t + 1) * HD], w_raw[t][:, :, :],
                                           f(ew.hi[1][:, :, t * HD:(t + 1) * HD]), ALU.subtract).then_inc(ew.w_lo, 1)

            steps(pool, step)
            pool.wait_ge(ms_ready, 1)
            pool.tensor_tensor(rms[:, :], ms[:, :], sh.power[:, :], ALU.pow).then_inc(rms_ready, 1)
            pool.wait_ge(x_nat_in, 16)
            for t in range(NT):
                pool.wait_ge(normalised, t + 1)
                pool.tensor_tensor(sh.x_nat[:, t, :], sh.x_nat[:, t, :], acc[:, t, :], ALU.add).then_inc(added, 1)
            ln.pool_root(pool)

        @block.scalar
        def _(act):
            def split_hi(h, t):
                act.wait_ge(w_in[t], 16 * (h + 1))
                wait(act, proj, NG * (h - 1) + 2 * t + 2)
                act.activation(w_hi[t][:, :, :], w_raw[t][:, :, :], ACT.Copy).then_inc(w_hi_done, 1)

            for j in range(2):
                for k in (2, 3):
                    cut = slice(j * HALF, (j + 1) * HALF)
                    act.dma_start(xT_raw[k][:, cut], xT[k * P:(k + 1) * P, cut]).then_inc(x_in[j][k], 16)
            for j in range(2):
                for k in range(KB):
                    cut = slice(j * HALF, (j + 1) * HALF)
                    act.wait_ge(x_in[j][k], 16)
                    act.activation(sh.xT_hi[:, k, cut], xT_raw[k][:, cut], ACT.Copy).then_inc(x_hi_done, 1)
                    if k >= 2:
                        split_hi(0, 2 * j + k - 2)

            def to_nat(h, b, j):
                wait(act, attn, 2 * h)
                act.wait_ge(kv_tr, 4 * h + 2 * j + 1)
                act.wait_ge(decay_in_sem[b], 8 * h + 16 - 8 * b)
                act.activation(k_nat[:, CH * j:CH * (j + 1), :], tk[:, :].rearrange("p (c d) -> p c d", c=CH),
                               ACT.Copy, scale=k_decay[b]).then_inc(kv_nat, 1)
                act.wait_ge(kv_tr, 4 * h + 2 * j + 2)
                act.activation(v_nat[:, CH * j:CH * (j + 1), :], tv[:, :].rearrange("p (c d) -> p c d", c=CH),
                               ACT.Copy).then_inc(kv_nat, 1)

            def square(h, j):
                cut = slice(j * HALF, (j + 1) * HALF)
                act.wait_ge(attn, 2 * h + j + 1)
                wait(act, sq_added, 2 * (h - 1) + j + 1)
                act.activation(squares[:, cut], o_ps[:, :], ACT.Square).then_inc(squared, 1)

            def gated_hi(h, b, j):
                cut = slice(j * HALF, (j + 1) * HALF)
                act.wait_ge(gated_done, 2 * h + j + 1)
                wait(act, y_done, NT * (h - 1))
                act.activation(ga_hi[b][:, cut], gated[:, cut], ACT.Copy).then_inc(ga_hi_done, 1)

            def sigmoid(g, bg, s):
                act.wait_ge(proj, NG * g + s + 1)
                half = s % 2
                if s // 2 == GATE:
                    wait(act, gated_done, 2 * (g - 1))
                    out = qkvg[GATE][bg][:, half * HALF:(half + 1) * HALF]
                else:
                    wait(act, silu, 6 * g + s - 1 if s >= 2 else 6 * (g - 1) + 5 + s)
                    out = sig_tmp[half][:, :]
                act.activation(out, pj[half][:, :], ACT.Sigmoid).then_inc(sig, 1)

            def step(h, b, attention, project, output, split):
                for s in range(NG):
                    if attention:
                        if s in (0, 2):
                            to_nat(h, b, s // 2)
                        if s == 3:
                            act.wait_ge(ow_in, 16 * (h + 1))
                            wait(act, y_done, NT * (h - 1))
                            act.activation(ow_hi[b][:, :], ow_raw[:, :], ACT.Copy).then_inc(ow_hi_done, 1)
                        if s in (5, 7):
                            square(h, s // 6)
                        if s == 6:
                            gated_hi(h, b, 0)
                    if project:
                        sigmoid(h + 1, 1 - b, s)
                    if split and s % 2:
                        split_hi(h + 2, s // 2)
                if attention:
                    gated_hi(h, b, 1)
                if isinstance(h, int) and h == HEADS - 2:
                    ew.split_high(act, 0)
                    for t in range(4):
                        act.wait_ge(w_in[t], 16 * (HEADS + 1))
                        act.activation(ew.hi[1][:, :, t * HD:(t + 1) * HD], w_raw[t][:, :, :],
                                       ACT.Copy).then_inc(ew.w_hi, 1)

            steps(act, step)
            act.wait_ge(rms_ready, 1)
            for t in range(NT):
                act.wait_ge(y_added, NT * (HEADS - 1) + t + 1)
                act.activation(acc[:, t, :], acc[:, t, :], ACT.Copy, scale=rms[:, t:t + 1]).then_inc(normalised, 1)

        @block.tensor
        def _(pe):
            def project_group(g, s):
                t, half = s // 2, s % 2
                cut = slice(half * HALF, (half + 1) * HALF)
                pe.wait_ge(w_lo_done, 4 * g + t + 1)
                if isinstance(g, int) and g == 0 and t == 0:
                    pe.wait_ge(x_split, KB * (half + 1))
                if s >= 2:
                    pe.wait_ge(silu, 6 * g + s - 1)
                else:
                    wait(pe, sig, NG * (g - 1) + 7 + s)
                for k in range(KB):
                    last = three_pass(pe, pj[half][:, :], w_hi[t][:, k, :], w_lo[t][:, k, :],
                                      sh.xT_hi[:, k, cut], sh.xT_lo[:, k, cut], k == 0, k == KB - 1)
                last.then_inc(proj, 1)

            def transposes(h, b, j):
                pe.wait_ge(silu, 6 * h + 5 + j)
                wait(pe, kv_nat, 4 * h + 2 * j)
                for t, out in ((1, tk), (2, tv)):
                    for c in range(CH):
                        at = (j * CH + c) * CHUNK
                        last = pe.transpose(out[:, c * CHUNK:(c + 1) * CHUNK], qkvg[t][b][:, at:at + CHUNK],
                                            sh.ident[:, :])
                    last.then_inc(kv_tr, 1)

            def scores(h, b, j):
                wait(pe, masked, 2 * h + j)
                for c in range(CH):
                    at = (j * CH + c) * CHUNK
                    last = pe.matmul(s_ps[:, c * CHUNK:(c + 1) * CHUNK], qkvg[1][b][:, at:at + CHUNK],
                                     qkvg[0][b][:, at:at + CHUNK], start=True, stop=True)
                last.then_inc(scored, 1)

            def updates(h, j):
                pe.wait_ge(kv_nat, 4 * h + 2 * j + 2)
                wait(pe, state_done, 7 * h + CH * j)
                for c in range(j * CH, min((j + 1) * CH, NT - 1)):
                    last = pe.matmul(u_ps[:, (c % CH) * HD:(c % CH + 1) * HD], k_nat[:, c, :], v_nat[:, c, :],
                                     start=True, stop=True)
                last.then_inc(upd, 1)

            def outputs(h, j):
                pe.wait_ge(masked, 2 * h + j + 1)
                pe.wait_ge(q_decayed, h + 1)
                wait(pe, squared, 2 * h + j)
                wait(pe, gated_done, 2 * h + j)
                for c in range(j * CH, (j + 1) * CH):
                    out = o_ps[:, (c % CH) * CHUNK:(c % CH + 1) * CHUNK]
                    at = c * CHUNK
                    last = pe.matmul(out, v_nat[:, c, :], s_masked[:, at:at + CHUNK], start=True, stop=(c == 0))
                    if c:
                        if c == j * CH or c == 1:
                            pe.wait_ge(state_done, 7 * h + (3 if j == 0 else 7))
                        last = pe.matmul(out, state[:, c, :], q_dec[:, at:at + CHUNK], start=False, stop=True)
                last.then_inc(attn, 1)

            def output_tile(h, b, t):
                pe.wait_ge(ga_lo_done, 2 * h + t // CH + 1)
                pe.wait_ge(ow_lo_done, h + 1)
                wait(pe, y_added, NT * h + (t - 1 if t and y_bank(h, 1) is not y_ps else t))
                cut = slice(t * P, (t + 1) * P)
                three_pass(pe, y_bank(h, t)[:, :], ga_hi[b][:, cut], ga_lo[b][:, cut], ow_hi[b][:, :], ow_lo[b][:, :],
                           True, True).then_inc(y_done, 1)

            def step(h, b, attention, project, output, split):
                for s in range(NG):
                    if attention:
                        if isinstance(h, int) and h == 0 and s == 0:
                            pe.wait_ge(zeroed, 6)
                        if s in (0, 2):
                            transposes(h, b, s // 2)
                        if s in (1, 3):
                            scores(h, b, s // 2)
                        if s in (4, 5):
                            updates(h, s - 4)
                        if s in (5, 7):
                            outputs(h, s // 6)
                    if project:
                        project_group(h + 1, s)
                    if output:
                        output_tile(h - 1, 1 - b, s)
                    if isinstance(h, int) and h == HEADS and s == CH - 1:
                        mean_squares()

            def mean_squares():
                pe.wait_ge(sq_added, 2 * HEADS)
                for t in range(NT):
                    last = pe.matmul(s_ps[:, t:t + 1], sq_sum[:, t * P:(t + 1) * P], ones[:, :], start=True,
                                     stop=True)
                last.then_inc(ms_done, 1)

            steps(pe, step)

        @block.vector
        def _(dve):
            for j in range(2):
                for k in range(KB):
                    cut = slice(j * HALF, (j + 1) * HALF)
                    dve.wait_ge(x_hi_done, KB * j + k + 1)
                    dve.wait_ge(x_in[j][k], 16)
                    dve.tensor_tensor(sh.xT_lo[:, k, cut], xT_raw[k][:, cut], f(sh.xT_hi[:, k, cut]),
                                      ALU.subtract).then_inc(x_split, 1)
            dve.wait_ge(x_split, 2 * KB)
            dve.wait_ge(const_in, 16)
            dve.wait_ge(zeroed, 6)

            def decay_q(h, b):
                dve.wait_ge(silu, 6 * h + 2)
                dve.wait_ge(decay_in_sem[b], 8 * h + 16 - 8 * b)
                wait(dve, attn, 2 * h)
                dve.tensor_tensor(q_dec[:, :].rearrange("p (c n) -> p c n", n=CHUNK),
                                  qkvg[0][b][:, :].rearrange("p (c n) -> p c n", n=CHUNK),
                                  q_decay[b].broadcast_to([P, NT, CHUNK]), ALU.mult).then_inc(q_decayed, 1)

            def mask_scores(h, b, j):
                dve.wait_ge(scored, 2 * h + j + 1)
                wait(dve, attn, 2 * (h - 1) + j + 1)
                dve.tensor_tensor(s_masked[:, j * HALF:(j + 1) * HALF].rearrange("p (c n) -> p c n", n=CHUNK),
                                  s_ps[:, :].rearrange("p (c n) -> p c n", n=CHUNK),
                                  mask[b].broadcast_to([P, CH, CHUNK]), ALU.mult).then_inc(masked, 1)

            def states(h, b, j):
                dve.wait_ge(upd, 2 * h + j + 1)
                wait(dve, attn, 2 * h)
                for c in range(j * CH, min((j + 1) * CH, NT - 1)):
                    u = u_ps[:, (c % CH) * HD:(c % CH + 1) * HD]
                    if c == 0:
                        ins = dve.tensor_copy(state[:, 1, :], u)
                    else:
                        dve.wait_ge(state_done, 7 * h + c)
                        ins = dve.scalar_tensor_tensor(out=state[:, c + 1, :], in0=state[:, c, :],
                                                       scalar=chunk_decay[b], in1=u,
                                                       op0=ALU.mult, op1=ALU.add)
                    ins.then_inc(state_done, 1)

            def gate_out(h, b, j):
                cut = slice(j * HALF, (j + 1) * HALF)
                dve.wait_ge(squared, 2 * h + j + 1)
                dve.wait_ge(sig, NG * h + 7 + j)
                wait(dve, ga_lo_done, 2 * (h - 1) + j + 1)
                dve.scalar_tensor_tensor(out=gated[:, cut], in0=o_ps[:, :], scalar=norm_sb[:, ds(h, 1)],
                                         in1=qkvg[GATE][b][:, cut], op0=ALU.mult, op1=ALU.mult).then_inc(gated_done, 1)

            def silu_half(g, bg, s):
                dve.wait_ge(sig, NG * g + s + 1)
                wait(dve, attn, 2 * (g - 1))
                half = s % 2
                dve.tensor_tensor(qkvg[s // 2][bg][:, half * HALF:(half + 1) * HALF], pj[half][:, :],
                                  sig_tmp[half][:, :], ALU.mult).then_inc(silu, 1)

            def add_output(h, t):
                dve.wait_ge(y_done, NT * h + t + 1)
                wait(dve, y_added, NT * (h - 1) + t + 1)
                dve.tensor_tensor(acc[:, t, :], acc[:, t, :], y_bank(h, t)[:, :], ALU.add).then_inc(y_added, 1)

            def step(h, b, attention, project, output, split):
                for s in range(NG):
                    if attention:
                        if s == 0:
                            decay_q(h, b)
                        if s in (1, 3):
                            mask_scores(h, b, s // 2)
                        if s in (4, 5):
                            states(h, b, s - 4)
                        if s in (5, 7):
                            gate_out(h, b, s // 6)
                    if project and s // 2 < GATE:
                        silu_half(h + 1, 1 - b, s)
                    if output:
                        add_output(h - 1, s)
                    if isinstance(h, int) and h == HEADS and s == CH - 1:
                        dve.wait_ge(ms_done, 1)
                        dve.tensor_scalar(ms[:, :], s_ps[:, 0:NT], 1.0 / (HEADS * HD), L0_EPS, ALU.mult,
                                          ALU.add).then_inc(ms_ready, 1)

            steps(dve, step)
            for t in range(NT):
                dve.wait_ge(added, t + 1)
                ln.vector_stats(dve, t)


EXPERTS = 8
RANK = 64


WIDTHS = (EXPERTS, EXPERTS * RANK, D)


class ExpertWeights:

    def __init__(self, nc, ctx):
        def sb(name, n, dt=F32R):
            return ctx.enter_context(nc.sbuf_tensor(f"e_{name}", [P, KB, n], dt))

        def sem(name):
            return ctx.enter_context(nc.semaphore(f"e_{name}"))

        self.raw = {0: sb("raw0", EXPERTS, F32)}
        self.hi = [sb(f"hi{i}", n) for i, n in enumerate(WIDTHS[:2])]
        self.lo = [sb(f"lo{i}", n) for i, n in enumerate(WIDTHS[:2])]
        self.w_in = {0: sem("w_in0"), 2: sem("w_in2")}
        self.w_hi, self.w_lo = sem("w_hi"), sem("w_lo")

    def load(self, sp, i, w):
        sp.dma_start(self.raw[i][:, :, :], w).then_inc(self.w_in[i], 16)

    def split_high(self, act, i):
        act.wait_ge(self.w_in[i], 16)
        act.activation(self.hi[i][:, :, :], self.raw[i][:, :, :], ACT.Copy).then_inc(self.w_hi, 1)

    def split_low(self, pool, i):
        pool.wait_ge(self.w_in[i], 16)
        pool.wait_ge(self.w_hi, 6 if i else 1)
        pool.tensor_tensor(self.lo[i][:, :, :], self.raw[i][:, :, :], f(self.hi[i][:, :, :]),
                           ALU.subtract).then_inc(self.w_lo, 1)


def l0_experts(nc, sh, ln_in, ln, ew, lora_b, aw, next_weights):
    with ExitStack() as ctx:
        def sb(name, shape, dt=F32):
            return ctx.enter_context(nc.sbuf_tensor(f"e_{name}", shape, dt))

        def bank(name):
            return ctx.enter_context(nc.psum_tensor(f"e_{name}", [P, HALF], F32))

        def sem(name):
            return ctx.enter_context(nc.semaphore(f"e_{name}"))

        hi, lo = ew.hi, ew.lo
        hi.append(sb("hi2", [P, KB, D], F32R))
        lo.append(sb("lo2", [P, KB, D], F32R))
        ew.raw[2] = sb("raw2", [P, KB, D])
        logits = sb("logits", [P, NT, EXPERTS])
        prob = sb("prob", [P, NT, EXPERTS])
        top = [sb(f"top{n}", [P, NT, 1]) for n in range(2)]
        chosen = [sb(f"chosen{n}", [P, NT, EXPERTS]) for n in range(2)]
        place = sb("place", [P, NT, EXPERTS])
        first = sb("first", [P, NT, 1])
        weight = sb("weight", [P, NT, EXPERTS])
        total = sb("total", [P, NT, 1])
        order_i = sb("order_i", [P, EXPERTS], I32)
        order = sb("order", [P, 1, EXPERTS])
        h_sb = sb("h_sb", [P, NT, EXPERTS * RANK])
        scaled = [sb(f"scaled{i}", [P, EXPERTS * RANK]) for i in range(2)]
        hT_hi = [sb(f"hT_hi{i}", [P, KB, P], F32R) for i in range(2)]
        hT_lo = [sb(f"hT_lo{i}", [P, KB, P], F32R) for i in range(2)]

        lg = bank("lg")
        h_ps = [bank(f"h_ps{i}") for i in range(2)]
        t_ps = [bank(f"t_ps{i}") for i in range(2)]
        y_ps = [bank(f"y_ps{i}") for i in range(2)]
        ln_banks = [t[:, :] for t in t_ps]

        order_ready = sem("order_ready")
        logits_ready, shifted, exp_ready = sem("logits_ready"), sem("shifted"), sem("exp_ready")
        h_ready, h_copied, h_scaled = sem("h_ready"), sem("h_copied"), sem("h_scaled")
        hT_ready, hT_hi_ready, hT_lo_ready = sem("hT_ready"), sem("hT_hi_ready"), sem("hT_lo_ready")
        y_ready, y_added = sem("y_ready"), sem("y_added")

        block = ctx.enter_context(nc.Block())

        @block.sync
        def _(sp):
            ew.load(sp, 2, lora_b)
            for kind in range(2):
                aw.load(sp, next_weights, 0, 0, kind)

        @block.gpsimd
        def _(pool):
            pool.iota(order_i[:, :], pattern=[[-1, EXPERTS]], base=EXPERTS,
                      channel_multiplier=0).then_inc(order_ready, 1)
            ew.split_low(pool, 2)
            for kind in range(2):
                aw.split_low(pool, 0, 0, kind)
            ln.pool_root(pool)

        @block.scalar
        def _(act):
            def copy_h(t):
                act.wait_ge(h_ready, t + 1)
                act.activation(h_sb[:, t, :], h_ps[t % 2][:, :], ACT.Copy).then_inc(h_copied, 1)

            for t in range(NT):
                ln_in.scalar_high(act, ln_banks, t)
                if t % 2 == 0 and t >= 2:
                    copy_h(t // 2 - 1)
            ew.split_high(act, 2)
            copy_h(3)
            act.wait_ge(shifted, 1)
            act.activation(prob[:, :, :], logits[:, :, :], ACT.Exp).then_inc(exp_ready, 1)
            for t in range(4, NT):
                copy_h(t)
            for kind in range(2):
                aw.split_high(act, 0, 0, kind)
            for t in range(NT):
                act.wait_ge(hT_ready, t + 1)
                if t >= 2:
                    act.wait_ge(y_ready, t - 1)
                act.activation(hT_hi[t % 2][:, :, :], t_ps[t % 2][:, :].rearrange("p (k n) -> p k n", k=KB),
                               ACT.Copy).then_inc(hT_hi_ready, 1)

        @block.tensor
        def _(pe):
            def product(out, lhs_hi, lhs_lo, i):
                for k in range(KB):
                    last = three_pass(pe, out, lhs_hi(k), lhs_lo(k), hi[i][:, k, :], lo[i][:, k, :],
                                      k == 0, k == KB - 1)
                return last

            def x_part(part, t):
                return lambda k: part[:, k, t * P:(t + 1) * P]

            def route(t):
                pe.wait_ge(ln_in.lo, t + 1)
                last = product(lg[:, t * EXPERTS:(t + 1) * EXPERTS], x_part(sh.xT_hi, t), x_part(sh.xT_lo, t), 0)
                if t == NT - 1:
                    last.then_inc(logits_ready, 1)

            def down(t):
                if t >= 2:
                    pe.wait_ge(h_copied, t - 1)
                product(h_ps[t % 2][:, :], x_part(sh.xT_hi, t), x_part(sh.xT_lo, t), 1).then_inc(h_ready, 1)

            for t in range(NT):
                ln_in.tensor_transpose(pe, ln_banks, t)
                if t:
                    route(t - 1)
                if t % 2 == 0 and t >= 2:
                    down(t // 2 - 1)
            route(NT - 1)
            for t in range(3, NT):
                down(t)
            for i in range(NT + 1):
                if i < NT:
                    pe.wait_ge(h_scaled, i + 1)
                    if i >= 2:
                        pe.wait_ge(hT_lo_ready, i - 1)
                    for k in range(KB):
                        last = pe.transpose(t_ps[i % 2][:, k * P:(k + 1) * P], scaled[i % 2][:, k * P:(k + 1) * P],
                                            sh.ident[:, :])
                    last.then_inc(hT_ready, 1)
                if i >= 1:
                    t = i - 1
                    pe.wait_ge(ew.w_lo, 6)
                    pe.wait_ge(hT_lo_ready, t + 1)
                    if t >= 2:
                        pe.wait_ge(y_added, t - 1)
                    product(y_ps[t % 2][:, :], lambda k: hT_hi[t % 2][:, k, :], lambda k: hT_lo[t % 2][:, k, :],
                            2).then_inc(y_ready, 1)

        @block.vector
        def _(dve):
            link = ln.link
            wide = [P, NT, EXPERTS]
            ln_in.vector(dve, ln_banks)
            dve.wait_ge(order_ready, 1)
            link(dve, dve.tensor_copy(order[:, 0, :], order_i[:, :]))
            dve.wait_ge(logits_ready, 1)
            lg_t = lg[:, 0:NT * EXPERTS].rearrange("p (t e) -> p t e", e=EXPERTS)
            link(dve, dve.tensor_reduce(total[:, :, :], lg_t, AX_X, ALU.max))
            dve.tensor_tensor(logits[:, :, :], lg_t, total[:, :, :].broadcast_to(wide),
                              ALU.subtract).then_inc(shifted, 1)
            dve.wait_ge(exp_ready, 1)
            link(dve, dve.tensor_reduce(total[:, :, :], prob[:, :, :], AX_X, ALU.add))
            link(dve, dve.reciprocal(total[:, :, :], total[:, :, :]))
            link(dve, dve.tensor_tensor(prob[:, :, :], prob[:, :, :], total[:, :, :].broadcast_to(wide), ALU.mult))
            for n in range(2):
                link(dve, dve.tensor_reduce(top[n][:, :, :], prob[:, :, :], AX_X, ALU.max))
                link(dve, dve.tensor_tensor(place[:, :, :], prob[:, :, :], top[n][:, :, :].broadcast_to(wide),
                                            ALU.is_equal))
                link(dve, dve.tensor_tensor(place[:, :, :], place[:, :, :], order[:, :, :].broadcast_to(wide),
                                            ALU.mult))
                link(dve, dve.tensor_reduce(first[:, :, :], place[:, :, :], AX_X, ALU.max))
                link(dve, dve.tensor_tensor(chosen[n][:, :, :], place[:, :, :], first[:, :, :].broadcast_to(wide),
                                            ALU.is_equal))
                if n == 0:
                    link(dve, dve.scalar_tensor_tensor(out=prob[:, :, :], in0=chosen[0][:, :, :], scalar=-2.0,
                                                       in1=prob[:, :, :], op0=ALU.mult, op1=ALU.add))
            link(dve, dve.tensor_tensor(total[:, :, :], top[0][:, :, :], top[1][:, :, :], ALU.add))
            link(dve, dve.reciprocal(total[:, :, :], total[:, :, :]))
            for n in range(2):
                link(dve, dve.tensor_tensor(top[n][:, :, :], top[n][:, :, :], total[:, :, :], ALU.mult))
                link(dve, dve.tensor_tensor(chosen[n][:, :, :], chosen[n][:, :, :],
                                            top[n][:, :, :].broadcast_to(wide), ALU.mult))
            link(dve, dve.tensor_tensor(weight[:, :, :], chosen[0][:, :, :], chosen[1][:, :, :], ALU.add))

            for i in range(NT + 2):
                if i < NT:
                    dve.wait_ge(h_copied, i + 1)
                    if i >= 2:
                        dve.wait_ge(hT_ready, i - 1)
                    dve.tensor_tensor(scaled[i % 2][:, :].rearrange("p (e r) -> p e r", e=EXPERTS),
                                      h_sb[:, i, :].rearrange("p (e r) -> p e r", e=EXPERTS),
                                      weight[:, i, :].unsqueeze(2).broadcast_to([P, EXPERTS, RANK]),
                                      ALU.mult).then_inc(h_scaled, 1)
                if 1 <= i <= NT:
                    t = i - 1
                    dve.wait_ge(hT_hi_ready, t + 1)
                    if t >= 2:
                        dve.wait_ge(y_ready, t - 1)
                    dve.tensor_tensor(hT_lo[t % 2][:, :, :], t_ps[t % 2][:, :].rearrange("p (k n) -> p k n", k=KB),
                                      f(hT_hi[t % 2][:, :, :]), ALU.subtract).then_inc(hT_lo_ready, 1)
                if i >= 2:
                    t = i - 2
                    dve.wait_ge(y_ready, t + 1)
                    dve.tensor_tensor(sh.x_nat[:, t, :], sh.x_nat[:, t, :], y_ps[t % 2][:, :],
                                      ALU.add).then_inc(y_added, 1)
                    dve.wait_ge(y_added, t + 1)
                    ln.vector_stats(dve, t)


L1_EPS = 1e-6


K, Q, V = range(3)


class AttentionWeights:

    def __init__(self, nc, ctx):
        def sb(name, i, dt=F32):
            return ctx.enter_context(nc.sbuf_tensor(f"b_{name}{i}", [P, KB, HD], dt))

        def sem(name):
            return ctx.enter_context(nc.semaphore(f"b_{name}"))

        self.raw = [sb("w_raw", i) for i in range(2)]
        self.hi = [sb("w_hi", i, F32R) for i in range(2)]
        self.lo = [sb("w_lo", i, F32R) for i in range(2)]
        self.w_in = [sem(f"w_in{i}") for i in range(2)]
        self.hi_done, self.lo_done = sem("w_hi_done"), sem("w_lo_done")
        self.proj = sem("proj")

    def loads(self, h, b, kind):
        return 8 * (3 * h + kind) + (8 if (b + kind) % 2 else 16)

    def load(self, sp, w, h, b, kind):
        slot = (b + kind) % 2
        wait(sp, self.lo_done, 3 * h + kind - 1)
        sp.dma_start(self.raw[slot][:, :, :], w[ds(h, 1), kind].rearrange("a p k d -> (a p) k d")).then_inc(
            self.w_in[slot], 16)

    def split_high(self, act, h, b, kind):
        slot = (b + kind) % 2
        act.wait_ge(self.w_in[slot], self.loads(h, b, kind))
        wait(act, self.proj, 2 * (3 * h + kind - 1))
        act.activation(self.hi[slot][:, :, :], self.raw[slot][:, :, :], ACT.Copy).then_inc(self.hi_done, 1)

    def split_low(self, pool, h, b, kind):
        slot = (b + kind) % 2
        pool.wait_ge(self.w_in[slot], self.loads(h, b, kind))
        pool.wait_ge(self.hi_done, 3 * h + kind + 1)
        wait(pool, self.proj, 2 * (3 * h + kind - 1))
        pool.tensor_tensor(self.lo[slot][:, :, :], self.raw[slot][:, :, :], f(self.hi[slot][:, :, :]),
                           ALU.subtract).then_inc(self.lo_done, 1)


def l1_attention(nc, sh, ln_in, ln, aw, mlp, w, ow, bias, bo, gains):
    NG = 6
    with ExitStack() as ctx:
        def sb(name, shape, dt=F32):
            return ctx.enter_context(nc.sbuf_tensor(f"b_{name}", shape, dt))

        def bank(name, shape):
            return ctx.enter_context(nc.psum_tensor(f"b_{name}", shape, F32))

        def sem(name):
            return ctx.enter_context(nc.semaphore(f"b_{name}"))

        w_hi, w_lo = aw.hi, aw.lo
        ow_raw = sb("ow_raw", [P, D])
        ow_hi = [sb(f"ow_hi{b}", [P, D], F32R) for b in range(2)]
        ow_lo = [sb(f"ow_lo{b}", [P, D], F32R) for b in range(2)]
        k_hi = [sb(f"k_hi{b}", [P, TOK], F32R) for b in range(2)]
        k_lo = [sb(f"k_lo{b}", [P, TOK], F32R) for b in range(2)]
        q_hi = [sb(f"q_hi{b}", [P, TOK], F32R) for b in range(2)]
        q_lo = [sb(f"q_lo{b}", [P, TOK], F32R) for b in range(2)]
        v_hi = [sb(f"v_hi{b}", [P, NT, HD], F32R) for b in range(2)]
        v_lo = [sb(f"v_lo{b}", [P, NT, HD], F32R) for b in range(2)]
        q_rstd = [sb(f"q_rstd{b}", [P, NT]) for b in range(2)]
        lin = [sb(f"lin{i}", [P, HALF]) for i in range(2)]
        sq = sb("sq", [P, HALF])
        sq_sum = sb("sq_sum", [P, CH])
        mean_sq = sb("mean_sq", [P, CH])
        k_rstd = sb("k_rstd", [P, CH])
        prob = [sb(f"prob{i}", [P, TOK]) for i in range(2)]
        row_max = sb("row_max", [P, NT])
        shift = sb("shift", [P, NT])
        row_sum = [sb(f"row_sum{b}", [P, NT]) for b in range(2)]
        row_inv = sb("row_inv", [P, NT])
        pT_hi = [mlp.pT0[0], sb("pT_hi1", [P, NT, HALF], F32R)]
        pT_lo = [mlp.pT0[1], sb("pT_lo1", [P, NT, HALF], F32R)]
        o_hi = sb("o_hi", [P, TOK], F32R)
        o_lo = sb("o_lo", [P, TOK], F32R)
        bias_sb = sb("bias_sb", [P, 3, HEADS])
        bias_now = sb("bias_now", [P, 3, 1])
        gain_in = sb("gain_in", [P, 2])
        gain = sb("gain", [P, 1])
        bo_sb = sb("bo_sb", [P, D])

        s_ps = bank("s_ps", [P, TOK])
        t_ps = bank("t_ps", [P, TOK])
        pj = bank("pj", [P, HALF])
        m_ps = bank("m_ps", [P, HALF])
        o_ps = bank("o_ps", [P, HALF])
        y_ps = bank("y_ps", [P, HALF])

        w_lo_done, proj = aw.lo_done, aw.proj
        ow_in, ow_hi_done, ow_lo_done = sem("ow_in"), sem("ow_hi_done"), sem("ow_lo_done")
        taken = sem("taken")
        sq_tr = sem("sq_tr")
        summed = sem("summed")
        mean_ready = sem("mean_ready")
        rstd_ready = sem("rstd_ready")
        spread = sem("spread")
        k_scaled, k_hi_done, k_lo_done = sem("k_scaled"), sem("k_hi_done"), sem("k_lo_done")
        q_hi_done, q_lo_done = sem("q_hi_done"), sem("q_lo_done")
        v_tr, v_hi_done, v_lo_done = sem("v_tr"), sem("v_hi_done"), sem("v_lo_done")
        scored, max_done, shift_done, exp_done = sem("scored"), sem("max_done"), sem("shift_done"), sem("exp_done")
        inv_done = sem("inv_done")
        p_tr, pT_hi_done, pT_lo_done = sem("p_tr"), sem("pT_hi_done"), sem("pT_lo_done")
        pv, o_hi_done, o_lo_done = sem("pv"), sem("o_hi_done"), sem("o_lo_done")
        y_done, y_added = sem("y_done"), sem("y_added")
        bias_picked = sem("bias_picked")
        const_in, bias_added, gain_ready = sem("const_in"), sem("bias_added"), sem("gain_ready")
        ln_banks = [s_ps[:, 0:HALF], s_ps[:, HALF:], t_ps[:, 0:HALF], t_ps[:, HALF:]]

        def steps(eng, step):
            def one(h):
                step(h, h % 2, 0 <= h < HEADS, h >= 1, h + 1 < HEADS, h + 2 < HEADS)
            for h in (-1, 0, 1):
                one(h)
            with eng.Fori(2, HEADS - 3, 2) as h:
                step(h, 0, True, True, True, True)
                step(h + 1, 1, True, True, True, True)
            for h in (HEADS - 2, HEADS - 1, HEADS):
                one(h)

        OUTPUT_TILES = [[0], [1], [2], [3], [], [4], [5, 6], [7]]
        VALUES = [None, (-1, 1, (0, 1)), (-1, 1, (1, 2)), (-1, 1, (2, 4)), (-1, 1, (4, 6)), (-1, 1, (6, 8)),
                  (0, 0, (0, 4)), (0, 0, (4, 8))]
        SPLITS = {2: (V, 1), 4: (K, 2), 6: (Q, 2)}

        def to_split(s, project, more):
            if s not in SPLITS:
                return None
            kind, ahead = SPLITS[s]
            return (kind, ahead) if (project if ahead == 1 else more) else None

        def y_bank(h, t):
            return pj if isinstance(h, int) and h == HEADS - 1 and t % 2 else y_ps

        block = ctx.enter_context(nc.Block())

        @block.sync
        def _(sp):
            sp.dma_start(bias_sb[:, :, :], bias).then_inc(const_in, 16)
            sp.dma_start(gain_in[:, :], gains).then_inc(const_in, 16)
            sp.dma_start(bo_sb[:, :], bo.partition_broadcast(P)).then_inc(const_in, 16)

            def load_output_weights(h):
                wait(sp, ow_lo_done, h)
                sp.dma_start(ow_raw[:, :], ow[ds(h, 1)].rearrange("a p d -> (a p) d")).then_inc(ow_in, 16)

            def load(h, b):
                aw.load(sp, w, h, b, K)
                aw.load(sp, w, h, b, Q)
                load_output_weights(h - 2)
                aw.load(sp, w, h, b, V)

            aw.load(sp, w, 0, 0, V)
            for kind in (K, Q, V):
                aw.load(sp, w, 1, 1, kind)
            with sp.Fori(2, HEADS - 1, 2) as h:
                load(h, 0)
                load(h + 1, 1)
            load_output_weights(HEADS - 2)
            load_output_weights(HEADS - 1)
            sp.wait_ge(pv, 2 * HEADS - 1)
            mlp.load(sp, 0, 0)

        @block.gpsimd
        def _(pool):
            def inverse_rms(g, bg, s):
                pool.wait_ge(mean_ready, 4 * g + s + 1)
                if s < 2:
                    wait(pool, spread, 2 * g + s)
                    out = k_rstd[:, :]
                else:
                    wait(pool, exp_done, NT * (g - 1))
                    out = q_rstd[bg][:, (s - 2) * CH:(s - 1) * CH]
                pool.tensor_tensor(out, mean_sq[:, :], sh.power[:, 0:CH], ALU.pow).then_inc(rstd_ready, 1)

            def k_low(g, bg, j):
                cut = slice(j * HALF, (j + 1) * HALF)
                pool.wait_ge(k_hi_done, 2 * g + j + 1)
                wait(pool, scored, NT * (g - 1))
                pool.tensor_tensor(k_lo[bg][:, cut], lin[j][:, :], f(k_hi[bg][:, cut]),
                                   ALU.subtract).then_inc(k_lo_done, 1)

            def step(h, b, attention, rest, project, more):
                for s in range(NT):
                    if attention and s == 4:
                        pool.wait_ge(ow_in, 16 * (h + 1))
                        pool.wait_ge(ow_hi_done, h + 1)
                        wait(pool, y_done, NT * (h - 1))
                        pool.tensor_tensor(ow_lo[b][:, :], ow_raw[:, :], f(ow_hi[b][:, :]),
                                           ALU.subtract).then_inc(ow_lo_done, 1)
                    if project and 1 <= s <= 4:
                        inverse_rms(h + 1, 1 - b, s - 1)
                    if project and 1 <= s <= 2:
                        k_low(h + 1, 1 - b, s - 1)
                    split = to_split(s, project, more)
                    if split:
                        kind, ahead = split
                        aw.split_low(pool, h + ahead, (b + ahead) % 2, kind)

            steps(pool, step)
            ln.pool_root(pool)

        @block.scalar
        def _(act):
            for t in range(NT):
                ln_in.scalar_high(act, ln_banks, t)

            def out_hi(h, j):
                act.wait_ge(pv, 2 * h + j + 1)
                wait(act, y_done, NT * (h - 1) + CH * (j + 1))
                act.activation(o_hi[:, j * HALF:(j + 1) * HALF], o_ps[:, :], ACT.Copy).then_inc(o_hi_done, 1)

            def prob_hi(h, t):
                j, at = t // CH, (t % CH) * P
                act.wait_ge(p_tr, NT * h + t + 1)
                wait(act, pv, 2 * (h - 1) + j + 1)
                act.activation(pT_hi[j][:, :, at:at + P], t_ps[:, :].rearrange("p (m n) -> p m n", m=NT),
                               ACT.Copy).then_inc(pT_hi_done, 1)

            def exponent(h, b, t):
                act.wait_ge(shift_done, NT * h + t + 1)
                wait(act, p_tr, NT * h + t - 1)
                act.activation(prob[t % 2][:, :], s_ps[:, :], ACT.Exp, bias=shift[:, t:t + 1],
                               scale=q_rstd[b][:, t:t + 1], accum_out=row_sum[b][:, t:t + 1]).then_inc(exp_done, 1)

            def take(g, bg, s):
                act.wait_ge(proj, NG * g + s + 1)
                if s < 2:
                    wait(act, v_tr, 2 * (g - 1) + s + 1)
                elif s < 4:
                    act.wait_ge(k_lo_done, 2 * g + s - 1)
                else:
                    act.wait_ge(q_lo_done, 2 * g + s - 3)
                b_ap = bias_now[:, s // 2, :]
                act.wait_ge(bias_picked, g + 1)
                ins = act.activation(lin[s % 2][:, :], pj[:, :], ACT.Identity, bias=b_ap)
                if s < 4:
                    wait(act, sq_tr, 4 * g + s)
                    ins = act.activation(sq[:, :], pj[:, :], ACT.Square, bias=b_ap)
                ins.then_inc(taken, 1)

            def k_high(g, bg, j):
                act.wait_ge(k_scaled, 2 * g + j + 1)
                wait(act, scored, NT * (g - 1))
                act.activation(k_hi[bg][:, j * HALF:(j + 1) * HALF], lin[j][:, :], ACT.Copy).then_inc(k_hi_done, 1)

            def v_high(g, bg, j):
                act.wait_ge(v_tr, 2 * g + j + 1)
                wait(act, pv, 2 * (g - 1))
                act.activation(v_hi[bg][:, j * CH:(j + 1) * CH, :], pj[:, :].rearrange("p (c d) -> p c d", c=CH),
                               ACT.Copy).then_inc(v_hi_done, 1)

            def step(h, b, attention, rest, project, more):
                for s in range(NT):
                    if project and s >= NG:
                        v_high(h + 1, 1 - b, s - NG)
                    if project and s < NG:
                        take(h + 1, 1 - b, s)
                    if rest and s == 5:
                        out_hi(h - 1, 1)
                    if attention and s == 7:
                        out_hi(h, 0)
                    if rest and s == 0:
                        prob_hi(h - 1, NT - 1)
                    if attention and s:
                        prob_hi(h, s - 1)
                    if attention:
                        exponent(h, b, s)
                    if project and 1 <= s <= 2:
                        k_high(h + 1, 1 - b, s - 1)
                    if attention and s == 4:
                        act.wait_ge(ow_in, 16 * (h + 1))
                        wait(act, y_done, NT * (h - 1))
                        act.activation(ow_hi[b][:, :], ow_raw[:, :], ACT.Copy).then_inc(ow_hi_done, 1)
                    split = to_split(s, project, more)
                    if split:
                        kind, ahead = split
                        aw.split_high(act, h + ahead, (b + ahead) % 2, kind)

            steps(act, step)

        @block.tensor
        def _(pe):
            def transpose_squares(g, s):
                pe.wait_ge(taken, NG * g + s + 1)
                if s % 3 == 0:
                    wait(pe, summed, 4 * g + s)
                else:
                    pe.wait_ge(k_scaled, 2 * g + s)
                for c in range(CH):
                    last = pe.transpose(m_ps[:, c * P:(c + 1) * P], sq[:, c * P:(c + 1) * P], sh.ident[:, :])
                last.then_inc(sq_tr, 1)

            def spread_k(g, j):
                pe.wait_ge(rstd_ready, 4 * g + j + 1)
                for c in range(CH):
                    last = pe.matmul(m_ps[:, c * P:(c + 1) * P], k_rstd[:, c:c + 1].broadcast_to([P, P]),
                                     sh.ident[:, :], start=True, stop=True)
                last.then_inc(spread, 1)

            def values(h, b, j, blocks):
                if blocks[0] == 0:
                    pe.wait_ge(pT_lo_done, NT * h + CH * (j + 1))
                    pe.wait_ge(v_lo_done, 2 * h + 2)
                    wait(pe, o_lo_done, 2 * h + j)
                for m in range(*blocks):
                    last = three_pass(pe, o_ps[:, :], v_hi[b][:, m, :], v_lo[b][:, m, :], pT_hi[j][:, m, :],
                                      pT_lo[j][:, m, :], m == 0, m == NT - 1)
                if blocks[1] == NT:
                    last.then_inc(pv, 1)

            def scores(h, b, t):
                if t == 0:
                    pe.wait_ge(k_lo_done, 2 * h + 2)
                    pe.wait_ge(q_lo_done, 2 * h + 2)
                wait(pe, exp_done, NT * h + t)
                cut = slice(t * P, (t + 1) * P)
                for j in range(2):
                    keys = slice(j * HALF, (j + 1) * HALF)
                    last = three_pass(pe, s_ps[:, keys], q_hi[b][:, cut], q_lo[b][:, cut], k_hi[b][:, keys],
                                      k_lo[b][:, keys], True, True)
                last.then_inc(scored, 1)

            def transpose_probs(h, t):
                pe.wait_ge(exp_done, NT * h + t + 1)
                wait(pe, pT_lo_done, NT * h + t)
                for m in range(NT):
                    cut = slice(m * P, (m + 1) * P)
                    last = pe.transpose(t_ps[:, cut], prob[t % 2][:, cut], sh.ident[:, :])
                last.then_inc(p_tr, 1)

            def project_group(g, bg, s):
                kind, half = s // 2, s % 2
                slot = (bg + kind) % 2
                pe.wait_ge(w_lo_done, 3 * g + kind + 1)
                if s == 0:
                    wait(pe, v_lo_done, 2 * g)
                else:
                    pe.wait_ge(taken, NG * g + s)
                cut = slice(half * HALF, (half + 1) * HALF)
                for k in range(KB):
                    last = three_pass(pe, pj[:, :], w_hi[slot][:, k, :], w_lo[slot][:, k, :], sh.xT_hi[:, k, cut],
                                      sh.xT_lo[:, k, cut], k == 0, k == KB - 1)
                last.then_inc(proj, 1)

            def transpose_v(g, j):
                pe.wait_ge(taken, NG * (g + 1))
                if j:
                    pe.wait_ge(v_lo_done, 2 * g + 1)
                for c in range(CH):
                    last = pe.transpose(pj[:, c * P:(c + 1) * P], lin[j][:, c * P:(c + 1) * P], sh.ident[:, :])
                last.then_inc(v_tr, 1)

            def output_tile(h, b, t):
                pe.wait_ge(o_lo_done, 2 * h + t // CH + 1)
                pe.wait_ge(ow_lo_done, h + 1)
                wait(pe, y_added, NT * h + (t - 1 if t and y_bank(h, 1) is not y_ps else t))
                cut = slice(t * P, (t + 1) * P)
                three_pass(pe, y_bank(h, t)[:, :], o_hi[:, cut], o_lo[:, cut], ow_hi[b][:, :], ow_lo[b][:, :],
                           True, True).then_inc(y_done, 1)

            def step(h, b, attention, rest, project, more):
                for s in range(NT):
                    if isinstance(h, int) and h == -1 and s < 2:
                        for t in range(s * CH, (s + 1) * CH):
                            ln_in.tensor_transpose(pe, ln_banks, t)
                        pe.wait_ge(ln_in.lo, (s + 1) * CH)
                    if project and s < NG:
                        project_group(h + 1, 1 - b, s)
                    if project and 1 <= s <= 4:
                        transpose_squares(h + 1, s - 1)
                    if project and s >= NG:
                        transpose_v(h + 1, s - NG)
                    if VALUES[s]:
                        ahead, j, blocks = VALUES[s]
                        if (attention, rest)[-ahead]:
                            values(h + ahead, (b + ahead) % 2, j, blocks)
                    if rest and s == 0:
                        transpose_probs(h - 1, NT - 1)
                    if attention and s:
                        transpose_probs(h, s - 1)
                    if rest and s == 6:
                        output_tile(h - 1, 1 - b, OUTPUT_TILES[s][0])
                    if attention:
                        scores(h, b, s)
                    if project and 1 <= s <= 2:
                        spread_k(h + 1, s - 1)
                    if rest and OUTPUT_TILES[s]:
                        output_tile(h - 1, 1 - b, OUTPUT_TILES[s][-1])

            steps(pe, step)

        @block.vector
        def _(dve):
            ln_in.vector(dve, ln_banks)
            dve.wait_ge(const_in, 48)
            ln.link(dve, dve.tensor_tensor(gain[:, :], gain_in[:, 0:1], gain_in[:, 1:2], ALU.mult))
            dve.tensor_scalar(gain[:, :], gain[:, :], float(HD) ** -0.5, None, ALU.mult).then_inc(gain_ready, 1)
            dve.wait_ge(gain_ready, 1)

            def maxima(h, b, t):
                dve.wait_ge(scored, NT * h + t + 1)
                dve.tensor_reduce(row_max[:, t:t + 1], s_ps[:, :], AX_X, ALU.max).then_inc(max_done, 1)
                dve.wait_ge(max_done, NT * h + t + 1)
                if t == 0:
                    dve.wait_ge(rstd_ready, 4 * h + 4)
                dve.tensor_scalar(shift[:, t:t + 1], row_max[:, t:t + 1], q_rstd[b][:, t:t + 1], -1.0,
                                  ALU.mult, ALU.mult).then_inc(shift_done, 1)

            def prob_lo(h, t):
                j, at = t // CH, (t % CH) * P
                dve.wait_ge(pT_hi_done, NT * h + t + 1)
                dve.tensor_tensor(pT_lo[j][:, :, at:at + P], t_ps[:, :].rearrange("p (m n) -> p m n", m=NT),
                                  f(pT_hi[j][:, :, at:at + P]), ALU.subtract).then_inc(pT_lo_done, 1)

            def invert_sums(h, b):
                dve.wait_ge(exp_done, NT * h + NT)
                wait(dve, y_added, NT * h)
                dve.reciprocal(row_inv[:, :], row_sum[b][:, :]).then_inc(inv_done, 1)

            def means(g, s):
                dve.wait_ge(sq_tr, 4 * g + s + 1)
                dve.tensor_reduce(sq_sum[:, :], m_ps[:, :].rearrange("p (c n) -> p c n", c=CH), AX_X,
                                  ALU.add).then_inc(summed, 1)
                dve.wait_ge(summed, 4 * g + s + 1)
                wait(dve, rstd_ready, 4 * g + s)
                dve.tensor_scalar(mean_sq[:, :], sq_sum[:, :], 1.0 / HD, L1_EPS, ALU.mult,
                                  ALU.add).then_inc(mean_ready, 1)

            def scale_k(g, j):
                dve.wait_ge(spread, 2 * g + j + 1)
                dve.tensor_tensor(lin[j][:, :], lin[j][:, :], m_ps[:, :], ALU.mult).then_inc(k_scaled, 1)

            def split_q(g, bg, j):
                cut = slice(j * HALF, (j + 1) * HALF)
                dve.wait_ge(taken, NG * g + j + 3)
                wait(dve, scored, NT * (g - 1))
                dve.tensor_scalar(q_hi[bg][:, cut], lin[j][:, :], gain[:, 0:1], None, ALU.mult).then_inc(q_hi_done, 1)
                dve.wait_ge(q_hi_done, 2 * g + j + 1)
                dve.scalar_tensor_tensor(out=q_lo[bg][:, cut], in0=lin[j][:, :], scalar=gain[:, 0:1],
                                         in1=f(q_hi[bg][:, cut]), op0=ALU.mult, op1=ALU.subtract).then_inc(q_lo_done, 1)

            def v_low(g, bg, j):
                dve.wait_ge(v_hi_done, 2 * g + j + 1)
                dve.tensor_tensor(v_lo[bg][:, j * CH:(j + 1) * CH, :], pj[:, :].rearrange("p (c d) -> p c d", c=CH),
                                  f(v_hi[bg][:, j * CH:(j + 1) * CH, :]), ALU.subtract).then_inc(v_lo_done, 1)

            def out_lo(h, j):
                cut = slice(j * HALF, (j + 1) * HALF)
                dve.wait_ge(o_hi_done, 2 * h + j + 1)
                dve.tensor_tensor(o_lo[:, cut], o_ps[:, :], f(o_hi[:, cut]), ALU.subtract).then_inc(o_lo_done, 1)

            def add_output(h, t):
                dve.wait_ge(y_done, NT * h + t + 1)
                dve.wait_ge(inv_done, h + 1)
                if isinstance(h, int) and h == 0:
                    dve.wait_ge(bias_added, t + 1)
                wait(dve, y_added, NT * (h - 1) + t + 1)
                dve.scalar_tensor_tensor(out=sh.x_nat[:, t, :], in0=y_bank(h, t)[:, :], scalar=row_inv[:, t:t + 1],
                                         in1=sh.x_nat[:, t, :], op0=ALU.mult, op1=ALU.add).then_inc(y_added, 1)

            def pick_bias(g):
                wait(dve, taken, NG * g)
                dve.tensor_scalar(bias_now[:, :, :], bias_sb[:, :, ds(g, 1)], 1.0, None,
                                  ALU.mult).then_inc(bias_picked, 1)

            def step(h, b, attention, rest, project, more):
                if project:
                    pick_bias(h + 1)
                for s in range(NT):
                    if rest and s == 0:
                        invert_sums(h - 1, 1 - b)
                    if project and 1 <= s <= 4:
                        means(h + 1, s - 1)
                    if project and s >= NG:
                        v_low(h + 1, 1 - b, s - NG)
                    if isinstance(h, int) and h == -1:
                        dve.wait_ge(ln_in.tr, s + 1)
                        dve.tensor_tensor(sh.x_nat[:, s, :], sh.x_nat[:, s, :], bo_sb[:, :], ALU.add).then_inc(
                            bias_added, 1)
                    if project and 3 <= s <= 4:
                        split_q(h + 1, 1 - b, s - 3)
                    if rest and s == 5:
                        out_lo(h - 1, 1)
                    if attention and s == 7:
                        out_lo(h, 0)
                    if rest and s == 6:
                        add_output(h - 1, OUTPUT_TILES[s][0])
                    if attention:
                        maxima(h, b, s)
                    if rest and s == 0:
                        prob_lo(h - 1, NT - 1)
                    if attention and s:
                        prob_lo(h, s - 1)
                    if project and 1 <= s <= 2:
                        scale_k(h + 1, s - 1)
                    if rest and OUTPUT_TILES[s]:
                        add_output(h - 1, OUTPUT_TILES[s][-1])

            steps(dve, step)
            for t in range(NT):
                dve.wait_ge(y_added, NT * (HEADS - 1) + t + 1)
                ln.vector_stats(dve, t)


GATE, UP, DOWN = range(3)


class MlpWeights:

    def __init__(self, nc, ctx, w, z, s, down_w, down_z, down_s):
        with ExitStack() as earlier:
            self.pT0 = [earlier.enter_context(nc.sbuf_tensor(f"pT_{n}0", [P, NT, HALF], F32R)) for n in ("hi", "lo")]
        self.nc, self.ctx = nc, ctx
        self.raw_w, self.raw_z, self.raw_s = [], [], []
        self.place(0)
        ctx.enter_context(nc.sbuf_tensor("m_beside", [P, (2 * NT - 9) * HALF], F32))
        self.w, self.z, self.s = w, z, s
        self.down = (down_w, down_z, down_s)
        self.raw_in = [[ctx.enter_context(nc.semaphore(f"m_raw_in{b}{i}")) for i in range(3)]
                       for b in range(2)]
        self.scaled = ctx.enter_context(nc.semaphore("m_scaled"))

    def place(self, b):
        for name, dt, raw in (("raw_w", I32, self.raw_w), ("raw_z", I32, self.raw_z), ("raw_s", F32, self.raw_s)):
            raw.append([self.ctx.enter_context(self.nc.sbuf_tensor(f"m_{name}{b}{i}", [P, D], dt))[:, :]
                        for i in range(3)])

    def load(self, sp, j, b):
        for i in range(3):
            wait(sp, self.scaled, 3 * (j - 2) + i + 1)
            if i == DOWN:
                parts = [a[ds(j, 1), :] for a in self.down[1:]]
                parts = [self.down[0][ds(j, 1)].rearrange("a p d -> (a p) d")] + parts
            else:
                parts = (self.w[ds(j, 1), i].rearrange("a p k f -> (a p) (k f)"),
                         self.z[ds(j, 1), i].rearrange("a k f -> a (k f)"),
                         self.s[ds(j, 1), i].rearrange("a k f -> a (k f)"))
            sp.dma_start(self.raw_w[b][i], parts[0]).then_inc(self.raw_in[b][i], 16)
            sp.dma_start(self.raw_z[b][i], parts[1].partition_broadcast(P)).then_inc(self.raw_in[b][i], 16)
            sp.dma_start(self.raw_s[b][i], parts[2].partition_broadcast(P)).then_inc(self.raw_in[b][i], 16)


def l1_mlp(nc, sh, ln_in, ln, mlp, out):
    FB = mlp.w.shape[0]
    with ExitStack() as ctx:
        def sb(name, shape, dt=F32):
            return ctx.enter_context(nc.sbuf_tensor(f"m_{name}", shape, dt))

        def bank(name):
            return ctx.enter_context(nc.psum_tensor(f"m_{name}", [P, HALF], F32))

        def sem(name):
            return ctx.enter_context(nc.semaphore(f"m_{name}"))

        mlp.place(1)
        raw_w, raw_z, raw_s = mlp.raw_w, mlp.raw_z, mlp.raw_s
        deq = [sb(f"deq{i}", [P, D]) for i in range(3)]
        w_hi = [[sb(f"w_hi{b}{i}", [P, D], F32R) for i in range(3)] for b in range(2)]
        w_lo = [[sb(f"w_lo{b}{i}", [P, D], F32R) for i in range(3)] for b in range(2)]
        sig = [sb(f"sig{i}", [P, HALF]) for i in range(2)]
        act_f = [sb(f"act_f{i}", [P, HALF]) for i in range(2)]
        a_hi = [sb(f"a_hi{b}", [P, TOK], F32R) for b in range(2)]
        a_lo = [sb(f"a_lo{b}", [P, TOK], F32R) for b in range(2)]

        g_ps = [bank(f"g_ps{i}") for i in range(2)]
        u_ps = [bank(f"u_ps{i}") for i in range(2)]
        y_ps = [bank(f"y_ps{i}") for i in range(2)]

        raw_in, scaled = mlp.raw_in, mlp.scaled
        subbed, dq_hi, dq_lo = sem("subbed"), sem("dq_hi"), sem("dq_lo")
        prod = sem("prod")
        sig_done, silu_done, act_done = sem("sig_done"), sem("silu_done"), sem("act_done")
        a_hi_done, a_lo_done = sem("a_hi_done"), sem("a_lo_done")
        y_done, y_added = sem("y_done"), sem("y_added")
        stored = sem("stored")
        ln_banks = [b[:, :] for b in (*g_ps, *u_ps)]

        def steps(eng, step):
            for j in (0, 1):
                step(j, j, True, j >= 1, True)
            with eng.Fori(2, FB - 3, 2) as j:
                step(j, 0, True, True, True)
                step(j + 1, 1, True, True, True)
            for j in (FB - 2, FB - 1, FB):
                step(j, j % 2, j < FB, True, j + 1 < FB)

        block = ctx.enter_context(nc.Block())

        @block.sync
        def _(sp):
            mlp.load(sp, 1, 1)
            with sp.Fori(2, FB - 1, 2) as j:
                mlp.load(sp, j, 0)
                mlp.load(sp, j + 1, 1)
            for t in range(NT):
                sp.wait_ge(ln.normed, t + 1)
                sp.dma_start(out[t * P:(t + 1) * P, :], sh.x_nat[:, t, :]).then_inc(stored, 16)
            sp.wait_ge(stored, 16 * NT)

        @block.gpsimd
        def _(pool):
            def dequantise(j, b, i):
                pool.wait_ge(subbed, 3 * j + i + 1)
                pool.tensor_tensor(deq[i][:, :], deq[i][:, :], raw_s[b][i], ALU.mult).then_inc(scaled, 1)
                pool.wait_ge(dq_hi, 3 * j + i + 1)
                pool.wait_ge(scaled, 3 * j + i + 1)
                if i == DOWN:
                    wait(pool, y_done, NT * (j - 1))
                else:
                    wait(pool, prod, 4 * (j - 1))
                pool.tensor_tensor(w_lo[b][i][:, :], deq[i][:, :], f(w_hi[b][i][:, :]), ALU.subtract).then_inc(dq_lo, 1)

            def act_low(j, b, half):
                cut = slice(half * HALF, (half + 1) * HALF)
                pool.wait_ge(a_hi_done, 2 * j + half + 1)
                wait(pool, y_done, NT * (j - 1))
                pool.tensor_tensor(a_lo[b][:, cut], act_f[half][:, :], f(a_hi[b][:, cut]),
                                   ALU.subtract).then_inc(a_lo_done, 1)

            def step(j, b, products, output, prepare):
                for q in range(4):
                    if products and q == 2:
                        act_low(j, b, 0)
                    if prepare and q < 3:
                        dequantise(j + 1, 1 - b, q)
                if products:
                    act_low(j, b, 1)

            for i in range(3):
                dequantise(0, 0, i)
            steps(pool, step)
            ln.pool_root(pool)

        @block.scalar
        def _(act):
            def weight_high(j, b, i):
                act.wait_ge(scaled, 3 * j + i + 1)
                if i == DOWN:
                    wait(act, y_done, NT * (j - 1))
                else:
                    wait(act, prod, 4 * (j - 1))
                act.activation(w_hi[b][i][:, :], deq[i][:, :], ACT.Copy).then_inc(dq_hi, 1)

            def sigmoid(j, half):
                act.wait_ge(prod, 4 * j + 2 * half + 1)
                wait(act, act_done, 2 * (j - 1) + half + 1)
                act.activation(sig[half][:, :], g_ps[half][:, :], ACT.Sigmoid).then_inc(sig_done, 1)

            def act_high(j, b, half):
                act.wait_ge(act_done, 2 * j + half + 1)
                wait(act, y_done, NT * (j - 1))
                act.activation(a_hi[b][:, half * HALF:(half + 1) * HALF], act_f[half][:, :],
                               ACT.Copy).then_inc(a_hi_done, 1)

            def step(j, b, products, output, prepare):
                for q in range(4):
                    if products and q % 2 == 0:
                        sigmoid(j, q // 2)
                    if products and q == 2:
                        act_high(j, b, 0)
                    if prepare and q < 3:
                        weight_high(j + 1, 1 - b, q)
                if products:
                    act_high(j, b, 1)

            weight_high(0, 0, GATE)
            for t in range(NT):
                ln_in.scalar_high(act, ln_banks, t)
                if t == CH - 1:
                    weight_high(0, 0, UP)
            weight_high(0, 0, DOWN)
            steps(act, step)

        @block.tensor
        def _(pe):
            def product(j, b, q):
                half, kind = q // 2, q % 2
                pe.wait_ge(dq_lo, 3 * j + kind + 1)
                wait(pe, (silu_done, act_done)[kind], 2 * (j - 1) + half + 1)
                out_ps = (g_ps, u_ps)[kind][half]
                cut = slice(half * HALF, (half + 1) * HALF)
                for k in range(KB):
                    col = slice(k * P, (k + 1) * P)
                    last = three_pass(pe, out_ps[:, :], w_hi[b][kind][:, col], w_lo[b][kind][:, col],
                                      sh.xT_hi[:, k, cut], sh.xT_lo[:, k, cut], k == 0, k == KB - 1)
                last.then_inc(prod, 1)

            def output_tile(j, b, t):
                pe.wait_ge(a_lo_done, 2 * j + t // CH + 1)
                pe.wait_ge(dq_lo, 3 * j + 3)
                wait(pe, y_added, NT * j + max(t - 1, 0))
                cut = slice(t * P, (t + 1) * P)
                three_pass(pe, y_ps[t % 2][:, :], a_hi[b][:, cut], a_lo[b][:, cut], w_hi[b][DOWN][:, :],
                           w_lo[b][DOWN][:, :], True, True).then_inc(y_done, 1)

            def step(j, b, products, output, prepare):
                for q in range(4):
                    if products:
                        product(j, b, q)
                    if output:
                        output_tile(j - 1, 1 - b, 2 * q)
                        output_tile(j - 1, 1 - b, 2 * q + 1)

            for t in range(NT):
                ln_in.tensor_transpose(pe, ln_banks, t)
            pe.wait_ge(ln_in.lo, NT)
            steps(pe, step)

        @block.vector
        def _(dve):
            def subtract_zeros(j, b, i):
                dve.wait_ge(raw_in[b][i], 24 * j - 24 * b + 48)
                wait(dve, dq_lo, 3 * (j - 1) + i + 1)
                dve.tensor_tensor(deq[i][:, :], raw_w[b][i], raw_z[b][i], ALU.subtract).then_inc(subbed, 1)

            def activate(j, half):
                dve.wait_ge(sig_done, 2 * j + half + 1)
                dve.tensor_tensor(sig[half][:, :], sig[half][:, :], g_ps[half][:, :], ALU.mult).then_inc(silu_done, 1)
                dve.wait_ge(silu_done, 2 * j + half + 1)
                dve.wait_ge(prod, 4 * j + 2 * half + 2)
                wait(dve, a_lo_done, 2 * (j - 1) + half + 1)
                dve.tensor_tensor(act_f[half][:, :], sig[half][:, :], u_ps[half][:, :], ALU.mult).then_inc(act_done, 1)

            def add_output(j, t):
                dve.wait_ge(y_done, NT * j + t + 1)
                wait(dve, y_added, NT * (j - 1) + t + 1)
                dve.tensor_tensor(sh.x_nat[:, t, :], sh.x_nat[:, t, :], y_ps[t % 2][:, :], ALU.add).then_inc(y_added, 1)

            def step(j, b, products, output, prepare):
                for q in range(4):
                    if prepare and q < 3:
                        subtract_zeros(j + 1, 1 - b, q)
                    if products and q % 2:
                        activate(j, q // 2)
                    if output:
                        for t in (2 * q, 2 * q + 1):
                            add_output(j - 1, t)
                            if not products:
                                dve.wait_ge(y_added, NT * (FB - 1) + t + 1)
                                ln.vector_stats(dve, t)

            subtract_zeros(0, 0, GATE)
            subtract_zeros(0, 0, UP)
            ln_in.vector(dve, ln_banks)
            subtract_zeros(0, 0, DOWN)
            steps(dve, step)
            for t in range(NT):
                ln.vector_norm(dve, t)


def transformer(nc, a, out):
    with ExitStack() as ctx:
        sh = Shared(nc, ctx)
        ln = [LayerNorm(nc, ctx, f"ln{i}", sh) for i in range(4)]
        aw = AttentionWeights(nc, ctx)
        with ExitStack() as layer:
            ew = ExpertWeights(nc, layer)
            l0_attention(nc, sh, ln[0], ew, aw, a["x"], a["xT"], a["w0"], a["ow0"], a["norm_w"], a["decay"],
                         (a["router"], a["lora_a"]))
            l0_experts(nc, sh, ln[0], ln[1], ew, a["lora_b"], aw, a["w1"])
        mlp = MlpWeights(nc, ctx, a["mlp_w"], a["mlp_z"], a["mlp_s"], a["down_w"], a["down_z"], a["down_s"])
        l1_attention(nc, sh, ln[1], ln[2], aw, mlp, a["w1"], a["ow1"], a["bias1"], a["bo"], a["gains"])
        l1_mlp(nc, sh, ln[2], ln[3], mlp, out)


def layouts(i):
    def blocks(w):
        return w.reshape(KB, P, -1).transpose(1, 0, 2)

    x = i["L0_attn_hidden_states"].reshape(TOK, D)
    qkv = i["L0_attn_qkv_w"].reshape(HEADS, 3, HD, KB, P)
    gate = i["L0_attn_gate_w"].reshape(HEADS, 1, HD, KB, P)
    w0 = np.concatenate([qkv, gate], 1).transpose(0, 1, 4, 3, 2)
    w1 = np.stack([i[f"L1_attn_W{n}"].reshape(KB, P, HEADS, HD) for n in "kqv"], 0).transpose(3, 0, 2, 1, 4)
    FB = i["L1_ffn_gate_w"].shape[1] // P
    def cut(w):
        return w.reshape(w.shape[0], FB, P).transpose(1, 0, 2)
    a = {
        "x": x, "xT": x.T, "w0": w0, "ow0": i["L0_attn_out_w"].T.reshape(HEADS, HD, D),
        "norm_w": i["L0_attn_norm_w"].reshape(HEADS, HD).T, "decay": decay_tables(),
        "router": blocks(i["L0_ffn_gate_w"].T),
        "lora_a": blocks(i["L0_ffn_lora_A"].reshape(-1, D).T),
        "lora_b": blocks(i["L0_ffn_lora_B"].transpose(0, 2, 1).reshape(-1, D)),
        "w1": w1, "ow1": i["L1_attn_Wo"].reshape(HEADS, HD, D),
        "bias1": np.stack([i[f"L1_attn_b{n}"].reshape(HEADS, HD).T for n in "kqv"], 1),
        "bo": i["L1_attn_bo"].reshape(1, D), "gains": np.stack([i["L1_attn_gq"], i["L1_attn_gk"]], 1),
        "mlp_w": np.stack([cut(i[f"L1_ffn_{n}_w"]).reshape(FB, KB, P, P).transpose(0, 2, 1, 3)
                           for n in ("gate", "up")], 1),
        "mlp_z": np.stack([cut(i[f"L1_ffn_{n}_z"]) for n in ("gate", "up")], 1),
        "mlp_s": np.stack([cut(i[f"L1_ffn_{n}_s"]) for n in ("gate", "up")], 1),
        "down_w": i["L1_ffn_down_w"].reshape(FB, P, D), "down_z": i["L1_ffn_down_z"], "down_s": i["L1_ffn_down_s"],
    }
    return {k: np.ascontiguousarray(v) for k, v in a.items()}


def kernel(**inputs):
    import concourse.bacc as bacc
    from concourse.bass_utils import run_bass_kernel_spmd

    arrays = layouts({k: np.asarray(v) for k, v in inputs.items()})
    nc = bacc.Bacc("TRN2", target_bir_lowering=False, num_devices=1)
    aps = {k: nc.dram_tensor(f"in_{k}", v.shape, mybir.dt.from_np(v.dtype), kind="ExternalInput").ap()
           for k, v in arrays.items()}
    out = nc.dram_tensor("out", (TOK, D), F32, kind="ExternalOutput").ap()
    transformer(nc, aps, out)
    r = run_bass_kernel_spmd(nc, [{f"in_{k}": v for k, v in arrays.items()}], core_ids=[0])
    return r.results[0]["out"].reshape(1, TOK, D)
```

```python
from contextlib import ExitStack

import numpy as np

import concourse.bass as bass
from concourse import mybir

F32 = mybir.dt.float32
F32R = mybir.dt.float32r
I32 = mybir.dt.int32
U32 = mybir.dt.uint32
ACT = mybir.ActivationFunctionType
ALU = mybir.AluOpType
AX_X = mybir.AxisListType.X
ds = bass.ds

P = 128
TOK = 1024
NT = TOK // P
D = 512
KB = D // P
HALF = 512
HEADS = 32
HD = 128
LN_EPS = 1e-5

CHUNK = P
CH = HALF // CHUNK
L0_EPS = 1e-5


def decay_tables():
    factor = 1.0 - 1 / (HEADS - 1 + 1e-05) + 1e-05
    slope = (1.0 / 2.0 ** (8.0 / HEADS)) ** (np.arange(HEADS) + 1.0) * factor
    r = np.arange(CHUNK, dtype=np.float64)
    diff = r[None, None, :] - r[None, :, None]
    mask = np.where(diff >= 0, np.exp(-slope[:, None, None] * np.maximum(diff, 0)), 0.0)
    q_decay = np.broadcast_to(np.exp(-slope[:, None] * (r + 1)[None, :])[:, None], (HEADS, P, CHUNK))
    k_decay = np.exp(-(CHUNK - 1 - r)[None, :, None] * slope[:, None, None])
    chunk_decay = np.broadcast_to(np.exp(-slope * CHUNK)[:, None, None], (HEADS, P, 1))
    return np.concatenate([mask, q_decay, k_decay, chunk_decay], 2).astype(np.float32)


def wait(eng, sem, value):
    if isinstance(value, int) and value <= 0:
        return
    eng.wait_ge(sem, value)


def f(ap):
    return ap.bitcast(F32)


def three_pass(pe, out, w_hi, w_lo, x_hi, x_lo, first, last):
    pe.matmul(out, w_hi, x_hi, start=first, stop=False)
    pe.matmul(out, w_hi, x_lo, start=False, stop=False)
    return pe.matmul(out, w_lo, x_hi, start=False, stop=last)


class Shared:

    def __init__(self, nc, ctx):
        def sb(name, shape, dt=F32):
            return ctx.enter_context(nc.sbuf_tensor(name, shape, dt))

        self.x_nat = sb("x_nat", [P, NT, D])
        self.xT_hi = sb("xT_hi", [P, KB, TOK], F32R)
        self.xT_lo = sb("xT_lo", [P, KB, TOK], F32R)
        self.ident = sb("ident", [P, P])
        self.stats = sb("ln_stats", [P, NT, 6])
        self.mv = sb("ln_mv", [P, NT, 2])
        self.var = sb("ln_var", [P, NT])
        self.rstd = sb("ln_rstd", [P, NT])
        self.power = sb("power", [P, NT])


class LayerNorm:

    def __init__(self, nc, ctx, name, sh):
        def sem(s):
            return ctx.enter_context(nc.semaphore(f"{name}_{s}"))

        self.sh = sh
        self.chain = sem("dve_chain")
        self.chained = 0
        self.stats_at = {}
        self.var_ready = sem("var_ready")
        self.root = sem("root_ready")
        self.normed = sem("normed")
        self.tr = sem("transposed")
        self.hi = sem("hi_ready")
        self.lo = sem("lo_ready")

    def link(self, dve, ins):
        self.chained += 1
        ins.then_inc(self.chain, 1)
        dve.wait_ge(self.chain, self.chained)

    def vector_stats(self, dve, t):
        sh = self.sh
        self.chained += 1
        dve.bn_stats(sh.stats[:, t, :], sh.x_nat[:, t, :]).then_inc(self.chain, 1)
        self.stats_at[t] = self.chained
        if t:
            self.aggregate(dve, t - 1)
        if t == NT - 1:
            self.aggregate(dve, t)
            for u in range(CH):
                self.vector_norm(dve, u)

    def aggregate(self, dve, t):
        sh = self.sh
        dve.wait_ge(self.chain, self.stats_at[t])
        ins = dve.bn_aggr(sh.mv[:, t, :], sh.stats[:, t, :])
        self.chained += 1
        ins.then_inc(self.chain, 1)
        if (t + 1) % CH == 0:
            dve.wait_ge(self.chain, self.chained)
            half = slice(t + 1 - CH, t + 1)
            dve.tensor_scalar(sh.var[:, half], sh.mv[:, half, 1], LN_EPS, None, ALU.add).then_inc(self.var_ready, 1)

    def pool_root(self, pool):
        sh = self.sh
        for j in range(2):
            half = slice(j * CH, (j + 1) * CH)
            pool.wait_ge(self.var_ready, j + 1)
            pool.tensor_tensor(sh.rstd[:, half], sh.var[:, half], sh.power[:, half], ALU.pow).then_inc(self.root, 1)

    def vector_norm(self, dve, t):
        sh = self.sh
        dve.wait_ge(self.root, t // CH + 1)
        dve.tensor_scalar(sh.x_nat[:, t, :], sh.x_nat[:, t, :], sh.mv[:, t, 0:1], sh.rstd[:, t:t + 1],
                          ALU.subtract, ALU.mult).then_inc(self.normed, 1)

    def tensor_transpose(self, pe, banks, t):
        sh = self.sh
        pe.wait_ge(self.normed, t + 1)
        if t >= len(banks):
            pe.wait_ge(self.lo, t + 1 - len(banks))
        for k in range(KB):
            last = pe.transpose(banks[t % len(banks)][:, k * P:(k + 1) * P],
                                sh.x_nat[:, t, k * P:(k + 1) * P], sh.ident[:, :])
        last.then_inc(self.tr, 1)

    def scalar_high(self, act, banks, t):
        act.wait_ge(self.tr, t + 1)
        act.activation(self.sh.xT_hi[:, :, t * P:(t + 1) * P],
                       banks[t % len(banks)].rearrange("p (k n) -> p k n", k=KB), ACT.Copy).then_inc(self.hi, 1)

    def vector_low(self, dve, banks, t):
        cut = slice(t * P, (t + 1) * P)
        dve.wait_ge(self.tr, t + 1)
        dve.wait_ge(self.hi, t + 1)
        dve.tensor_tensor(self.sh.xT_lo[:, :, cut], banks[t % len(banks)].rearrange("p (k n) -> p k n", k=KB),
                          f(self.sh.xT_hi[:, :, cut]), ALU.subtract).then_inc(self.lo, 1)

    def vector(self, dve, banks, start=0, end=NT + 1):
        for t in range(start, end):
            if CH <= t < NT:
                self.vector_norm(dve, t)
            if t:
                self.vector_low(dve, banks, t - 1)


def l0_attention(nc, sh, ln, ew, aw, x, xT, w, ow, norm_w, decay_in, expert_weights):
    NG = 8
    KV, Q, GATE = slice(0, 4), slice(4, 6), slice(6, 8)
    K_W, V_W, Q_W, GATE_W = range(4)
    USED = (KV.stop, KV.stop, Q.stop, GATE.stop)
    SPLITS = {3: K_W, 4: V_W, 5: Q_W, 7: GATE_W}
    with ExitStack() as ctx:
        def sb(name, shape, dt=F32):
            return ctx.enter_context(nc.sbuf_tensor(f"a_{name}", shape, dt))

        def bank(name, shape):
            return ctx.enter_context(nc.psum_tensor(f"a_{name}", shape, F32))

        def sem(name):
            return ctx.enter_context(nc.semaphore(f"a_{name}"))

        def three_of(part):
            return [part[:, :, t * HD:(t + 1) * HD] for t in range(3)]

        kv_hi, kv_lo = (part[0][:, :, 0:2 * HD] for part in (aw.hi, aw.lo))
        w_raw = three_of(aw.raw) + [sb("w_raw3", [P, KB, HD])[:, :, :]]
        w_hi = three_of(aw.hi[0]) + [sb("w_hi3", [P, KB, HD], F32R)[:, :, :]]
        w_lo = three_of(aw.lo[0]) + [sb("w_lo3", [P, KB, HD], F32R)[:, :, :]]
        ow_raw = sb("ow_raw", [P, D])
        ow_hi = [sb(f"ow_hi{b}", [P, D], F32R) for b in range(2)]
        ow_lo = [sb(f"ow_lo{b}", [P, D], F32R) for b in range(2)]
        q_T = [sb(f"q_T{b}", [P, TOK]) for b in range(2)]
        gate_T = [sb(f"gate_T{b}", [P, TOK]) for b in range(2)]
        kv_nat = [sb(f"kv_nat{b}", [P, NT, 2 * HD]) for b in range(2)]
        k_T = sb("k_T", [P, TOK])
        sig_tmp = [sb(f"sig{i}", [P, HALF]) for i in range(2)]
        q_dec = sb("q_dec", [P, TOK])
        k_dec = sb("k_dec", [P, NT, HD])
        s_masked = sb("s_masked", [P, TOK])
        state = sb("state", [P, NT, HD])
        gated = sb("gated", [P, TOK])
        ga_hi = [sb(f"ga_hi{b}", [P, TOK], F32R) for b in range(2)]
        ga_lo = [sb(f"ga_lo{b}", [P, TOK], F32R) for b in range(2)]
        squares = sb("squares", [P, TOK])
        sq_sum = sb("sq_sum", [P, TOK])
        acc = sb("acc", [P, NT, D])
        decay = [sb(f"decay{b}", [P, 2 * CHUNK + 2]) for b in range(2)]
        mask = [d[:, 0:CHUNK].unsqueeze(1) for d in decay]
        q_decay = [d[:, CHUNK:2 * CHUNK].unsqueeze(1) for d in decay]
        k_decay = [d[:, 2 * CHUNK:2 * CHUNK + 1] for d in decay]
        chunk_decay = [d[:, 2 * CHUNK + 1:2 * CHUNK + 2] for d in decay]
        norm_sb = sb("norm_sb", [P, HEADS])
        ones = sb("ones", [P, 1])
        ms = sb("ms", [P, NT])
        rms = sb("rms", [P, NT])

        pj = [bank(f"pj{i}", [P, HALF]) for i in range(2)]
        tk = [bank(f"tk{j}", [P, HALF]) for j in range(2)]
        s_ps = bank("s_ps", [P, HALF])
        u_ps = bank("u_ps", [P, HALF])
        o_ps = bank("o_ps", [P, HALF])
        y_ps = bank("y_ps", [P, HALF])

        w_in = [sem(f"w_in{t}") for t in range(4)]
        ow_in = sem("ow_in")
        decay_in_sem = [sem(f"decay_in{b}") for b in range(2)]
        w_hi_done, w_lo_done = sem("w_hi_done"), sem("w_lo_done")
        ow_hi_done, ow_lo_done = sem("ow_hi_done"), sem("ow_lo_done")
        proj = sem("proj")
        sig = sem("sig")
        silu = sem("silu")
        k_tr = sem("k_tr")
        k_T_done = sem("k_T_done")
        k_decayed = sem("k_decayed")
        scored, masked = sem("scored"), sem("masked")
        q_decayed = sem("q_decayed")
        upd, state_done = sem("upd"), sem("state_done")
        attn = sem("attn")
        squared, sq_added = sem("squared"), sem("sq_added")
        gated_done, ga_hi_done, ga_lo_done = sem("gated_done"), sem("ga_hi_done"), sem("ga_lo_done")
        y_done, y_added = sem("y_done"), sem("y_added")
        x_in = [[sem(f"x_in{j}{k}") for k in range(KB)] for j in range(2)]
        const_in = sem("const_in")
        x_hi_done, x_split = sem("x_hi_done"), sem("x_split")
        zeroed = sem("zeroed")
        ms_done, ms_ready, rms_ready = sem("ms_done"), sem("ms_ready"), sem("rms_ready")
        x_nat_in, normalised, added, added_odd = sem("x_nat_in"), sem("normalised"), sem("added"), sem("added_odd")
        xT_raw = [gated, squares, sq_sum, q_dec]

        def y_bank(h, t):
            return pj[0] if isinstance(h, int) and h == HEADS - 1 and t % 2 else y_ps

        def steps(eng, step):
            def one(h):
                step(h, h % 2, 0 <= h < HEADS, h + 1 < HEADS, h >= 1, h + 2 < HEADS)
            for h in (-1, 0, 1):
                one(h)
            with eng.Fori(2, HEADS - 3, 2) as h:
                step(h, 0, True, True, True, True)
                step(h + 1, 1, True, True, True, True)
            for h in (HEADS - 2, HEADS - 1, HEADS):
                one(h)

        block = ctx.enter_context(nc.Block())

        @block.sync
        def _(sp):
            def load_weights(h, t):
                wait(sp, w_lo_done, 4 * (h - 1) + t + 1)
                sp.dma_start(w_raw[t][:, :, :], w[ds(h, 1), t].rearrange("a p k d -> (a p) k d")).then_inc(w_in[t], 16)

            load_weights(0, K_W)
            for j in range(2):
                for k in (range(2), range(KB))[j]:
                    cut = slice(j * HALF, (j + 1) * HALF)
                    sp.dma_start(xT_raw[k][:, cut], xT[k * P:(k + 1) * P, cut]).then_inc(x_in[j][k], 16)

            def load_output_weights(h):
                wait(sp, ow_lo_done, h)
                sp.dma_start(ow_raw[:, :], ow[ds(h, 1)].rearrange("a p d -> (a p) d")).then_inc(ow_in, 16)

            def load_decays(h, b):
                wait(sp, attn, 2 * (h - 1))
                sp.dma_start(decay[b][:, :], decay_in[ds(h, 1)].rearrange("a p n -> (a p) n")).then_inc(
                    decay_in_sem[b], 16)

            def load(h, b):
                load_weights(h, 0)
                load_weights(h, 1)
                load_output_weights(h - 2)
                load_weights(h, 2)
                load_weights(h, 3)
                load_decays(h - 1, 1 - b)

            for h in range(2):
                for t in range(4):
                    if h or t not in (K_W, V_W):
                        load_weights(h, t)
            load_decays(0, 0)
            sp.dma_start(sh.x_nat[:, :, :], x.rearrange("(t p) d -> p t d", p=P)).then_inc(x_nat_in, 16)
            with sp.Fori(2, HEADS - 1, 2) as h:
                load(h, 0)
                load(h + 1, 1)
            load_output_weights(HEADS - 2)
            load_decays(HEADS - 1, 1)
            load_output_weights(HEADS - 1)
            ew.load(sp, 0, expert_weights[0])
            for t in range(4):
                wait(sp, w_lo_done, 4 * HEADS + t - 3)
                sp.dma_start(w_raw[t][:, :, :], expert_weights[1][:, :, t * HD:(t + 1) * HD]).then_inc(w_in[t], 16)

        @block.gpsimd
        def _(pool):
            pool.dma_start(norm_sb[:, :], norm_w).then_inc(const_in, 16)
            pool.memset(sh.ident[:, :], 0.0).then_inc(zeroed, 1)
            pool.wait_ge(zeroed, 1)
            pool.affine_select(out=sh.ident[:, :], in_=sh.ident[:, :], compare_op=ALU.not_equal, fill=1.0, base=0,
                               pattern=[[-1, P]], channel_multiplier=1).then_inc(zeroed, 1)
            pool.memset(ones[:, :], 1.0).then_inc(zeroed, 1)
            pool.memset(sh.power[:, :], -0.5).then_inc(zeroed, 1)
            pool.memset(acc[:, :, :], 0.0).then_inc(zeroed, 1)

            def split_lo(h, t):
                pool.wait_ge(w_in[t], 16 * (h + 1))
                pool.wait_ge(w_hi_done, 4 * h + t + 1)
                wait(pool, proj, NG * (h - 1) + USED[t])
                pool.tensor_tensor(w_lo[t][:, :, :], w_raw[t][:, :, :], f(w_hi[t][:, :, :]),
                                   ALU.subtract).then_inc(w_lo_done, 1)

            for t in range(4):
                split_lo(0, t)
            pool.wait_ge(x_split, 2 * KB)
            pool.memset(sq_sum[:, :], 0.0).then_inc(zeroed, 1)
            pool.wait_ge(zeroed, 6)

            def half_out(h, b, j):
                cut = slice(j * HALF, (j + 1) * HALF)
                pool.wait_ge(ga_hi_done, 2 * h + j + 1)
                pool.wait_ge(gated_done, 2 * h + j + 1)
                wait(pool, y_done, NT * (h - 1))
                pool.tensor_tensor(ga_lo[b][:, cut], gated[:, cut], f(ga_hi[b][:, cut]),
                                   ALU.subtract).then_inc(ga_lo_done, 1)
                pool.wait_ge(squared, 2 * h + j + 1)
                wait(pool, sq_added, 2 * (h - 1) + j + 1)
                pool.tensor_tensor(sq_sum[:, cut], sq_sum[:, cut], squares[:, cut], ALU.add).then_inc(sq_added, 1)

            def step(h, b, attention, project, output, split):
                for s in range(NG):
                    if attention and s == 3:
                        pool.wait_ge(ow_in, 16 * (h + 1))
                        pool.wait_ge(ow_hi_done, h + 1)
                        wait(pool, y_done, NT * (h - 1))
                        pool.tensor_tensor(ow_lo[b][:, :], ow_raw[:, :], f(ow_hi[b][:, :]),
                                           ALU.subtract).then_inc(ow_lo_done, 1)
                    if attention and s == 6:
                        half_out(h, b, 0)
                    if split and s in SPLITS:
                        split_lo(h + 2, SPLITS[s])
                if attention:
                    half_out(h, b, 1)
                if isinstance(h, int) and h == HEADS - 2:
                    ew.split_low(pool, 0)
                    for t in range(4):
                        pool.wait_ge(w_in[t], 16 * (HEADS + 1))
                        pool.wait_ge(ew.w_hi, 2 + t)
                        pool.tensor_tensor(ew.lo[1][:, :, t * HD:(t + 1) * HD], w_raw[t][:, :, :],
                                           f(ew.hi[1][:, :, t * HD:(t + 1) * HD]), ALU.subtract).then_inc(ew.w_lo, 1)

            steps(pool, step)
            pool.wait_ge(ms_ready, 1)
            pool.tensor_tensor(rms[:, :], ms[:, :], sh.power[:, :], ALU.pow).then_inc(rms_ready, 1)
            pool.wait_ge(x_nat_in, 16)
            for t in range(0, NT, 2):
                pool.wait_ge(normalised, t // 2 + 1)
                pool.tensor_tensor(sh.x_nat[:, t, :], sh.x_nat[:, t, :], acc[:, t, :], ALU.add).then_inc(added, 1)
            ln.pool_root(pool)

        @block.scalar
        def _(act):
            def split_hi(h, t):
                act.wait_ge(w_in[t], 16 * (h + 1))
                wait(act, proj, NG * (h - 1) + USED[t])
                act.activation(w_hi[t][:, :, :], w_raw[t][:, :, :], ACT.Copy).then_inc(w_hi_done, 1)

            act.dma_start(w_raw[V_W][:, :, :], w[0, V_W]).then_inc(w_in[V_W], 16)
            for k in (2, 3):
                act.dma_start(xT_raw[k][:, 0:HALF], xT[k * P:(k + 1) * P, 0:HALF]).then_inc(x_in[0][k], 16)
            for j in range(2):
                split_hi(0, 2 * j)
                split_hi(0, 2 * j + 1)
                for k in range(KB):
                    cut = slice(j * HALF, (j + 1) * HALF)
                    act.wait_ge(x_in[j][k], 16)
                    act.activation(sh.xT_hi[:, k, cut], xT_raw[k][:, cut], ACT.Copy).then_inc(x_hi_done, 1)

            def copy_k(h, b, j):
                act.wait_ge(k_tr, 2 * h + j + 1)
                wait(act, scored, 2 * (h - 1) + j + 1)
                act.activation(k_T[:, j * HALF:(j + 1) * HALF], tk[j][:, :], ACT.Copy).then_inc(k_T_done, 1)

            def decay_k(h, b, j):
                act.wait_ge(silu, 6 * h + 2 * j + 2)
                act.wait_ge(decay_in_sem[b], 8 * h + 16 - 8 * b)
                wait(act, upd, 2 * (h - 1) + j + 1)
                act.activation(k_dec[:, CH * j:CH * (j + 1), :], kv_nat[b][:, CH * j:CH * (j + 1), 0:HD],
                               ACT.Copy, scale=k_decay[b]).then_inc(k_decayed, 1)

            def square(h, j):
                cut = slice(j * HALF, (j + 1) * HALF)
                act.wait_ge(attn, 2 * h + j + 1)
                wait(act, sq_added, 2 * (h - 1) + j + 1)
                act.activation(squares[:, cut], o_ps[:, :], ACT.Square).then_inc(squared, 1)

            def gated_hi(h, b, j):
                cut = slice(j * HALF, (j + 1) * HALF)
                act.wait_ge(gated_done, 2 * h + j + 1)
                wait(act, y_done, NT * (h - 1))
                act.activation(ga_hi[b][:, cut], gated[:, cut], ACT.Copy).then_inc(ga_hi_done, 1)

            def sigmoid(g, bg, s):
                act.wait_ge(proj, NG * g + s + 1)
                half = s % 2
                if s >= GATE.start:
                    wait(act, gated_done, 2 * (g - 1))
                    out = gate_T[bg][:, half * HALF:(half + 1) * HALF]
                else:
                    wait(act, silu, 6 * g + s - 1 if s >= 2 else 6 * (g - 1) + 5 + s)
                    out = sig_tmp[half][:, :]
                act.activation(out, pj[half][:, :], ACT.Sigmoid).then_inc(sig, 1)

            def step(h, b, attention, project, output, split):
                for s in range(NG):
                    if attention:
                        if s in (0, 2):
                            copy_k(h, b, s // 2)
                            decay_k(h, b, s // 2)
                        if s == 3:
                            act.wait_ge(ow_in, 16 * (h + 1))
                            wait(act, y_done, NT * (h - 1))
                            act.activation(ow_hi[b][:, :], ow_raw[:, :], ACT.Copy).then_inc(ow_hi_done, 1)
                        if s in (5, 7):
                            square(h, s // 6)
                        if s == 6:
                            gated_hi(h, b, 0)
                    if project:
                        sigmoid(h + 1, 1 - b, s)
                    if split and s in SPLITS:
                        split_hi(h + 2, SPLITS[s])
                if attention:
                    gated_hi(h, b, 1)
                if isinstance(h, int) and h == HEADS - 2:
                    ew.split_high(act, 0)
                    for t in range(4):
                        act.wait_ge(w_in[t], 16 * (HEADS + 1))
                        act.activation(ew.hi[1][:, :, t * HD:(t + 1) * HD], w_raw[t][:, :, :],
                                       ACT.Copy).then_inc(ew.w_hi, 1)

            steps(act, step)
            act.wait_ge(rms_ready, 1)
            for t in range(0, NT, 2):
                act.wait_ge(y_added, NT * (HEADS - 1) + t + 1)
                act.activation(acc[:, t, :], acc[:, t, :], ACT.Copy, scale=rms[:, t:t + 1]).then_inc(normalised, 1)

        @block.tensor
        def _(pe):
            def project_group(g, s):
                half = s % 2
                pe.wait_ge(w_lo_done, 4 * g + (2, 2, 2, 2, 3, 3, 4, 4)[s])
                if isinstance(g, int) and g == 0 and s < KV.stop:
                    pe.wait_ge(x_split, KB * (s // 2 + 1))
                if s >= 2:
                    pe.wait_ge(silu, 6 * g + s - 1)
                else:
                    wait(pe, sig, NG * (g - 1) + 7 + s)
                if s < KV.stop:
                    for u in range(2):
                        cut = slice((2 * s + u) * P, (2 * s + u + 1) * P)
                        for k in range(KB):
                            last = three_pass(pe, pj[half][:, u * 2 * HD:(u + 1) * 2 * HD], sh.xT_hi[:, k, cut],
                                              sh.xT_lo[:, k, cut], kv_hi[:, k, :], kv_lo[:, k, :], k == 0,
                                              k == KB - 1)
                else:
                    t = Q_W if s < Q.stop else GATE_W
                    cut = slice(half * HALF, (half + 1) * HALF)
                    for k in range(KB):
                        last = three_pass(pe, pj[half][:, :], w_hi[t][:, k, :], w_lo[t][:, k, :],
                                          sh.xT_hi[:, k, cut], sh.xT_lo[:, k, cut], k == 0, k == KB - 1)
                last.then_inc(proj, 1)

            def transposes(h, b, j):
                pe.wait_ge(silu, 6 * h + 2 * j + 2)
                wait(pe, k_T_done, 2 * (h - 1) + j + 1)
                for c in range(CH):
                    last = pe.transpose(tk[j][:, c * CHUNK:(c + 1) * CHUNK], kv_nat[b][:, j * CH + c, 0:HD],
                                        sh.ident[:, :])
                last.then_inc(k_tr, 1)

            def scores(h, b, j):
                pe.wait_ge(k_T_done, 2 * h + j + 1)
                pe.wait_ge(silu, 6 * h + 6)
                wait(pe, masked, 2 * h + j)
                for c in range(CH):
                    at = (j * CH + c) * CHUNK
                    last = pe.matmul(s_ps[:, c * CHUNK:(c + 1) * CHUNK], k_T[:, at:at + CHUNK],
                                     q_T[b][:, at:at + CHUNK], start=True, stop=True)
                last.then_inc(scored, 1)

            def updates(h, b, j):
                pe.wait_ge(k_decayed, 2 * h + j + 1)
                wait(pe, state_done, 7 * h + CH * j)
                for c in range(j * CH, min((j + 1) * CH, NT - 1)):
                    last = pe.matmul(u_ps[:, (c % CH) * HD:(c % CH + 1) * HD], k_dec[:, c, :],
                                     kv_nat[b][:, c, HD:], start=True, stop=True)
                last.then_inc(upd, 1)

            def outputs(h, b, j):
                pe.wait_ge(masked, 2 * h + j + 1)
                pe.wait_ge(q_decayed, h + 1)
                wait(pe, squared, 2 * h + j)
                wait(pe, gated_done, 2 * h + j)
                for c in range(j * CH, (j + 1) * CH):
                    out = o_ps[:, (c % CH) * CHUNK:(c % CH + 1) * CHUNK]
                    at = c * CHUNK
                    last = pe.matmul(out, kv_nat[b][:, c, HD:], s_masked[:, at:at + CHUNK], start=True,
                                     stop=(c == 0))
                    if c:
                        if c == j * CH or c == 1:
                            pe.wait_ge(state_done, 7 * h + (3 if j == 0 else 7))
                        last = pe.matmul(out, state[:, c, :], q_dec[:, at:at + CHUNK], start=False, stop=True)
                last.then_inc(attn, 1)

            def output_tile(h, b, t):
                pe.wait_ge(ga_lo_done, 2 * h + t // CH + 1)
                pe.wait_ge(ow_lo_done, h + 1)
                wait(pe, y_added, NT * h + (t - 1 if t and y_bank(h, 1) is not y_ps else t))
                cut = slice(t * P, (t + 1) * P)
                three_pass(pe, y_bank(h, t)[:, :], ga_hi[b][:, cut], ga_lo[b][:, cut], ow_hi[b][:, :], ow_lo[b][:, :],
                           True, True).then_inc(y_done, 1)

            def step(h, b, attention, project, output, split):
                for s in range(NG):
                    if attention:
                        if isinstance(h, int) and h == 0 and s == 0:
                            pe.wait_ge(zeroed, 6)
                        if s in (0, 2):
                            transposes(h, b, s // 2)
                        if s in (1, 3):
                            scores(h, b, s // 2)
                        if s in (4, 5):
                            updates(h, b, s - 4)
                        if s in (5, 7):
                            outputs(h, b, s // 6)
                    if project:
                        project_group(h + 1, s)
                    if output:
                        output_tile(h - 1, 1 - b, s)
                    if isinstance(h, int) and h == HEADS and s == CH - 1:
                        mean_squares()

            def mean_squares():
                pe.wait_ge(sq_added, 2 * HEADS)
                for t in range(NT):
                    last = pe.matmul(s_ps[:, t:t + 1], sq_sum[:, t * P:(t + 1) * P], ones[:, :], start=True,
                                     stop=True)
                last.then_inc(ms_done, 1)

            steps(pe, step)

        @block.vector
        def _(dve):
            for j in range(2):
                for k in range(KB):
                    cut = slice(j * HALF, (j + 1) * HALF)
                    dve.wait_ge(x_hi_done, KB * j + k + 1)
                    dve.wait_ge(x_in[j][k], 16)
                    dve.tensor_tensor(sh.xT_lo[:, k, cut], xT_raw[k][:, cut], f(sh.xT_hi[:, k, cut]),
                                      ALU.subtract).then_inc(x_split, 1)
            dve.wait_ge(x_split, 2 * KB)
            dve.wait_ge(const_in, 16)
            dve.wait_ge(zeroed, 6)

            def decay_q(h, b):
                dve.wait_ge(silu, 6 * h + 6)
                dve.wait_ge(decay_in_sem[b], 8 * h + 16 - 8 * b)
                wait(dve, attn, 2 * h)
                dve.tensor_tensor(q_dec[:, :].rearrange("p (c n) -> p c n", n=CHUNK),
                                  q_T[b][:, :].rearrange("p (c n) -> p c n", n=CHUNK),
                                  q_decay[b].broadcast_to([P, NT, CHUNK]), ALU.mult).then_inc(q_decayed, 1)

            def mask_scores(h, b, j):
                dve.wait_ge(scored, 2 * h + j + 1)
                wait(dve, attn, 2 * (h - 1) + j + 1)
                dve.tensor_tensor(s_masked[:, j * HALF:(j + 1) * HALF].rearrange("p (c n) -> p c n", n=CHUNK),
                                  s_ps[:, :].rearrange("p (c n) -> p c n", n=CHUNK),
                                  mask[b].broadcast_to([P, CH, CHUNK]), ALU.mult).then_inc(masked, 1)

            def states(h, b, j):
                dve.wait_ge(upd, 2 * h + j + 1)
                wait(dve, attn, 2 * h)
                for c in range(j * CH, min((j + 1) * CH, NT - 1)):
                    u = u_ps[:, (c % CH) * HD:(c % CH + 1) * HD]
                    if c == 0:
                        ins = dve.tensor_copy(state[:, 1, :], u)
                    else:
                        dve.wait_ge(state_done, 7 * h + c)
                        ins = dve.scalar_tensor_tensor(out=state[:, c + 1, :], in0=state[:, c, :],
                                                       scalar=chunk_decay[b], in1=u,
                                                       op0=ALU.mult, op1=ALU.add)
                    ins.then_inc(state_done, 1)

            def gate_out(h, b, j):
                cut = slice(j * HALF, (j + 1) * HALF)
                dve.wait_ge(squared, 2 * h + j + 1)
                dve.wait_ge(sig, NG * h + 7 + j)
                wait(dve, ga_lo_done, 2 * (h - 1) + j + 1)
                dve.scalar_tensor_tensor(out=gated[:, cut], in0=o_ps[:, :], scalar=norm_sb[:, ds(h, 1)],
                                         in1=gate_T[b][:, cut], op0=ALU.mult, op1=ALU.mult).then_inc(gated_done, 1)

            def silu_half(g, bg, s):
                dve.wait_ge(sig, NG * g + s + 1)
                wait(dve, attn, 2 * (g - 1))
                half = s % 2
                if s < KV.stop:
                    out = kv_nat[bg][:, 2 * s:2 * s + 2, :].rearrange("p t c -> p (t c)")
                else:
                    out = q_T[bg][:, half * HALF:(half + 1) * HALF]
                dve.tensor_tensor(out, pj[half][:, :], sig_tmp[half][:, :], ALU.mult).then_inc(silu, 1)

            def add_output(h, t):
                dve.wait_ge(y_done, NT * h + t + 1)
                wait(dve, y_added, NT * (h - 1) + t + 1)
                dve.tensor_tensor(acc[:, t, :], acc[:, t, :], y_bank(h, t)[:, :], ALU.add).then_inc(y_added, 1)

            def step(h, b, attention, project, output, split):
                for s in range(NG):
                    if attention:
                        if s == 0:
                            decay_q(h, b)
                        if s in (1, 3):
                            mask_scores(h, b, s // 2)
                        if s in (4, 5):
                            states(h, b, s - 4)
                        if s in (5, 7):
                            gate_out(h, b, s // 6)
                    if project and s < GATE.start:
                        silu_half(h + 1, 1 - b, s)
                    if output:
                        add_output(h - 1, s)
                    if isinstance(h, int) and h == HEADS and s == CH - 1:
                        dve.wait_ge(ms_done, 1)
                        dve.tensor_scalar(ms[:, :], s_ps[:, 0:NT], 1.0 / (HEADS * HD), L0_EPS, ALU.mult,
                                          ALU.add).then_inc(ms_ready, 1)

            steps(dve, step)
            dve.wait_ge(rms_ready, 1)
            dve.wait_ge(x_nat_in, 16)
            dve.wait_ge(y_added, NT * HEADS)
            for t in range(0, NT, 2):
                dve.scalar_tensor_tensor(out=sh.x_nat[:, t + 1, :], in0=acc[:, t + 1, :], scalar=rms[:, t + 1:t + 2],
                                         in1=sh.x_nat[:, t + 1, :], op0=ALU.mult, op1=ALU.add).then_inc(added_odd, 1)
                dve.wait_ge(added, t // 2 + 1)
                ln.vector_stats(dve, t)
                dve.wait_ge(added_odd, t // 2 + 1)
                ln.vector_stats(dve, t + 1)


EXPERTS = 8
RANK = 64


WIDTHS = (EXPERTS, EXPERTS * RANK, D)


class ExpertWeights:

    def __init__(self, nc, ctx):
        def sb(name, n, dt=F32R):
            return ctx.enter_context(nc.sbuf_tensor(f"e_{name}", [P, KB, n], dt))

        def sem(name):
            return ctx.enter_context(nc.semaphore(f"e_{name}"))

        self.raw = {0: sb("raw0", EXPERTS, F32)}
        self.hi = [sb(f"hi{i}", n) for i, n in enumerate(WIDTHS[:2])]
        self.lo = [sb(f"lo{i}", n) for i, n in enumerate(WIDTHS[:2])]
        self.w_in = {0: sem("w_in0"), 2: sem("w_in2")}
        self.w_hi, self.w_lo = sem("w_hi"), sem("w_lo")

    def load(self, sp, i, w):
        sp.dma_start(self.raw[i][:, :, :], w).then_inc(self.w_in[i], 16)

    def split_high(self, act, i):
        act.wait_ge(self.w_in[i], 16)
        act.activation(self.hi[i][:, :, :], self.raw[i][:, :, :], ACT.Copy).then_inc(self.w_hi, 1)

    def split_low(self, pool, i):
        pool.wait_ge(self.w_in[i], 16)
        pool.wait_ge(self.w_hi, 6 if i else 1)
        pool.tensor_tensor(self.lo[i][:, :, :], self.raw[i][:, :, :], f(self.hi[i][:, :, :]),
                           ALU.subtract).then_inc(self.w_lo, 1)


def l0_experts(nc, sh, ln_in, ln, ew, lora_b, aw, next_weights):
    with ExitStack() as ctx:
        def sb(name, shape, dt=F32):
            return ctx.enter_context(nc.sbuf_tensor(f"e_{name}", shape, dt))

        def bank(name):
            return ctx.enter_context(nc.psum_tensor(f"e_{name}", [P, HALF], F32))

        def sem(name):
            return ctx.enter_context(nc.semaphore(f"e_{name}"))

        hi, lo = ew.hi, ew.lo
        hi.append(sb("hi2", [P, KB, D], F32R))
        lo.append(sb("lo2", [P, KB, D], F32R))
        ew.raw[2] = sb("raw2", [P, KB, D])
        logits_T = sb("logits_T", [EXPERTS, TOK])
        logits = sb("logits", [P, NT, EXPERTS])
        prob = sb("prob", [P, NT, EXPERTS])
        top = [sb(f"top{n}", [P, NT, 1]) for n in range(2)]
        chosen = [sb(f"chosen{n}", [P, NT, EXPERTS]) for n in range(2)]
        place = sb("place", [P, NT, EXPERTS])
        first = sb("first", [P, NT, 1])
        weight = sb("weight", [P, NT, EXPERTS])
        total = sb("total", [P, NT, 1])
        order_i = sb("order_i", [P, EXPERTS], I32)
        order = sb("order", [P, 1, EXPERTS])
        h_sb = sb("h_sb", [P, NT, EXPERTS * RANK])
        scaled = [sb(f"scaled{i}", [P, EXPERTS * RANK]) for i in range(2)]
        hT_hi = [sb(f"hT_hi{i}", [P, KB, P], F32R) for i in range(2)]
        hT_lo = [sb(f"hT_lo{i}", [P, KB, P], F32R) for i in range(2)]

        lg = bank("lg")
        h_ps = [bank(f"h_ps{i}") for i in range(2)]
        t_ps = [bank(f"t_ps{i}") for i in range(2)]
        y_ps = [bank(f"y_ps{i}") for i in range(2)]
        ln_banks = [t[:, :] for t in t_ps]

        order_ready = sem("order_ready")
        routed, routed_sb = sem("routed"), sem("routed_sb")
        logits_ready, shifted, exp_ready = sem("logits_ready"), sem("shifted"), sem("exp_ready")
        h_ready, h_copied, h_scaled = sem("h_ready"), sem("h_copied"), sem("h_scaled")
        hT_ready, hT_hi_ready, hT_lo_ready = sem("hT_ready"), sem("hT_hi_ready"), sem("hT_lo_ready")
        y_ready, y_added = sem("y_ready"), sem("y_added")

        ORDER = [("x", 0), ("x", 1), ("x", 2), ("h", 0), ("x", 3), ("x", 4), ("h", 1), ("x", 5), ("x", 6), ("r", 0),
                 ("x", 7), ("h", 2), ("r", 1), ("h", 3)]

        block = ctx.enter_context(nc.Block())

        @block.sync
        def _(sp):
            ew.load(sp, 2, lora_b)
            aw.load(sp, next_weights, 0)

        @block.gpsimd
        def _(pool):
            pool.iota(order_i[:, :], pattern=[[-1, EXPERTS]], base=EXPERTS,
                      channel_multiplier=0).then_inc(order_ready, 1)
            ew.split_low(pool, 2)
            for kind in range(3):
                aw.split_low(pool, 0, 0, kind)
            ln.pool_root(pool)

        @block.scalar
        def _(act):
            def copy_h(t):
                act.wait_ge(h_ready, t + 1)
                act.activation(h_sb[:, t, :], h_ps[t % 2][:, :], ACT.Copy).then_inc(h_copied, 1)

            for do, t in ORDER:
                if do == "x":
                    ln_in.scalar_high(act, ln_banks, t)
                if do == "h":
                    copy_h(t)
                if do == "r":
                    act.wait_ge(routed, t + 1)
                    act.activation(logits_T[:, t * HALF:(t + 1) * HALF], y_ps[t][0:EXPERTS, :],
                                   ACT.Copy).then_inc(routed_sb, 1)
            ew.split_high(act, 2)
            act.wait_ge(shifted, 1)
            act.activation(prob[:, :, :], logits[:, :, :], ACT.Exp).then_inc(exp_ready, 1)
            for t in range(4, NT):
                copy_h(t)
            for kind in range(3):
                aw.split_high(act, 0, 0, kind)
            for t in range(NT):
                act.wait_ge(hT_ready, t + 1)
                if t >= 2:
                    act.wait_ge(y_ready, t - 1)
                act.activation(hT_hi[t % 2][:, :, :], t_ps[t % 2][:, :].rearrange("p (k n) -> p k n", k=KB),
                               ACT.Copy).then_inc(hT_hi_ready, 1)

        @block.tensor
        def _(pe):
            def product(out, lhs_hi, lhs_lo, i):
                for k in range(KB):
                    last = three_pass(pe, out, lhs_hi(k), lhs_lo(k), hi[i][:, k, :], lo[i][:, k, :],
                                      k == 0, k == KB - 1)
                return last

            def x_part(part, t):
                return lambda k: part[:, k, t * P:(t + 1) * P]

            def route(j):
                pe.wait_ge(ln_in.lo, CH * (j + 1))
                cut = slice(j * HALF, (j + 1) * HALF)
                for k in range(KB):
                    last = three_pass(pe, y_ps[j][0:EXPERTS, :], hi[0][:, k, :], lo[0][:, k, :], sh.xT_hi[:, k, cut],
                                      sh.xT_lo[:, k, cut], k == 0, k == KB - 1)
                last.then_inc(routed, 1)

            def down(t):
                pe.wait_ge(ln_in.lo, t + 1)
                if t >= 2:
                    pe.wait_ge(h_copied, t - 1)
                product(h_ps[t % 2][:, :], x_part(sh.xT_hi, t), x_part(sh.xT_lo, t), 1).then_inc(h_ready, 1)

            for do, t in ORDER:
                if do == "x":
                    ln_in.tensor_transpose(pe, ln_banks, t)
                else:
                    (down if do == "h" else route)(t)
            pe.wait_ge(routed_sb, 2)
            for t in range(NT):
                last = pe.transpose(lg[:, t * EXPERTS:(t + 1) * EXPERTS], logits_T[:, t * P:(t + 1) * P],
                                    sh.ident[0:EXPERTS, 0:EXPERTS])
            last.then_inc(logits_ready, 1)
            for t in range(4, NT):
                down(t)
            for i in range(NT + 1):
                if i < NT:
                    pe.wait_ge(h_scaled, i + 1)
                    if i >= 2:
                        pe.wait_ge(hT_lo_ready, i - 1)
                    for k in range(KB):
                        last = pe.transpose(t_ps[i % 2][:, k * P:(k + 1) * P], scaled[i % 2][:, k * P:(k + 1) * P],
                                            sh.ident[:, :])
                    last.then_inc(hT_ready, 1)
                if i >= 1:
                    t = i - 1
                    pe.wait_ge(ew.w_lo, 6)
                    pe.wait_ge(hT_lo_ready, t + 1)
                    if t >= 2:
                        pe.wait_ge(y_added, t - 1)
                    product(y_ps[t % 2][:, :], lambda k: hT_hi[t % 2][:, k, :], lambda k: hT_lo[t % 2][:, k, :],
                            2).then_inc(y_ready, 1)

        @block.vector
        def _(dve):
            link = ln.link
            wide = [P, NT, EXPERTS]
            ln_in.vector(dve, ln_banks)
            dve.wait_ge(order_ready, 1)
            link(dve, dve.tensor_copy(order[:, 0, :], order_i[:, :]))
            dve.wait_ge(logits_ready, 1)
            lg_t = lg[:, 0:NT * EXPERTS].rearrange("p (t e) -> p t e", e=EXPERTS)
            link(dve, dve.tensor_reduce(total[:, :, :], lg_t, AX_X, ALU.max))
            dve.tensor_tensor(logits[:, :, :], lg_t, total[:, :, :].broadcast_to(wide),
                              ALU.subtract).then_inc(shifted, 1)
            dve.wait_ge(exp_ready, 1)
            link(dve, dve.tensor_reduce(total[:, :, :], prob[:, :, :], AX_X, ALU.add))
            link(dve, dve.reciprocal(total[:, :, :], total[:, :, :]))
            link(dve, dve.tensor_tensor(prob[:, :, :], prob[:, :, :], total[:, :, :].broadcast_to(wide), ALU.mult))
            for n in range(2):
                link(dve, dve.tensor_reduce(top[n][:, :, :], prob[:, :, :], AX_X, ALU.max))
                link(dve, dve.tensor_tensor(place[:, :, :], prob[:, :, :], top[n][:, :, :].broadcast_to(wide),
                                            ALU.is_equal))
                link(dve, dve.tensor_tensor(place[:, :, :], place[:, :, :], order[:, :, :].broadcast_to(wide),
                                            ALU.mult))
                link(dve, dve.tensor_reduce(first[:, :, :], place[:, :, :], AX_X, ALU.max))
                link(dve, dve.tensor_tensor(chosen[n][:, :, :], place[:, :, :], first[:, :, :].broadcast_to(wide),
                                            ALU.is_equal))
                if n == 0:
                    link(dve, dve.scalar_tensor_tensor(out=prob[:, :, :], in0=chosen[0][:, :, :], scalar=-2.0,
                                                       in1=prob[:, :, :], op0=ALU.mult, op1=ALU.add))
            link(dve, dve.tensor_tensor(total[:, :, :], top[0][:, :, :], top[1][:, :, :], ALU.add))
            link(dve, dve.reciprocal(total[:, :, :], total[:, :, :]))
            for n in range(2):
                link(dve, dve.tensor_tensor(top[n][:, :, :], top[n][:, :, :], total[:, :, :], ALU.mult))
                link(dve, dve.tensor_tensor(chosen[n][:, :, :], chosen[n][:, :, :],
                                            top[n][:, :, :].broadcast_to(wide), ALU.mult))
            link(dve, dve.tensor_tensor(weight[:, :, :], chosen[0][:, :, :], chosen[1][:, :, :], ALU.add))

            for i in range(NT + 2):
                if i < NT:
                    dve.wait_ge(h_copied, i + 1)
                    if i >= 2:
                        dve.wait_ge(hT_ready, i - 1)
                    dve.tensor_tensor(scaled[i % 2][:, :].rearrange("p (e r) -> p e r", e=EXPERTS),
                                      h_sb[:, i, :].rearrange("p (e r) -> p e r", e=EXPERTS),
                                      weight[:, i, :].unsqueeze(2).broadcast_to([P, EXPERTS, RANK]),
                                      ALU.mult).then_inc(h_scaled, 1)
                if 1 <= i <= NT:
                    t = i - 1
                    dve.wait_ge(hT_hi_ready, t + 1)
                    if t >= 2:
                        dve.wait_ge(y_ready, t - 1)
                    dve.tensor_tensor(hT_lo[t % 2][:, :, :], t_ps[t % 2][:, :].rearrange("p (k n) -> p k n", k=KB),
                                      f(hT_hi[t % 2][:, :, :]), ALU.subtract).then_inc(hT_lo_ready, 1)
                if i >= 2:
                    t = i - 2
                    dve.wait_ge(y_ready, t + 1)
                    dve.tensor_tensor(sh.x_nat[:, t, :], sh.x_nat[:, t, :], y_ps[t % 2][:, :],
                                      ALU.add).then_inc(y_added, 1)
                    dve.wait_ge(y_added, t + 1)
                    ln.vector_stats(dve, t)


L1_EPS = 1e-6


KQV = 3 * HD


class AttentionWeights:

    def __init__(self, nc, ctx):
        self.nc = nc
        self.raw = ctx.enter_context(nc.sbuf_tensor("b_w_raw", [P, KB, KQV], F32))
        self.hi, self.lo = [], []
        self.place(ctx, 0)
        self.w_in, self.hi_done, self.lo_done, self.proj = (
            ctx.enter_context(nc.semaphore(f"b_{name}"))
            for name in ("w_in",
                         "w_hi_done", "w_lo_done",
                         "proj"))

    def place(self, ctx, b):
        for name, part in (("hi", self.hi), ("lo", self.lo)):
            part.append(ctx.enter_context(self.nc.sbuf_tensor(f"b_w_{name}{b}", [P, KB, KQV], F32R)))

    def load(self, sp, w, h):
        wait(sp, self.lo_done, 3 * h)
        sp.dma_start(self.raw[:, :, :], w[ds(h, 1)].rearrange("a p k d -> (a p) k d")).then_inc(self.w_in, 16)

    def split_high(self, act, h, b, kind):
        cut = slice(kind * HD, (kind + 1) * HD)
        act.wait_ge(self.w_in, 16 * (h + 1))
        wait(act, self.proj, NT * (h - 1))
        act.activation(self.hi[b][:, :, cut], self.raw[:, :, cut], ACT.Copy).then_inc(self.hi_done, 1)

    def split_low(self, pool, h, b, kind):
        cut = slice(kind * HD, (kind + 1) * HD)
        pool.wait_ge(self.w_in, 16 * (h + 1))
        pool.wait_ge(self.hi_done, 3 * h + kind + 1)
        wait(pool, self.proj, NT * (h - 1))
        pool.tensor_tensor(self.lo[b][:, :, cut], self.raw[:, :, cut], f(self.hi[b][:, :, cut]),
                           ALU.subtract).then_inc(self.lo_done, 1)


def l1_attention(nc, sh, ln_in, ln, aw, mlp, w, ow, bias, bo, gains):
    with ExitStack() as ctx:
        def sb(name, shape, dt=F32):
            return ctx.enter_context(nc.sbuf_tensor(f"b_{name}", shape, dt))

        def bank(name, shape):
            return ctx.enter_context(nc.psum_tensor(f"b_{name}", shape, F32))

        def sem(name):
            return ctx.enter_context(nc.semaphore(f"b_{name}"))

        BATCH = 2
        NB = NT // BATCH
        WIDE = BATCH * P
        aw.place(ctx, 1)
        w_hi, w_lo = aw.hi, aw.lo
        ow_raw = sb("ow_raw", [P, D])
        ow_hi = [sb(f"ow_hi{b}", [P, D], F32R) for b in range(2)]
        ow_lo = [sb(f"ow_lo{b}", [P, D], F32R) for b in range(2)]
        bias_sb = [sb(f"bias{b}", [P, KQV]) for b in range(2)]
        nat = [sb(f"nat{i}", [P, BATCH, KQV]) for i in range(NB)]
        sq = sb("sq", [P, BATCH, 2, HD])
        sq_sum = sb("sq_sum", [P, BATCH, 2])
        mean_sq = sb("mean_sq", [P, BATCH, 2])
        rstd = [sb(f"rstd{b}", [P, NT, 2]) for b in range(2)]
        k_hi = [sb(f"k_hi{b}", [P, TOK], F32R) for b in range(2)]
        k_lo = [sb(f"k_lo{b}", [P, TOK], F32R) for b in range(2)]
        q_hi = [sb(f"q_hi{b}", [P, TOK], F32R) for b in range(2)]
        q_lo = [sb(f"q_lo{b}", [P, TOK], F32R) for b in range(2)]
        v_hi = [sb(f"v_hi{b}", [P, NT, HD], F32R) for b in range(2)]
        v_lo = [sb(f"v_lo{b}", [P, NT, HD], F32R) for b in range(2)]
        prob = sb("prob", [P, TOK])
        row_max = sb("row_max", [P, NT])
        shift = sb("shift", [P, NT])
        row_sum = sb("row_sum", [P, NT])
        row_inv = sb("row_inv", [P, NT])
        pT_hi = [mlp.pT0[0], sb("pT_hi1", [P, NT, WIDE], F32R)]
        pT_lo = [mlp.pT0[1], sb("pT_lo1", [P, NT, WIDE], F32R)]
        o_hi = [sb(f"o_hi{i}", [P, WIDE], F32R) for i in range(2)]
        o_lo = [sb(f"o_lo{i}", [P, WIDE], F32R) for i in range(2)]
        gain_in = sb("gain_in", [P, 2])
        gain = sb("gain", [P, 1])
        bo_sb = sb("bo_sb", [P, D])

        s_ps = bank("s_ps", [P, TOK])
        t_ps = bank("t_ps", [P, TOK])
        pj_kq = bank("pj_kq", [P, TOK])
        pj, kq_ps = pj_kq[:, 0:HALF], pj_kq[:, HALF:].rearrange("p (k n) -> p k n", k=2)
        o_ps = bank("o_ps", [P, HALF])
        y_ps = bank("y_ps", [P, HALF])
        ln_banks = [s_ps[:, 0:HALF], s_ps[:, HALF:], t_ps[:, 0:HALF], t_ps[:, HALF:]]

        w_lo_done, proj = aw.lo_done, aw.proj
        bias_in = [sem(f"bias_in{b}") for b in range(2)]
        ow_in, ow_hi_done, ow_lo_done = sem("ow_in"), sem("ow_hi_done"), sem("ow_lo_done")
        taken = sem("taken")
        squared, summed, mean_ready, rstd_ready = (
            sem("squared"), sem("summed"), sem("mean_ready"), sem("rstd_ready"))
        k_scaled, kq_tr, kq_hi_done, kq_lo_done = sem("k_scaled"), sem("kq_tr"), sem("kq_hi_done"), sem("kq_lo_done")
        v_hi_done, v_lo_done = sem("v_hi_done"), sem("v_lo_done")
        scored, max_done, shift_done, exp_done = sem("scored"), sem("max_done"), sem("shift_done"), sem("exp_done")
        p_tr, pT_hi_done, pT_lo_done = sem("p_tr"), sem("pT_hi_done"), sem("pT_lo_done")
        inv_done = sem("inv_done")
        pv, o_hi_done, o_lo_done = sem("pv"), sem("o_hi_done"), sem("o_lo_done")
        y_done, y_added = sem("y_done"), sem("y_added")
        const_in, bias_added, gain_ready = sem("const_in"), sem("bias_added"), sem("gain_ready")

        def peeled(h, *which):
            return isinstance(h, int) and h in which

        def y_bank(h, t):
            return pj if peeled(h, HEADS - 1) and t >= 3 and t % 2 else y_ps[:, :]

        def project_bank(g, t):
            return y_ps[:, 0:KQV] if peeled(g, 0) and t % 2 else pj[:, 0:KQV]

        def score_banks(h, t):
            return pj_kq if peeled(h, HEADS - 1) and t % 2 else s_ps

        def steps(eng, step):
            def one(h):
                step(h, h % 2, 0 <= h < HEADS, h >= 1, 0 <= h + 1 < HEADS, h + 2 < HEADS)
            for h in (-2, -1, 0, 1):
                one(h)
            with eng.Fori(2, HEADS - 3, 2) as h:
                step(h, 0, True, True, True, True)
                step(h + 1, 1, True, True, True, True)
            for h in (HEADS - 2, HEADS - 1, HEADS):
                one(h)

        def scored_in(h, cur, s):
            if not cur:
                return ()
            if peeled(h, HEADS - 1):
                return (0, 1) if s == 0 else range(s + 1, min(s + 2, NT))
            return (s,)

        def projected(h, b, nxt, more, s):
            if s < 6:
                return (h + 1, 1 - b, s + 2) if nxt else None
            return (h + 2, b, s - 6) if more else None

        def quarter(h, b, cur, rest, s):
            n = (s - 3) % 8
            if s >= 3:
                return (h, b, n // 2, n % 2) if cur else None
            return (h - 1, 1 - b, n // 2, n % 2) if rest else None

        def output(h, b, cur, rest, s):
            if s >= 5:
                return (h, b, s - 5) if cur else None
            return (h - 1, 1 - b, s + 3) if rest else None

        def v_batch(h, b, cur, nxt, s):
            if s % 2 == 0:
                return None
            if s == 1:
                return (h, b, NB - 1) if cur else None
            return (h + 1, 1 - b, (s - 3) // 2) if nxt else None

        block = ctx.enter_context(nc.Block())

        @block.sync
        def _(sp):
            def load_bias(h, b):
                wait(sp, taken, NT * (h - 1))
                sp.dma_start(bias_sb[b][:, :], bias[ds(h, 1), :].partition_broadcast(P)).then_inc(bias_in[b], 16)

            def load_output_weights(h):
                wait(sp, ow_lo_done, h)
                sp.dma_start(ow_raw[:, :], ow[ds(h, 1)].rearrange("a p d -> (a p) d")).then_inc(ow_in, 16)

            def load(h, b):
                aw.load(sp, w, h)
                load_bias(h, b)
                load_output_weights(h - 2)

            load_bias(0, 0)
            sp.dma_start(gain_in[:, :], gains).then_inc(const_in, 16)
            aw.load(sp, w, 1)
            load_bias(1, 1)
            sp.dma_start(bo_sb[:, :], bo.partition_broadcast(P)).then_inc(const_in, 16)
            with sp.Fori(2, HEADS - 1, 2) as h:
                load(h, 0)
                load(h + 1, 1)
            load_output_weights(HEADS - 2)
            load_output_weights(HEADS - 1)
            sp.wait_ge(pv, NB * HEADS - 1)
            mlp.load(sp, 0, 0)

        @block.gpsimd
        def _(pool):
            def inverse_rms(g, bg, i):
                pool.wait_ge(mean_ready, NB * g + i + 1)
                wait(pool, exp_done, NT * (g - 1))
                pool.tensor_tensor(rstd[bg][:, BATCH * i:BATCH * (i + 1), :].rearrange("p t k -> p (t k)"),
                                   mean_sq[:, :, :].rearrange("p t k -> p (t k)"), sh.power[:, 0:2 * BATCH],
                                   ALU.pow).then_inc(rstd_ready, 1)

            def v_low(g, bg, i):
                pool.wait_ge(v_hi_done, NB * g + i + 1)
                wait(pool, pv, NB * (g - 1))
                pool.tensor_tensor(v_lo[bg][:, BATCH * i:BATCH * (i + 1), :], nat[i][:, :, 2 * HD:],
                                   f(v_hi[bg][:, BATCH * i:BATCH * (i + 1), :]), ALU.subtract).then_inc(v_lo_done, 1)

            def step(h, b, cur, rest, nxt, more):
                for s in range(NT):
                    if nxt and s % 2 == 0:
                        inverse_rms(h + 1, 1 - b, s // 2)
                    if v_batch(h, b, cur, nxt, s):
                        v_low(*v_batch(h, b, cur, nxt, s))
                    if cur and s == 3:
                        pool.wait_ge(ow_in, 16 * (h + 1))
                        pool.wait_ge(ow_hi_done, h + 1)
                        wait(pool, y_done, NT * (h - 1))
                        pool.tensor_tensor(ow_lo[b][:, :], ow_raw[:, :], f(ow_hi[b][:, :]),
                                           ALU.subtract).then_inc(ow_lo_done, 1)
                    if nxt and more and s in (0, 2, 4):
                        aw.split_low(pool, h + 2, b, s // 2)

            steps(pool, step)
            ln.pool_root(pool)

        @block.scalar
        def _(act):
            for t in range(NT):
                ln_in.scalar_high(act, ln_banks, t)

            def square(g, i):
                act.wait_ge(taken, NT * g + BATCH * (i + 1))
                wait(act, summed, NB * g + i)
                act.activation(sq[:, :, :, :].rearrange("p t k d -> p t (k d)"), nat[i][:, :, 0:2 * HD],
                               ACT.Square).then_inc(squared, 1)

            def kq_high(g, bg, i):
                cut = slice(i * WIDE, (i + 1) * WIDE)
                act.wait_ge(kq_tr, NB * g + i + 1)
                wait(act, scored, NT * (g - 1))
                act.activation(k_hi[bg][:, cut], kq_ps[:, 0, :], ACT.Copy)
                act.activation(q_hi[bg][:, cut], kq_ps[:, 1, :], ACT.Copy, scale=gain[:, 0:1]).then_inc(kq_hi_done, 1)

            def v_high(g, bg, i):
                act.wait_ge(taken, NT * g + BATCH * (i + 1))
                wait(act, pv, NB * (g - 1))
                act.activation(v_hi[bg][:, BATCH * i:BATCH * (i + 1), :], nat[i][:, :, 2 * HD:],
                               ACT.Copy).then_inc(v_hi_done, 1)

            def out_hi(h, i):
                act.wait_ge(pv, NB * h + i + 1)
                wait(act, y_done, NT * h + BATCH * (i - 1))
                act.activation(o_hi[i % 2][:, :], o_ps[:, 0:WIDE], ACT.Copy).then_inc(o_hi_done, 1)

            def prob_hi(h, t):
                i, at = t // BATCH, (t % BATCH) * P
                act.wait_ge(p_tr, NT * h + t + 1)
                wait(act, pv, NB * h + i - 1)
                act.activation(pT_hi[i % 2][:, :, at:at + P], t_ps[:, :].rearrange("p (m n) -> p m n", m=NT),
                               ACT.Copy).then_inc(pT_hi_done, 1)

            def exponent(h, b, t):
                act.wait_ge(shift_done, NT * h + t + 1)
                wait(act, p_tr, NT * h + t)
                act.activation(prob[:, :], score_banks(h, t)[:, :], ACT.Exp, bias=shift[:, t:t + 1],
                               scale=rstd[b][:, t, 1:2], accum_out=row_sum[:, t:t + 1]).then_inc(exp_done, 1)

            def step(h, b, cur, rest, nxt, more):
                if peeled(h, -1):
                    act.wait_ge(gain_ready, 1)
                for s in range(NT):
                    if nxt and s % 2 == 0:
                        square(h + 1, s // 2)
                    if v_batch(h, b, cur, nxt, s):
                        v_high(*v_batch(h, b, cur, nxt, s))
                    q = quarter(h, b, cur, rest, s)
                    if q and q[3]:
                        out_hi(q[0], q[2])
                    if nxt and s % 2:
                        kq_high(h + 1, 1 - b, s // 2)
                    if rest and s == 0:
                        prob_hi(h - 1, NT - 1)
                    if cur and s:
                        prob_hi(h, s - 1)
                    if cur:
                        exponent(h, b, s)
                    if cur and s == 3:
                        act.wait_ge(ow_in, 16 * (h + 1))
                        wait(act, y_done, NT * (h - 1))
                        act.activation(ow_hi[b][:, :], ow_raw[:, :], ACT.Copy).then_inc(ow_hi_done, 1)
                    if nxt and more and s in (0, 2, 4):
                        aw.split_high(act, h + 2, b, s // 2)

            steps(act, step)

        @block.tensor
        def _(pe):
            def project_tile(g, bg, t):
                if peeled(g, 0):
                    for u in range(3 * t, min(3 * t + 3, NT)):
                        ln_in.tensor_transpose(pe, ln_banks, u)
                    pe.wait_ge(ln_in.lo, t + 1)
                pe.wait_ge(w_lo_done, 3 * (g + 1))
                wait(pe, taken, NT * g + (t - 1 if peeled(g, 0) else t))
                cut = slice(t * P, (t + 1) * P)
                for k in range(KB):
                    last = three_pass(pe, project_bank(g, t), sh.xT_hi[:, k, cut], sh.xT_lo[:, k, cut],
                                      w_hi[bg][:, k, :], w_lo[bg][:, k, :], k == 0, k == KB - 1)
                last.then_inc(proj, 1)

            def transpose_kq(g, i):
                pe.wait_ge(k_scaled, NB * g + i + 1)
                wait(pe, kq_lo_done, NB * g + i)
                for kind in range(2):
                    for u in range(BATCH):
                        last = pe.transpose(kq_ps[:, kind, u * P:(u + 1) * P], nat[i][:, u, kind * HD:(kind + 1) * HD],
                                            sh.ident[:, :])
                last.then_inc(kq_tr, 1)

            def values(h, b, i, part):
                if part == 0:
                    pe.wait_ge(pT_lo_done, NT * h + BATCH * (i + 1))
                    pe.wait_ge(v_lo_done, NB * (h + 1))
                    wait(pe, o_lo_done, NB * h + i)
                for m in range(part * NT // 2, (part + 1) * NT // 2):
                    last = three_pass(pe, o_ps[:, 0:WIDE], v_hi[b][:, m, :], v_lo[b][:, m, :], pT_hi[i % 2][:, m, :],
                                      pT_lo[i % 2][:, m, :], m == 0, m == NT - 1)
                if part:
                    last.then_inc(pv, 1)

            def scores(h, b, t):
                if t == 0:
                    pe.wait_ge(kq_lo_done, NB * (h + 1))
                wait(pe, exp_done, NT * h + (t - 1 if peeled(h, HEADS - 1) and t else t))
                cut = slice(t * P, (t + 1) * P)
                for j in range(2):
                    keys = slice(j * HALF, (j + 1) * HALF)
                    last = three_pass(pe, score_banks(h, t)[:, keys], q_hi[b][:, cut], q_lo[b][:, cut],
                                      k_hi[b][:, keys], k_lo[b][:, keys], True, True)
                last.then_inc(scored, 1)

            def transpose_probs(h, t):
                pe.wait_ge(exp_done, NT * h + t + 1)
                wait(pe, pT_lo_done, NT * h + t)
                for m in range(NT):
                    cut = slice(m * P, (m + 1) * P)
                    last = pe.transpose(t_ps[:, cut], prob[:, cut], sh.ident[:, :])
                last.then_inc(p_tr, 1)

            def output_tile(h, b, t):
                i, at = t // BATCH, (t % BATCH) * P
                pe.wait_ge(o_lo_done, NB * h + i + 1)
                pe.wait_ge(ow_lo_done, h + 1)
                wait(pe, y_added, NT * h + (t - 1 if peeled(h, HEADS - 1) and t >= 3 else t))
                three_pass(pe, y_bank(h, t), o_hi[i % 2][:, at:at + P], o_lo[i % 2][:, at:at + P],
                           ow_hi[b][:, :], ow_lo[b][:, :], True, True).then_inc(y_done, 1)

            def step(h, b, cur, rest, nxt, more):
                for s in range(NT):
                    if projected(h, b, nxt, more, s):
                        project_tile(*projected(h, b, nxt, more, s))
                    if quarter(h, b, cur, rest, s):
                        values(*quarter(h, b, cur, rest, s))
                    if nxt and s % 2:
                        transpose_kq(h + 1, s // 2)
                    if rest and s == 0:
                        transpose_probs(h - 1, NT - 1)
                    if cur and s:
                        transpose_probs(h, s - 1)
                    for t in scored_in(h, cur, s):
                        scores(h, b, t)
                    if output(h, b, cur, rest, s):
                        output_tile(*output(h, b, cur, rest, s))

            steps(pe, step)

        @block.vector
        def _(dve):
            def take(g, bg, t):
                i, u = t // BATCH, t % BATCH
                if peeled(g, 0) and t < 2:
                    ln_in.vector(dve, ln_banks, (0, 4)[t], (4, 7)[t])
                dve.wait_ge(proj, NT * g + t + 1)
                if t == 0:
                    dve.wait_ge(bias_in[bg], 8 * g + 16 - 8 * bg)
                if u == 0:
                    wait(dve, kq_tr, NB * (g - 1) + i + 1)
                    wait(dve, v_lo_done, NB * (g - 1) + i + 1)
                dve.tensor_tensor(nat[i][:, u, :], project_bank(g, t), bias_sb[bg][:, :], ALU.add).then_inc(taken, 1)
                if peeled(g, 0) and t == 1:
                    ln_in.vector(dve, ln_banks, 7)

            def means(g, i):
                dve.wait_ge(squared, NB * g + i + 1)
                dve.tensor_reduce(sq_sum[:, :, :], sq[:, :, :, :], AX_X, ALU.add).then_inc(summed, 1)
                dve.wait_ge(summed, NB * g + i + 1)
                wait(dve, rstd_ready, NB * g + i)
                dve.tensor_scalar(mean_sq[:, :, :], sq_sum[:, :, :], 1.0 / HD, L1_EPS, ALU.mult,
                                  ALU.add).then_inc(mean_ready, 1)

            def scale_k(g, bg, i):
                dve.wait_ge(rstd_ready, NB * g + i + 1)
                dve.tensor_tensor(nat[i][:, :, 0:HD], nat[i][:, :, 0:HD],
                                  rstd[bg][:, BATCH * i:BATCH * (i + 1), 0:1].broadcast_to([P, BATCH, HD]),
                                  ALU.mult).then_inc(k_scaled, 1)

            def kq_low(g, bg, i):
                cut = slice(i * WIDE, (i + 1) * WIDE)
                dve.wait_ge(kq_hi_done, NB * g + i + 1)
                dve.tensor_tensor(k_lo[bg][:, cut], kq_ps[:, 0, :], f(k_hi[bg][:, cut]), ALU.subtract)
                dve.scalar_tensor_tensor(out=q_lo[bg][:, cut], in0=kq_ps[:, 1, :], scalar=gain[:, 0:1],
                                         in1=f(q_hi[bg][:, cut]), op0=ALU.mult,
                                         op1=ALU.subtract).then_inc(kq_lo_done, 1)

            def maxima(h, b, t):
                dve.wait_ge(scored, NT * h + t + 1)
                dve.tensor_reduce(row_max[:, t:t + 1], score_banks(h, t)[:, :], AX_X, ALU.max).then_inc(max_done, 1)
                dve.wait_ge(max_done, NT * h + t + 1)
                dve.tensor_scalar(shift[:, t:t + 1], row_max[:, t:t + 1], rstd[b][:, t, 1:2], -1.0,
                                  ALU.mult, ALU.mult).then_inc(shift_done, 1)

            def prob_lo(h, t):
                i, at = t // BATCH, (t % BATCH) * P
                dve.wait_ge(pT_hi_done, NT * h + t + 1)
                dve.tensor_tensor(pT_lo[i % 2][:, :, at:at + P], t_ps[:, :].rearrange("p (m n) -> p m n", m=NT),
                                  f(pT_hi[i % 2][:, :, at:at + P]), ALU.subtract).then_inc(pT_lo_done, 1)

            def invert_sums(h, i):
                cut = slice(i * BATCH, (i + 1) * BATCH)
                dve.wait_ge(exp_done, NT * h + BATCH * (i + 1))
                wait(dve, y_added, NT * (h - 1) + BATCH * (i + 1))
                dve.reciprocal(row_inv[:, cut], row_sum[:, cut]).then_inc(inv_done, 1)

            def out_lo(h, i):
                dve.wait_ge(o_hi_done, NB * h + i + 1)
                dve.tensor_tensor(o_lo[i % 2][:, :], o_ps[:, 0:WIDE], f(o_hi[i % 2][:, :]),
                                  ALU.subtract).then_inc(o_lo_done, 1)

            def add_output(h, b, t):
                dve.wait_ge(y_done, NT * h + t + 1)
                dve.wait_ge(inv_done, NB * h + t // BATCH + 1)
                if peeled(h, 0):
                    dve.wait_ge(bias_added, t + 1)
                wait(dve, y_added, NT * (h - 1) + t + 1)
                dve.scalar_tensor_tensor(out=sh.x_nat[:, t, :], in0=y_bank(h, t), scalar=row_inv[:, t:t + 1],
                                         in1=sh.x_nat[:, t, :], op0=ALU.mult, op1=ALU.add).then_inc(y_added, 1)

            def step(h, b, cur, rest, nxt, more):
                if peeled(h, -1):
                    dve.wait_ge(const_in, 32)
                    ln.link(dve, dve.tensor_tensor(gain[:, :], gain_in[:, 0:1], gain_in[:, 1:2], ALU.mult))
                    dve.tensor_scalar(gain[:, :], gain[:, :], float(HD) ** -0.5, None,
                                      ALU.mult).then_inc(gain_ready, 1)
                    dve.wait_ge(gain_ready, 1)
                for s in range(NT):
                    q = quarter(h, b, cur, rest, s)
                    if nxt and s % 2 == 0:
                        means(h + 1, s // 2)
                    if projected(h, b, nxt, more, s):
                        take(*projected(h, b, nxt, more, s))
                    if peeled(h, -1):
                        dve.wait_ge(ln_in.tr, s + 1)
                        dve.tensor_tensor(sh.x_nat[:, s, :], sh.x_nat[:, s, :], bo_sb[:, :], ALU.add).then_inc(
                            bias_added, 1)
                    if q and not q[3]:
                        invert_sums(q[0], q[2])
                    if nxt and s % 2 == 0:
                        scale_k(h + 1, 1 - b, s // 2)
                    if q and q[3]:
                        out_lo(q[0], q[2])
                    if nxt and s % 2:
                        kq_low(h + 1, 1 - b, s // 2)
                    early = s % 2 and not peeled(h, HEADS - 1)
                    if early:
                        for t in scored_in(h, cur, s):
                            maxima(h, b, t)
                    if rest and s == 0:
                        prob_lo(h - 1, NT - 1)
                    if cur and s:
                        prob_lo(h, s - 1)
                    if not early:
                        for t in scored_in(h, cur, s):
                            maxima(h, b, t)
                    if output(h, b, cur, rest, s):
                        add_output(*output(h, b, cur, rest, s))

            steps(dve, step)
            for t in range(NT):
                dve.wait_ge(y_added, NT * (HEADS - 1) + t + 1)
                ln.vector_stats(dve, t)


GATE, UP, DOWN = range(3)


class MlpWeights:

    def __init__(self, nc, ctx, w, z, s, down_w, down_z, down_s):
        with ExitStack() as earlier:
            self.pT0 = [earlier.enter_context(nc.sbuf_tensor(f"pT_{n}0", [P, NT, 2 * P], F32R)) for n in ("hi", "lo")]
        self.nc, self.ctx = nc, ctx
        self.raw_w, self.raw_z, self.raw_s = [], [], []
        self.place(0)
        self.w, self.z, self.s = w, z, s
        self.down = (down_w, down_z, down_s)
        self.raw_in = [[ctx.enter_context(nc.semaphore(f"m_raw_in{b}{i}")) for i in range(3)]
                       for b in range(2)]
        self.scaled = ctx.enter_context(nc.semaphore("m_scaled"))

    def place(self, b):
        for name, dt, raw in (("raw_w", I32, self.raw_w), ("raw_z", I32, self.raw_z), ("raw_s", F32, self.raw_s)):
            raw.append([self.ctx.enter_context(self.nc.sbuf_tensor(f"m_{name}{b}{i}", [P, D], dt))[:, :]
                        for i in range(3)])

    def load(self, sp, j, b):
        for i in range(3):
            wait(sp, self.scaled, 3 * (j - 2) + i + 1)
            if i == DOWN:
                parts = [a[ds(j, 1), :] for a in self.down[1:]]
                parts = [self.down[0][ds(j, 1)].rearrange("a p d -> (a p) d")] + parts
            else:
                parts = (self.w[ds(j, 1), i].rearrange("a p k f -> (a p) (k f)"),
                         self.z[ds(j, 1), i].rearrange("a k f -> a (k f)"),
                         self.s[ds(j, 1), i].rearrange("a k f -> a (k f)"))
            sp.dma_start(self.raw_w[b][i], parts[0]).then_inc(self.raw_in[b][i], 16)
            sp.dma_start(self.raw_z[b][i], parts[1].partition_broadcast(P)).then_inc(self.raw_in[b][i], 16)
            sp.dma_start(self.raw_s[b][i], parts[2].partition_broadcast(P)).then_inc(self.raw_in[b][i], 16)


def l1_mlp(nc, sh, ln_in, ln, mlp, out):
    FB = mlp.w.shape[0]
    with ExitStack() as ctx:
        def sb(name, shape, dt=F32):
            return ctx.enter_context(nc.sbuf_tensor(f"m_{name}", shape, dt))

        def bank(name):
            return ctx.enter_context(nc.psum_tensor(f"m_{name}", [P, HALF], F32))

        def sem(name):
            return ctx.enter_context(nc.semaphore(f"m_{name}"))

        mlp.place(1)
        raw_w, raw_z, raw_s = mlp.raw_w, mlp.raw_z, mlp.raw_s
        deq = [sb(f"deq{i}", [P, D]) for i in range(3)]
        w_hi = [[sb(f"w_hi{b}{i}", [P, D], F32R) for i in range(3)] for b in range(2)]
        w_lo = [[sb(f"w_lo{b}{i}", [P, D], F32R) for i in range(3)] for b in range(2)]
        sig = [sb(f"sig{i}", [P, HALF]) for i in range(2)]
        act_f = [sb(f"act_f{i}", [P, HALF]) for i in range(2)]
        a_hi = [sb(f"a_hi{b}", [P, TOK], F32R) for b in range(2)]
        a_lo = [sb(f"a_lo{b}", [P, TOK], F32R) for b in range(2)]

        g_ps = [bank(f"g_ps{i}") for i in range(2)]
        u_ps = [bank(f"u_ps{i}") for i in range(2)]
        y_ps = [bank(f"y_ps{i}") for i in range(2)]

        raw_in, scaled = mlp.raw_in, mlp.scaled
        subbed, dq_hi, dq_lo = sem("subbed"), sem("dq_hi"), sem("dq_lo")
        prod = sem("prod")
        sig_done, silu_done, act_done = sem("sig_done"), sem("silu_done"), sem("act_done")
        a_hi_done, a_lo_done = sem("a_hi_done"), sem("a_lo_done")
        y_done, y_added = sem("y_done"), sem("y_added")
        y_copied, y_odd = sem("y_copied"), sem("y_odd")
        y_odd_sb = sig + act_f
        stored = sem("stored")
        ln_banks = [b[:, :] for b in (g_ps[1], u_ps[1], *y_ps)]

        def steps(eng, step):
            for j in (0, 1):
                step(j, j, True, j >= 1, True)
            with eng.Fori(2, FB - 3, 2) as j:
                step(j, 0, True, True, True)
                step(j + 1, 1, True, True, True)
            for j in (FB - 2, FB - 1, FB):
                step(j, j % 2, j < FB, True, j + 1 < FB)

        block = ctx.enter_context(nc.Block())

        @block.sync
        def _(sp):
            mlp.load(sp, 1, 1)
            with sp.Fori(2, FB - 1, 2) as j:
                mlp.load(sp, j, 0)
                mlp.load(sp, j + 1, 1)
            for t in range(NT):
                sp.wait_ge(ln.normed, t + 1)
                sp.dma_start(out[t * P:(t + 1) * P, :], sh.x_nat[:, t, :]).then_inc(stored, 16)
            sp.wait_ge(stored, 16 * NT)

        @block.gpsimd
        def _(pool):
            def dequantise(j, b, i):
                pool.wait_ge(subbed, 3 * j + i + 1)
                pool.tensor_tensor(deq[i][:, :], deq[i][:, :], raw_s[b][i], ALU.mult).then_inc(scaled, 1)
                pool.wait_ge(dq_hi, 3 * j + i + 1)
                pool.wait_ge(scaled, 3 * j + i + 1)
                if i == DOWN:
                    wait(pool, y_done, NT * (j - 1))
                else:
                    wait(pool, prod, 4 * (j - 1))
                pool.tensor_tensor(w_lo[b][i][:, :], deq[i][:, :], f(w_hi[b][i][:, :]), ALU.subtract).then_inc(dq_lo, 1)

            def act_low(j, b, half):
                cut = slice(half * HALF, (half + 1) * HALF)
                pool.wait_ge(a_hi_done, 2 * j + half + 1)
                wait(pool, y_done, NT * (j - 1))
                pool.tensor_tensor(a_lo[b][:, cut], act_f[half][:, :], f(a_hi[b][:, cut]),
                                   ALU.subtract).then_inc(a_lo_done, 1)

            def step(j, b, products, output, prepare):
                for q in range(4):
                    if products and q == 2:
                        act_low(j, b, 0)
                    if prepare and q < 3:
                        dequantise(j + 1, 1 - b, q)
                if products:
                    act_low(j, b, 1)
                else:
                    for t in range(1, NT, 2):
                        pool.wait_ge(y_copied, t // 2 + 1)
                        pool.wait_ge(y_added, NT * (FB - 2) + t + 1)
                        pool.tensor_tensor(sh.x_nat[:, t, :], sh.x_nat[:, t, :], y_odd_sb[t // 2][:, :],
                                           ALU.add).then_inc(y_odd, 1)

            for i in range(3):
                dequantise(0, 0, i)
            steps(pool, step)
            ln.pool_root(pool)

        @block.scalar
        def _(act):
            def weight_high(j, b, i):
                act.wait_ge(scaled, 3 * j + i + 1)
                if i == DOWN:
                    wait(act, y_done, NT * (j - 1))
                else:
                    wait(act, prod, 4 * (j - 1))
                act.activation(w_hi[b][i][:, :], deq[i][:, :], ACT.Copy).then_inc(dq_hi, 1)

            def sigmoid(j, half):
                act.wait_ge(prod, 4 * j + 2 * half + 1)
                wait(act, act_done, 2 * (j - 1) + half + 1)
                act.activation(sig[half][:, :], g_ps[half][:, :], ACT.Sigmoid).then_inc(sig_done, 1)

            def act_high(j, b, half):
                act.wait_ge(act_done, 2 * j + half + 1)
                wait(act, y_done, NT * (j - 1))
                act.activation(a_hi[b][:, half * HALF:(half + 1) * HALF], act_f[half][:, :],
                               ACT.Copy).then_inc(a_hi_done, 1)

            def step(j, b, products, output, prepare):
                for q in range(4):
                    if products and q % 2 == 0:
                        sigmoid(j, q // 2)
                    if products and q == 2:
                        act_high(j, b, 0)
                    if prepare and q < 3:
                        weight_high(j + 1, 1 - b, q)
                if products:
                    act_high(j, b, 1)
                else:
                    for t in range(1, NT, 2):
                        act.wait_ge(y_done, NT * (FB - 1) + t + 1)
                        act.activation(y_odd_sb[t // 2][:, :], y_ps[t % 2][:, :], ACT.Copy).then_inc(y_copied, 1)

            for t in range(NT):
                ln_in.scalar_high(act, ln_banks, t)
                if t in (CH - 1, CH):
                    weight_high(0, 0, (GATE, UP)[t - CH + 1])
            weight_high(0, 0, DOWN)
            steps(act, step)

        @block.tensor
        def _(pe):
            def product(j, b, q):
                half, kind = q // 2, q % 2
                if isinstance(j, int) and j == 0:
                    if half == 0:
                        for t in (range(CH + 1), range(CH + 1, NT))[kind]:
                            ln_in.tensor_transpose(pe, ln_banks, t)
                    pe.wait_ge(ln_in.lo, CH * (half + 1))
                pe.wait_ge(dq_lo, 3 * j + kind + 1)
                wait(pe, (silu_done, act_done)[kind], 2 * (j - 1) + half + 1)
                out_ps = (g_ps, u_ps)[kind][half]
                cut = slice(half * HALF, (half + 1) * HALF)
                for k in range(KB):
                    col = slice(k * P, (k + 1) * P)
                    last = three_pass(pe, out_ps[:, :], w_hi[b][kind][:, col], w_lo[b][kind][:, col],
                                      sh.xT_hi[:, k, cut], sh.xT_lo[:, k, cut], k == 0, k == KB - 1)
                last.then_inc(prod, 1)

            def output_tile(j, b, t):
                pe.wait_ge(a_lo_done, 2 * j + t // CH + 1)
                pe.wait_ge(dq_lo, 3 * j + 3)
                if isinstance(j, int) and j == FB - 1 and t >= 2:
                    pe.wait_ge(*((y_added, NT * j + t // 2) if t % 2 == 0 else (y_copied, t // 2)))
                else:
                    wait(pe, y_added, NT * j + max(t - 1, 0))
                cut = slice(t * P, (t + 1) * P)
                three_pass(pe, y_ps[t % 2][:, :], a_hi[b][:, cut], a_lo[b][:, cut], w_hi[b][DOWN][:, :],
                           w_lo[b][DOWN][:, :], True, True).then_inc(y_done, 1)

            def step(j, b, products, output, prepare):
                for q in range(4):
                    if products:
                        product(j, b, q)
                    if output:
                        output_tile(j - 1, 1 - b, 2 * q)
                        output_tile(j - 1, 1 - b, 2 * q + 1)

            steps(pe, step)

        @block.vector
        def _(dve):
            def subtract_zeros(j, b, i):
                dve.wait_ge(raw_in[b][i], 24 * j - 24 * b + 48)
                wait(dve, dq_lo, 3 * (j - 1) + i + 1)
                dve.tensor_tensor(deq[i][:, :], raw_w[b][i], raw_z[b][i], ALU.subtract).then_inc(subbed, 1)

            def activate(j, half):
                dve.wait_ge(sig_done, 2 * j + half + 1)
                dve.tensor_tensor(sig[half][:, :], sig[half][:, :], g_ps[half][:, :], ALU.mult).then_inc(silu_done, 1)
                dve.wait_ge(silu_done, 2 * j + half + 1)
                dve.wait_ge(prod, 4 * j + 2 * half + 2)
                wait(dve, a_lo_done, 2 * (j - 1) + half + 1)
                dve.tensor_tensor(act_f[half][:, :], sig[half][:, :], u_ps[half][:, :], ALU.mult).then_inc(act_done, 1)

            def add_output(j, t):
                dve.wait_ge(y_done, NT * j + t + 1)
                wait(dve, y_added, NT * (j - 1) + t + 1)
                dve.tensor_tensor(sh.x_nat[:, t, :], sh.x_nat[:, t, :], y_ps[t % 2][:, :], ALU.add).then_inc(y_added, 1)

            def step(j, b, products, output, prepare):
                for q in range(4):
                    if prepare and q < 3:
                        subtract_zeros(j + 1, 1 - b, q)
                    if products and q % 2:
                        activate(j, q // 2)
                    if output:
                        add_output(j - 1, 2 * q)
                        if products:
                            add_output(j - 1, 2 * q + 1)
                        else:
                            dve.wait_ge(y_added, NT * (FB - 1) + q + 1)
                            ln.vector_stats(dve, 2 * q)
                            dve.wait_ge(y_odd, q + 1)
                            ln.vector_stats(dve, 2 * q + 1)

            subtract_zeros(0, 0, GATE)
            ln_in.vector(dve, ln_banks, 0, 3)
            subtract_zeros(0, 0, UP)
            ln_in.vector(dve, ln_banks, 3)
            subtract_zeros(0, 0, DOWN)
            steps(dve, step)
            for t in range(CH, NT):
                ln.vector_norm(dve, t)


def transformer(nc, a, out):
    with ExitStack() as ctx:
        sh = Shared(nc, ctx)
        ln = [LayerNorm(nc, ctx, f"ln{i}", sh) for i in range(4)]
        aw = AttentionWeights(nc, ctx)
        with ExitStack() as layer:
            ew = ExpertWeights(nc, layer)
            l0_attention(nc, sh, ln[0], ew, aw, a["x"], a["xT"], a["w0"], a["ow0"], a["norm_w"], a["decay"],
                         (a["router"], a["lora_a"]))
            l0_experts(nc, sh, ln[0], ln[1], ew, a["lora_b"], aw, a["w1"])
        mlp = MlpWeights(nc, ctx, a["mlp_w"], a["mlp_z"], a["mlp_s"], a["down_w"], a["down_z"], a["down_s"])
        l1_attention(nc, sh, ln[1], ln[2], aw, mlp, a["w1"], a["ow1"], a["bias1"], a["bo"], a["gains"])
        l1_mlp(nc, sh, ln[2], ln[3], mlp, out)


def layouts(i):
    def blocks(w):
        return w.reshape(KB, P, -1).transpose(1, 0, 2)

    x = i["L0_attn_hidden_states"].reshape(TOK, D)
    qkv = i["L0_attn_qkv_w"].reshape(HEADS, 3, HD, KB, P)
    gate = i["L0_attn_gate_w"].reshape(HEADS, 1, HD, KB, P)
    w0 = np.concatenate([qkv[:, [1, 2, 0]], gate], 1).transpose(0, 1, 4, 3, 2)
    w1 = np.stack([i[f"L1_attn_W{n}"].reshape(KB, P, HEADS, HD) for n in "kqv"], 3).transpose(2, 1, 0, 3, 4)
    FB = i["L1_ffn_gate_w"].shape[1] // P
    def cut(w):
        return w.reshape(w.shape[0], FB, P).transpose(1, 0, 2)
    a = {
        "x": x, "xT": x.T, "w0": w0, "ow0": i["L0_attn_out_w"].T.reshape(HEADS, HD, D),
        "norm_w": i["L0_attn_norm_w"].reshape(HEADS, HD).T, "decay": decay_tables(),
        "router": blocks(i["L0_ffn_gate_w"].T),
        "lora_a": blocks(i["L0_ffn_lora_A"].reshape(-1, D).T),
        "lora_b": blocks(i["L0_ffn_lora_B"].transpose(0, 2, 1).reshape(-1, D)),
        "w1": w1.reshape(HEADS, P, KB, KQV), "ow1": i["L1_attn_Wo"].reshape(HEADS, HD, D),
        "bias1": np.concatenate([i[f"L1_attn_b{n}"].reshape(HEADS, HD) for n in "kqv"], 1),
        "bo": i["L1_attn_bo"].reshape(1, D), "gains": np.stack([i["L1_attn_gq"], i["L1_attn_gk"]], 1),
        "mlp_w": np.stack([cut(i[f"L1_ffn_{n}_w"]).reshape(FB, KB, P, P).transpose(0, 2, 1, 3)
                           for n in ("gate", "up")], 1),
        "mlp_z": np.stack([cut(i[f"L1_ffn_{n}_z"]) for n in ("gate", "up")], 1),
        "mlp_s": np.stack([cut(i[f"L1_ffn_{n}_s"]) for n in ("gate", "up")], 1),
        "down_w": i["L1_ffn_down_w"].reshape(FB, P, D), "down_z": i["L1_ffn_down_z"], "down_s": i["L1_ffn_down_s"],
    }
    return {k: np.ascontiguousarray(v) for k, v in a.items()}


def kernel(**inputs):
    import concourse.bacc as bacc
    from concourse.bass_utils import run_bass_kernel_spmd

    arrays = layouts({k: np.asarray(v) for k, v in inputs.items()})
    nc = bacc.Bacc("TRN2", target_bir_lowering=False, num_devices=1)
    aps = {k: nc.dram_tensor(f"in_{k}", v.shape, mybir.dt.from_np(v.dtype), kind="ExternalInput").ap()
           for k, v in arrays.items()}
    out = nc.dram_tensor("out", (TOK, D), F32, kind="ExternalOutput").ap()
    transformer(nc, aps, out)
    r = run_bass_kernel_spmd(nc, [{f"in_{k}": v for k, v in arrays.items()}], core_ids=[0])
    return r.results[0]["out"].reshape(1, TOK, D)
```
